# Optimizing a Trainium2 kernel written in Bass

```python
import numpy as np
import jax
import jax.numpy as jnp

def _softmax(x, axis=-1):
    return jax.nn.softmax(x, axis=axis)

def _gelu(x):
    return jax.nn.gelu(x, approximate=True)

def _silu(x):
    return jax.nn.silu(x)

def _sigmoid(x):
    return jax.nn.sigmoid(x)

def _layernorm(x, axis=-1, eps=1e-05):
    m = jnp.mean(x, axis=axis, keepdims=True)
    v = jnp.var(x, axis=axis, keepdims=True)
    return (x - m) / jnp.sqrt(v + eps)

def _scatter_add(tgt, idx, src, axis=0):
    return tgt.at[idx].add(src)

def _segment_sum(src, seg, n):
    return jax.ops.segment_sum(src, seg, n)
kernel_name = 'mk_seq_postln_d2_jaxref_r8_9dad73'

def setup_inputs(seed: int=0):
    np.random.seed(seed)
    _w = jnp.asarray

    def _L0_attn_setup():
        import jax, jax.numpy as jnp
        import numpy as np
        HEAD_SIZE = 64
        key = jax.random.key(seed)
        ks = jax.random.split(key, 5)
        B, N, D, H, E, O = (2, 256, 128, 16, HEAD_SIZE, 128)
        return {'query': jax.random.normal(ks[0], (B, N, D), dtype=jnp.float32), 'Wq': jax.random.normal(ks[1], (H, D, E), dtype=jnp.float32) / np.sqrt(D), 'Wk': jax.random.normal(ks[2], (H, D, E), dtype=jnp.float32) / np.sqrt(D), 'Wv': jax.random.normal(ks[3], (H, D, E), dtype=jnp.float32) / np.sqrt(D), 'Wp': jax.random.normal(ks[4], (H * E, O), dtype=jnp.float32) / np.sqrt(H * E), 'bp': jnp.zeros((O,), dtype=jnp.float32)}
    _L0_attn_in = _L0_attn_setup()

    def _L0_ffn_setup():
        import jax, jax.numpy as jnp
        import numpy as np
        B, S, H, F, G = (8, 256, 128, 512, 128)
        EPS = 1e-05

        def _dequant(q, scales, g):
            K, N = q.shape
            w = (q.astype(jnp.float32) - 128.0).reshape(K // g, g, N) * scales[:, None, :]
            return w.reshape(K, N)
        key = jax.random.key(seed)
        ks = jax.random.split(key, 8)
        x = jax.random.normal(ks[0], (B, S, H), dtype=jnp.float32)
        ln_gamma = jnp.ones((H,), jnp.float32)
        ln_beta = jnp.zeros((H,), jnp.float32)
        fc1_q = jax.random.randint(ks[1], (H, F), 0, 32, dtype=jnp.int32)
        fc2_q = jax.random.randint(ks[2], (F, H), 0, 32, dtype=jnp.int32)
        fc1_scales = jax.random.uniform(ks[3], (H // G, F), jnp.float32) * 0.02 + 0.001
        fc2_scales = jax.random.uniform(ks[4], (F // G, H), jnp.float32) * 0.02 + 0.001
        fc1_bias = jax.random.normal(ks[5], (F,), jnp.float32) * 0.02
        fc2_bias = jax.random.normal(ks[6], (H,), jnp.float32) * 0.02
        return {'x': x, 'ln_gamma': ln_gamma, 'ln_beta': ln_beta, 'fc1_q': fc1_q, 'fc1_scales': fc1_scales, 'fc1_bias': fc1_bias, 'fc2_q': fc2_q, 'fc2_scales': fc2_scales, 'fc2_bias': fc2_bias}
    _L0_ffn_in = _L0_ffn_setup()

    def _L1_attn_setup():
        import jax, jax.numpy as jnp
        import numpy as np
        D_MODEL = 128
        HEADS = 16
        SCALE = float(np.sqrt(D_MODEL / HEADS))
        key = jax.random.key(seed)
        ks = jax.random.split(key, 5)
        B, S, D = (4, 256, D_MODEL)
        q = jax.random.normal(ks[0], (B, S, D), dtype=jnp.float32)
        init = 0.02
        wq = jax.random.normal(ks[1], (D, D), dtype=jnp.float32) * init
        wk = jax.random.normal(ks[2], (D, D), dtype=jnp.float32) * init
        wv = jax.random.normal(ks[3], (D, D), dtype=jnp.float32) * init
        wo = jax.random.normal(ks[4], (D, D), dtype=jnp.float32) * init
        return {'q': q, 'wq': wq, 'wk': wk, 'wv': wv, 'wo': wo}
    _L1_attn_in = _L1_attn_setup()

    def _L1_ffn_setup():
        import jax, jax.numpy as jnp
        import numpy as np
        D, H, O, E, TOPK = (128, 512, 128, 8, 2)
        B, S = (4, 128)
        key = jax.random.key(seed)
        ks = jax.random.split(key, 12)
        std = 0.02
        return {'hidden_states': jax.random.normal(ks[0], (B, S, D), dtype=jnp.float32), 'norm_weight': jnp.ones((D,), dtype=jnp.float32), 'router_w': jax.random.normal(ks[1], (E, D), dtype=jnp.float32) * std, 'sw1': jax.random.normal(ks[2], (D, H), dtype=jnp.float32) * (1.0 / np.sqrt(D)), 'sb1': jnp.zeros((H,), dtype=jnp.float32), 'sw2': jax.random.normal(ks[3], (H, O), dtype=jnp.float32) * (1.0 / np.sqrt(H)), 'sb2': jnp.zeros((O,), dtype=jnp.float32), 'ew1': jax.random.normal(ks[4], (E, D, H), dtype=jnp.float32) * (1.0 / np.sqrt(D)), 'eb1': jnp.zeros((E, H), dtype=jnp.float32), 'ew2': jax.random.normal(ks[5], (E, H, O), dtype=jnp.float32) * (1.0 / np.sqrt(H)), 'eb2': jnp.zeros((E, O), dtype=jnp.float32)}
    _L1_ffn_in = _L1_ffn_setup()
    _d = {'L0_attn_query': _L0_attn_in['query'], 'L0_attn_Wq': _L0_attn_in['Wq'], 'L0_attn_Wk': _L0_attn_in['Wk'], 'L0_attn_Wv': _L0_attn_in['Wv'], 'L0_attn_Wp': _L0_attn_in['Wp'], 'L0_attn_bp': _L0_attn_in['bp'], 'L0_ffn_ln_gamma': _L0_ffn_in['ln_gamma'], 'L0_ffn_ln_beta': _L0_ffn_in['ln_beta'], 'L0_ffn_fc1_q': _L0_ffn_in['fc1_q'], 'L0_ffn_fc1_scales': _L0_ffn_in['fc1_scales'], 'L0_ffn_fc1_bias': _L0_ffn_in['fc1_bias'], 'L0_ffn_fc2_q': _L0_ffn_in['fc2_q'], 'L0_ffn_fc2_scales': _L0_ffn_in['fc2_scales'], 'L0_ffn_fc2_bias': _L0_ffn_in['fc2_bias'], 'L1_attn_wq': _L1_attn_in['wq'], 'L1_attn_wk': _L1_attn_in['wk'], 'L1_attn_wv': _L1_attn_in['wv'], 'L1_attn_wo': _L1_attn_in['wo'], 'L1_ffn_norm_weight': _L1_ffn_in['norm_weight'], 'L1_ffn_router_w': _L1_ffn_in['router_w'], 'L1_ffn_sw1': _L1_ffn_in['sw1'], 'L1_ffn_sb1': _L1_ffn_in['sb1'], 'L1_ffn_sw2': _L1_ffn_in['sw2'], 'L1_ffn_sb2': _L1_ffn_in['sb2'], 'L1_ffn_ew1': _L1_ffn_in['ew1'], 'L1_ffn_eb1': _L1_ffn_in['eb1'], 'L1_ffn_ew2': _L1_ffn_in['ew2'], 'L1_ffn_eb2': _L1_ffn_in['eb2']}
    _x0 = _d['L0_attn_query']
    _d['L0_attn_query'] = jax.random.normal(jax.random.fold_in(jax.random.key(seed), 1), (2, 1024, 128), dtype=_x0.dtype)
    del _x0
    return _d

def reference(L0_attn_query, L0_attn_Wq, L0_attn_Wk, L0_attn_Wv, L0_attn_Wp, L0_attn_bp, L0_ffn_ln_gamma, L0_ffn_ln_beta, L0_ffn_fc1_q, L0_ffn_fc1_scales, L0_ffn_fc1_bias, L0_ffn_fc2_q, L0_ffn_fc2_scales, L0_ffn_fc2_bias, L1_attn_wq, L1_attn_wk, L1_attn_wv, L1_attn_wo, L1_ffn_norm_weight, L1_ffn_router_w, L1_ffn_sw1, L1_ffn_sb1, L1_ffn_sw2, L1_ffn_sb2, L1_ffn_ew1, L1_ffn_eb1, L1_ffn_ew2, L1_ffn_eb2):

    def _L0_attn_ref(query, Wq, Wk, Wv, Wp, bp):
        import jax, jax.numpy as jnp
        import numpy as np
        HEAD_SIZE = 64
        B, N, D = query.shape
        H, _, E = Wq.shape
        scale = 1.0 / jnp.sqrt(jnp.asarray(E, query.dtype))
        q = jnp.einsum('bnd,hde->bhne', query, Wq) * scale
        k = jnp.einsum('bmd,hde->bhme', query, Wk)
        v = jnp.einsum('bmd,hde->bhme', query, Wv)
        logits = jnp.einsum('bhne,bhme->bhnm', q, k)
        attn = jax.nn.softmax(logits, axis=-1)
        out = jnp.einsum('bhnm,bhme->bnhe', attn, v)
        out = jnp.swapaxes(out, -1, -2).reshape(B, N, E * H)
        return jnp.dot(out, Wp) + bp

    def _L0_ffn_ref(x, ln_gamma, ln_beta, fc1_q, fc1_scales, fc1_bias, fc2_q, fc2_scales, fc2_bias):
        import jax, jax.numpy as jnp
        import numpy as np
        B, S, H, F, G = (8, 256, 128, 512, 128)
        EPS = 1e-05

        def _dequant(q, scales, g):
            K, N = q.shape
            w = (q.astype(jnp.float32) - 128.0).reshape(K // g, g, N) * scales[:, None, :]
            return w.reshape(K, N)
        residual = x
        mu = jnp.mean(x, axis=-1, keepdims=True)
        var = jnp.mean(jnp.square(x - mu), axis=-1, keepdims=True)
        h = (x - mu) * jax.lax.rsqrt(var + EPS) * ln_gamma + ln_beta
        hf = h.reshape(-1, H)
        w1 = _dequant(fc1_q, fc1_scales, G)
        y = hf @ w1 + fc1_bias
        y = jax.nn.silu(y)
        w2 = _dequant(fc2_q, fc2_scales, G)
        z = y @ w2 + fc2_bias
        return residual + 0.5 * z.reshape(residual.shape)

    def _L1_attn_ref(q, wq, wk, wv, wo):
        import jax, jax.numpy as jnp
        import numpy as np
        D_MODEL = 128
        HEADS = 16
        SCALE = float(np.sqrt(D_MODEL / HEADS))
        B, S, D = q.shape
        Q = jnp.einsum('bsd,ed->bse', q, wq)
        K = jnp.einsum('bsd,ed->bse', q, wk)
        V = jnp.einsum('bsd,ed->bse', q, wv)
        scores = jnp.einsum('bqe,bke->bqk', Q, K) / SCALE
        attn = jax.nn.softmax(scores, axis=-1)
        out = jnp.einsum('bqk,bke->bqe', attn, V)
        out = jnp.transpose(out, (0, 2, 1)).reshape(B, S, D)
        return jnp.einsum('bsd,ed->bse', out, wo)

    def _L1_ffn_ref(hidden_states, norm_weight, router_w, sw1, sb1, sw2, sb2, ew1, eb1, ew2, eb2):
        import jax, jax.numpy as jnp
        import numpy as np
        D, H, O, E, TOPK = (128, 512, 128, 8, 2)
        B, S = (4, 128)
        b, s, d = hidden_states.shape
        var = jnp.mean(jnp.square(hidden_states), axis=-1, keepdims=True)
        normed = hidden_states * jax.lax.rsqrt(var + 1e-08) * norm_weight
        shared = jnp.maximum(normed @ sw1 + sb1, 0.0) @ sw2 + sb2
        flat = normed.reshape(-1, d)
        T = flat.shape[0]
        probs = jax.nn.sigmoid(flat @ router_w.T)
        scores, idx = jax.lax.top_k(probs, TOPK)
        w = scores / (jnp.sum(scores, axis=-1, keepdims=True) + 1e-06)
        comb = jnp.zeros((T, E), dtype=flat.dtype)
        comb = comb.at[jnp.arange(T)[:, None], idx].add(w)
        h = jnp.maximum(jnp.einsum('td,edh->teh', flat, ew1) + eb1[None, :, :], 0.0)
        eo = jnp.einsum('teh,eho->teo', h, ew2) + eb2[None, :, :]
        routed = jnp.einsum('teo,te->to', eo, comb)
        return shared + routed.reshape(b, s, -1)
    x = L0_attn_query
    x = _layernorm(x + _L0_attn_ref(x, L0_attn_Wq, L0_attn_Wk, L0_attn_Wv, L0_attn_Wp, L0_attn_bp), axis=-1)
    x = _layernorm(x + _L0_ffn_ref(x, L0_ffn_ln_gamma, L0_ffn_ln_beta, L0_ffn_fc1_q, L0_ffn_fc1_scales, L0_ffn_fc1_bias, L0_ffn_fc2_q, L0_ffn_fc2_scales, L0_ffn_fc2_bias), axis=-1)
    x = _layernorm(x + _L1_attn_ref(x, L1_attn_wq, L1_attn_wk, L1_attn_wv, L1_attn_wo), axis=-1)
    x = _layernorm(x + _L1_ffn_ref(x, L1_ffn_norm_weight, L1_ffn_router_w, L1_ffn_sw1, L1_ffn_sb1, L1_ffn_sw2, L1_ffn_sb2, L1_ffn_ew1, L1_ffn_eb1, L1_ffn_ew2, L1_ffn_eb2), axis=-1)
    return x

_drawn_inputs = setup_inputs


def setup_inputs(seed=0):
    import zlib

    import numpy as np

    out = dict(_drawn_inputs(seed))
    spreads = {'L0_attn_bp': (0.0, 0.1),
     'L0_ffn_ln_gamma': (1.0, 0.2),
     'L0_ffn_ln_beta': (0.0, 0.1),
     'L1_ffn_norm_weight': (1.0, 0.2),
     'L1_ffn_sb1': (0.0, 0.1),
     'L1_ffn_sb2': (0.0, 0.1),
     'L1_ffn_eb1': (0.0, 0.1),
     'L1_ffn_eb2': (0.0, 0.1)}
    factors = {'L0_ffn_fc2_bias': 3.817}
    for name, (base, spread) in spreads.items():
        noise = np.random.default_rng([zlib.crc32(name.encode()), seed]).standard_normal(out[name].shape)
        drawn = base * np.exp(spread * noise) if base else spread * noise
        out[name] = jnp.asarray(drawn.astype(out[name].dtype))
    for name, factor in factors.items():
        out[name] = (out[name] * factor).astype(out[name].dtype)
    return out
```

```python
from contextlib import ExitStack

import concourse.bass as bass
from concourse import mybir

ALU = mybir.AluOpType
ACT = mybir.ActivationFunctionType
AX = mybir.AxisListType
F32 = mybir.dt.float32
F32R = mybir.dt.float32r
F16 = mybir.dt.float16
BF16 = mybir.dt.bfloat16
I32 = mybir.dt.int32
U32 = mybir.dt.uint32

P = 128
CH = 512


def make_identity(nc, pool, ident, zeroed, done):
    nc.gpsimd.memset(ident[:], 0.0).then_inc(zeroed, 1)
    pool.wait_ge(zeroed, 1)
    nc.gpsimd.affine_select(out=ident[:], in_=ident[:], compare_op=ALU.not_equal, fill=1.0, base=0,
                            pattern=[[-1, P]], channel_multiplier=1).then_inc(done, 1)


def project_values(nc, x, wv, bp, persist):
    X, xhi, xlo, V, ident = (persist[k] for k in ("X", "xhi", "xlo", "V", "ident"))
    T = X.shape[1]
    H = V.shape[1]
    E = P // 2
    HB = CH // E
    with ExitStack() as ctx:
        sb = lambda n, s, d: ctx.enter_context(nc.sbuf_tensor(n, s, d))
        sem = lambda n: ctx.enter_context(nc.semaphore(n))
        wv_raw = sb("wv_raw", [P, H * E], F32)
        wv_hi = sb("wv_hi", [P, H * E], F32R)
        wv_lo = sb("wv_lo", [P, H * E], F32R)
        bp_row = sb("bp_row", [P, P], F32)
        ps_t = [ctx.enter_context(nc.psum_tensor(f"ps_t{i}", [P, CH], F32)) for i in range(2)]
        ps_v = [ctx.enter_context(nc.psum_tensor(f"ps_v{i}", [P, CH], F32)) for i in range(4)]
        x_in, wv_in, bp_in = sem("x_in"), sem("wv_in"), sem("bp_in")
        zeroed, ident_ready, ones_ready = sem("ident_zeroed"), sem("ident_ready"), sem("v_ones_ready")
        turned, xhi_ready, xlo_ready = sem("x_turned"), sem("xhi_ready"), sem("xlo_ready")
        wvhi_ready, wvlo_ready = sem("wvhi_ready"), sem("wvlo_ready")
        v_ready, vhi_done, vlo_done = sem("v_ready"), sem("vhi_done"), sem("vlo_done")
        bias_added = sem("bias_added")
        block = ctx.enter_context(nc.Block())

        @block.sync
        def _(sp):
            sp.dma_start(X[:], x.rearrange("b (t p) d -> p (b t) d", p=P)).then_inc(x_in, 16)

        @block.gpsimd
        def _(pool):
            make_identity(nc, pool, ident, zeroed, ident_ready)
            nc.gpsimd.memset(V[:, :, :, 2 * E + 1:2 * E + 2], 0.0).then_inc(ones_ready, 1)
            nc.gpsimd.memset(V[:, :, :, E:E + 1], 1.0).then_inc(ones_ready, 1)
            pool.wait_ge(ones_ready, 2)

        @block.scalar
        def _(act):
            act.dma_start(wv_raw[:].rearrange("d (h e) -> d h e", e=E), wv.rearrange("h d e -> d h e")).then_inc(wv_in, 16)
            act.dma_start(bp_row[:], bp.rearrange("(o n) -> o n", o=1).broadcast_to((P, P))).then_inc(bp_in, 16)
            act.wait_ge(wv_in, 16)
            nc.scalar.copy(wv_hi[:], wv_raw[:]).then_inc(wvhi_ready, 1)
            for g in range(T // 4):
                act.wait_ge(turned, g + 1)
                nc.scalar.copy(xhi[:, g * CH:(g + 1) * CH], ps_t[g % 2][:]).then_inc(xhi_ready, 1)
            for n in range(T * H // HB):
                t, hb = n // (H // HB), n % (H // HB)
                act.wait_ge(v_ready, n + 1)
                nc.scalar.copy(V[:, hb * HB:(hb + 1) * HB, t, 0:E],
                               ps_v[n % 4][:].rearrange("p (h e) -> p h e", e=E)).then_inc(vhi_done, 1)

        @block.vector
        def _(dve):
            dve.wait_ge(wvhi_ready, 1)
            nc.vector.tensor_tensor(wv_lo[:], wv_raw[:], wv_hi[:].bitcast(F32), ALU.subtract).then_inc(wvlo_ready, 1)
            for g in range(T // 4):
                dve.wait_ge(xhi_ready, g + 1)
                nc.vector.tensor_tensor(xlo[:, g * CH:(g + 1) * CH], ps_t[g % 2][:],
                                        xhi[:, g * CH:(g + 1) * CH].bitcast(F32), ALU.subtract).then_inc(xlo_ready, 1)
            for n in range(T * H // HB):
                t, hb = n // (H // HB), n % (H // HB)
                dve.wait_ge(vhi_done, n + 1)
                nc.vector.tensor_tensor(V[:, hb * HB:(hb + 1) * HB, t, E + 1:2 * E + 1],
                                        ps_v[n % 4][:].rearrange("p (h e) -> p h e", e=E),
                                        V[:, hb * HB:(hb + 1) * HB, t, 0:E], ALU.subtract).then_inc(vlo_done, 1)
            dve.wait_ge(bp_in, 16)
            dve.wait_ge(turned, T // 4)
            nc.vector.tensor_tensor(X[:], X[:], bp_row[:].unsqueeze(1).broadcast_to((P, T, P)), ALU.add).then_inc(bias_added, 1)
            dve.wait_ge(bias_added, 1)

        @block.tensor
        def _(pe):
            pe.wait_ge(x_in, 16)
            pe.wait_ge(ident_ready, 1)
            for g in range(T // 4):
                if g >= 2:
                    pe.wait_ge(xlo_ready, g - 1)
                for j in range(4):
                    last = nc.tensor.transpose(ps_t[g % 2][:, j * P:(j + 1) * P], X[:, 4 * g + j, :], ident[:])
                last.then_inc(turned, 1)
            pe.wait_ge(wvlo_ready, 1)
            for n in range(T * H // HB):
                t, hb = n // (H // HB), n % (H // HB)
                if hb == 0:
                    pe.wait_ge(xlo_ready, t // 4 + 1)
                if n >= 4:
                    pe.wait_ge(vlo_done, n - 3)
                out, ws = ps_v[n % 4][:], slice(hb * CH, (hb + 1) * CH)
                xs = slice(t * P, (t + 1) * P)
                nc.tensor.matmul(out, xlo[:, xs], wv_hi[:, ws], start=True, stop=False)
                nc.tensor.matmul(out, xhi[:, xs], wv_lo[:, ws], start=False, stop=False)
                nc.tensor.matmul(out, xhi[:, xs], wv_hi[:, ws], start=False, stop=True).then_inc(v_ready, 1)


def attend_heads(nc, persist):
    X, xhi, xlo, V, ident = (persist[k] for k in ("X", "xhi", "xlo", "V", "ident"))
    E = P // 2
    T, H, VW = X.shape[1], V.shape[1], V.shape[3]
    PAIRS = H // 2
    TB = T // persist["B"]
    N = TB * P
    PAIRS_ALL = PAIRS * persist["B"]
    UNITS = N // P
    SCALE = float(E) ** -0.5
    DEN = E
    MAX_N = 2 * UNITS
    MAX_LAG = 4
    PV_TO = [0, 4, 9, 14, 18, 23, 28, 32]
    GROUP_AT = {2: 0, 4: 1, 6: 2, 7: 3}
    POOL_UNITS = [(0, 2, 4, 6), (0, 2, 4, 6), (0, 2, 3, 5, 6), (0, 2, 3, 5, 6)]
    OT_AT, Y_AT = 3, 6
    PROJECT_AT = {(0, 4): ("q", 0, 0), (0, 6): ("q", 1, 1), (1, 1): ("k", 0, 2), (1, 4): ("k", 1, 3)}
    by_pool = [sum(len(POOL_UNITS[j]) for j in range(s + 1)) for s in range(4)]
    by_dve = [UNITS * (s + 1) - by_pool[s] for s in range(4)]

    with ExitStack() as ctx:
        sb = lambda n, s, d: ctx.enter_context(nc.sbuf_tensor(n, s, d))
        ps = lambda n: ctx.enter_context(nc.psum_tensor(n, [P, CH], F32))
        sem = lambda n: ctx.enter_context(nc.semaphore(n))
        probs = sb("probs", [P, 2, UNITS, CH], F32)
        probs_lo = sb("probs_lo", [P, 2, UNITS, CH], F16)
        ka = [sb(f"ka{i}", [P, N], F32R) for i in range(2)]
        kb = [sb(f"kb{i}", [P, N], F32R) for i in range(2)]
        qa = [sb(f"qa{i}", [P, N], F32R) for i in range(2)]
        qb = [sb(f"qb{i}", [P, N], F32R) for i in range(2)]
        t_hi = {w: sb(f"t{w}_hi", [P, N], F32R) for w in "qk"}
        t_lo = {w: sb(f"t{w}_lo", [P, N], F32R) for w in "qk"}
        full = sb("full", [P, 2, CH], F32)
        v_now = [sb(f"v_now{i}", [P, UNITS, VW], F16) for i in range(2)]
        w_raw = {w: sb(f"w{w}_raw", [P, P], F32) for w in "qk"}
        w_hi = {w: sb(f"w{w}_hi", [P, P], F32R) for w in "qk"}
        w_lo = {w: sb(f"w{w}_lo", [P, P], F32R) for w in "qk"}
        o_parts = sb("o_parts", [P, 2, 4, P + 1], F32)
        o_pair = sb("o_pair", [P, 2, 4, P], F32)
        o_turned = sb("o_turned", [P, CH], F32)
        wp_pair = sb("wp_pair", [P, P], F32)
        rden = sb("rden", [P, 4], F32)
        maxes = sb("maxes", [P, UNITS, 2], F32)
        negmax = sb("negmax", [P, 4, 4], F32R)
        bank_s = [ps(f"bank_s{i}") for i in range(2)]
        bank_m = [ps(f"bank_m{i}") for i in range(2)]
        bank_o = [ps(f"bank_o{i}") for i in range(2)]
        bank_x = [ps(f"bank_x{i}") for i in range(2)]

        ones_ready = sem("kb_ones_ready")
        staged = sem("weights_staged")
        x_filled = [sem(f"bank_x{i}_filled") for i in range(2)]
        x_taken = [sem(f"bank_x{i}_taken") for i in range(2)]
        lo_made = sem("qk_lo_ready")
        head_in = [sem(f"head{i}_in") for i in range(2)]
        tail_in = [sem(f"tail{i}_in") for i in range(2)]
        v_in = [sem(f"v_now{i}_in") for i in range(2)]
        wp_in = sem("wp_pair_in")
        row_in = [sem(f"negmax_row{i}_in") for i in range(4)]
        m_filled, m_reduced = sem("max_scores_ready"), sem("max_reduced")
        c_ready = sem("negmax_ready")
        s_filled, exp_done = sem("scores_ready"), sem("exp_done")
        lo_dve, lo_pool = sem("probs_lo_by_vector"), sem("probs_lo_by_gpsimd")
        pv_done, rden_ready, o_taken, o_added = sem("pv_done"), sem("rden_ready"), sem("o_taken"), sem("o_added")
        y_added = sem("y_added")
        raw_in = sem("weights_raw_in")
        zeros, zeros_ready = sb("zeros", [P, P], F32), sem("zeros_ready")
        wstep = sem("weights_hi_staged")
        block = ctx.enter_context(nc.Block())

        HEAD_DMAS, TAIL_DMAS = 16 * 4, 16 * 2

        def over_steps(eng, step, before, after):
            before()
            step(0, 0, first=True)
            step(0, 1, first=True)
            with eng.Fori(0, PAIRS_ALL - 1) as i:
                step(i, 2)
                step(i, 3)
                step(i + 1, 0)
                step(i + 1, 1)
            step(PAIRS_ALL - 1, 2, last=True)
            step(PAIRS_ALL - 1, 3, last=True)
            after()

        def max_at(i, s, u, first, last):
            h, c = s // 2, s % 2
            j = c * UNITS + u - MAX_LAG
            if j < 0:
                return None if first and s == 0 else (h, 2 * i + h, j + MAX_N)
            return None if last and h == 1 else (1 - h, 2 * i + h + 1, j)

        x0_base = lambda i: 4 * i - 2
        x1_base = lambda i: 4 * i + 2

        @block.sync
        def _(sp):
            value = lambda v: v if isinstance(v, int) else sp.snap(v)

            def load_head(h, i, used_up=0):
                parts, used_up = value(4 * i + 4), value(used_up)
                if not (isinstance(used_up, int) and used_up == 0):
                    sp.wait_ge(s_filled, used_up)
                sp.wait_ge(lo_made, parts)
                rows = slice(h * E, (h + 1) * E)
                f = lambda a: a.bitcast(F32)
                for dst, src in ((ka[h][0:E, :], t_hi["k"]), (qa[h][0:E, :], t_hi["q"]), (qa[h][E:P, :], t_hi["q"]),
                                 (ka[h][E:P, :], t_lo["k"])):
                    sp.dma_start(f(dst), f(src[rows, :])).then_inc(head_in[h], 16)
                for dst, src in ((kb[h][0:E, :], t_hi["k"]), (qb[h][0:E, :], t_lo["q"])):
                    sp.dma_start(f(dst), f(src[rows, :])).then_inc(tail_in[h], 16)

            def load_row(h, c, n):
                sp.wait_ge(c_ready, n + 1)
                dst = qb[h][E:E + 1, c * CH:(c + 1) * CH].bitcast(F32).rearrange("o (p t) -> o p t", t=4)
                sp.dma_start(dst, negmax[:, 2 * h + c, :].bitcast(F32)).then_inc(row_in[2 * h + c], 16)

            def load_weights(i):
                first_head = value((i % PAIRS) * 2)
                if not (isinstance(i, int) and i == 0):
                    sp.wait_ge(staged, i)
                for w in "qk":
                    src = persist["W" + w][bass.ds(first_head, 2), :, :].rearrange("h d e -> d h e")
                    sp.dma_start(w_raw[w][:].rearrange("d (h e) -> d h e", e=E), src).then_inc(raw_in, 16)

            def load_v(h, i, used_up=0):
                at = (((i % PAIRS) * 2 + h) * T + (i // PAIRS) * TB) * VW
                if not (isinstance(used_up, int) and used_up == 0):
                    sp.wait_ge(pv_done, used_up)
                src = V[:].rearrange("p h t v -> p (h t v)")[:, bass.ds(at, UNITS * VW)]
                sp.dma_start(v_now[h][:].rearrange("p t v -> p (t v)"), src).then_inc(v_in[h], 16)

            def load_wp(i, first):
                head = value((i % PAIRS) * 2)
                if not first:
                    sp.wait_ge(x_taken[0], x0_base(i) + 4)
                rows_of = persist["Wp"].rearrange("(e h) o -> h e o", h=H)
                src = rows_of[bass.ds(head, 2), :, :]
                sp.dma_start(wp_pair[0:E, :], src[0]).then_inc(wp_in, 16)
                sp.dma_start(wp_pair[E:P, :], src[1]).then_inc(wp_in, 16)

            def before():
                load_weights(0)
                load_weights(1)
                load_head(0, 0)
                load_row(0, 0, 0)
                load_row(0, 1, 1)
                load_v(0, 0)

            def step(i, s, first=False, last=False):
                if s == 0:
                    load_head(1, i, 0 if first else 32 * i)
                    load_weights(i + 2)
                    if not first:
                        load_row(0, 1, 4 * i + 1)
                if s == 1:
                    load_v(1, i, 0 if first else 16 * i)
                    load_row(1, 0, 4 * i + 2)
                if s == 2:
                    if not last:
                        load_head(0, i + 1, 32 * i + 16)
                    load_row(1, 1, 4 * i + 3)
                    load_wp(i, isinstance(i, int) and i == 0)
                if s == 3 and not last:
                    load_v(0, i + 1, 16 * i + 8)
                    load_row(0, 0, 4 * i + 4)

            over_steps(sp, step, before, lambda: None)

        @block.tensor
        def _(pe):
            def project(which, c, i, bank, use):
                pe.wait_ge(staged, i + 1)
                if not (isinstance(use, int) and use == 0):
                    pe.wait_ge(x_taken[bank], use)
                col = ((i // PAIRS) % persist["B"]) * N + c * CH
                out, xs = bank_x[bank][:], bass.ds(col, CH)
                nc.tensor.matmul(out, w_lo[which][:], xhi[:, xs], start=True, stop=False)
                nc.tensor.matmul(out, w_hi[which][:], xlo[:, xs], start=False, stop=False)
                nc.tensor.matmul(out, w_hi[which][:], xhi[:, xs], start=False, stop=True).then_inc(x_filled[bank], 1)

            def max_scores(h, j, n):
                if not (isinstance(n, int) and n < 2):
                    pe.wait_ge(m_reduced, n - 1)
                qt, half = j // 2, j % 2
                qs = qa[h][:, (qt // 4) * CH:(qt // 4 + 1) * CH].rearrange("d (p t) -> d t p", t=4)[:, qt % 4, :]
                nc.tensor.matmul(bank_m[j % 2][:], qs, ka[h][:, half * CH:(half + 1) * CH],
                                 start=True, stop=True).then_inc(m_filled, 1)

            def times_v(i, s, done, upto):
                v = v_now[s // 2]
                hi_of = probs[:, s % 2].bitcast(BF16).rearrange("p k (q two) -> p k q two", two=2)
                for n in range(done, upto):
                    qt, kt = n // UNITS, n % UNITS
                    if n == 0 and s % 2 == 0:
                        pe.wait_ge(v_in[s // 2], 16 * (i + 1))
                    if kt == 0 and not (isinstance(i, int) and i == 0 and s == 0 and qt < 2):
                        pe.wait_ge(o_taken, 16 * i + 4 * s + qt - 1)
                    if n == 0:
                        pe.wait_ge(lo_pool, by_pool[3] * i + by_pool[s])
                        pe.wait_ge(lo_dve, by_dve[3] * i + by_dve[s])
                    qs = slice(qt * P, (qt + 1) * P)
                    acc = bank_o[qt % 2]
                    low = lambda: nc.tensor.matmul(acc[:, 0:E + 1], probs_lo[:, s % 2, kt, qs], v[:, kt, 0:E + 1],
                                                   start=False, stop=False, skip_group_check=True)
                    if kt == UNITS - 1:
                        low()
                    last = nc.tensor.matmul(acc[:, 0:2 * E + 1], hi_of[:, kt, qs, 1], v[:, kt, 0:2 * E + 1],
                                            start=(kt == 0), stop=(kt == UNITS - 1))
                    if kt < UNITS - 1:
                        low()
                    else:
                        last.then_inc(pv_done, 1)

            def turn_o(i, c, use):
                pe.wait_ge(o_added, 4 * i + c + 3)
                pe.wait_ge(x_taken[0], use)
                for t in range(4):
                    last = nc.tensor.transpose(bank_x[0][:, t * P:(t + 1) * P], o_pair[:, c, t, :], ident[:])
                last.then_inc(x_filled[0], 1)

            def times_wp(i, c, use):
                pe.wait_ge(x_taken[0], use)
                pe.wait_ge(wp_in, 32 * (i + 1))
                for t in range(4):
                    last = nc.tensor.matmul(bank_x[0][:, t * P:(t + 1) * P], o_turned[:, t * P:(t + 1) * P],
                                            wp_pair[:], start=True, stop=True)
                last.then_inc(x_filled[0], 1)

            def before():
                for n, (w, c, bank, use) in enumerate((("q", 0, 1, 0), ("q", 1, 0, 0), ("k", 0, 1, 1), ("k", 1, 0, 1))):
                    project(w, c, 0, bank, use)
                pe.wait_ge(head_in[0], HEAD_DMAS)
                for j in range(MAX_N):
                    max_scores(0, j, j)

            def step(i, s, first=False, last=False):
                h, c = s // 2, s % 2
                for u in range(UNITS):
                    n = 32 * i + 8 * s + u
                    if u == 0:
                        pe.wait_ge(row_in[s], 16 * (i + 1))
                        if s == 0 and first:
                            pe.wait_ge(ones_ready, 1)
                        if c == 0:
                            pe.wait_ge(tail_in[h], TAIL_DMAS * (i + 1))
                    if not (first and s == 0 and u < 2):
                        pe.wait_ge(exp_done, n - 1)
                    ks, qs = slice(u * P, (u + 1) * P), slice(c * CH, (c + 1) * CH)
                    nc.tensor.matmul(bank_s[u % 2][:], kb[h][0:E + 1, ks], qb[h][0:E + 1, qs], start=True, stop=False)
                    nc.tensor.matmul(bank_s[u % 2][:], ka[h][:, ks], qa[h][:, qs], start=False, stop=True).then_inc(s_filled, 1)
                    if m := max_at(i, s, u, first, last):
                        if m[2] == 0:
                            pe.wait_ge(head_in[1 - h], HEAD_DMAS * (i + 1 + h))
                        max_scores(m[0], m[2], MAX_N * m[1] + m[2])
                    if not (first and s == 0):
                        pi, psn = (i, s - 1) if s else (i - 1, 3)
                        times_v(pi, psn, PV_TO[u - 1] if u else 0, PV_TO[u])
                    if (s, u) in PROJECT_AT:
                        w, ch, k = PROJECT_AT[s, u]
                        project(w, ch, i + 1, 1, x1_base(i) + k)
                    if not first and s < 2:
                        if u == OT_AT:
                            turn_o(i - 1, s, x0_base(i) + 2 * s)
                        if u == Y_AT:
                            times_wp(i - 1, s, x0_base(i) + 2 * s + 1)

            def after():
                i = PAIRS_ALL
                times_v(i - 1, 3, 0, 4 * UNITS)
                for c in range(2):
                    turn_o(i - 1, c, x0_base(i) + 2 * c)
                    times_wp(i - 1, c, x0_base(i) + 2 * c + 1)

            over_steps(pe, step, before, after)

        @block.scalar
        def _(act):
            def take_part(which, c, bank, filled, n):
                act.wait_ge(x_filled[bank], filled)
                cs = slice(c * CH, (c + 1) * CH)
                if not (isinstance(n, int) and n < 2):
                    act.wait_ge(lo_made, n - 1)
                nc.scalar.copy(full[:, c, :], bank_x[bank][:])
                nc.scalar.copy(t_hi[which][:, cs], bank_x[bank][:]).then_inc(x_taken[bank], 1)

            def take_o(i, s, qt):
                act.wait_ge(rden_ready, 16 * i + 4 * s + qt + 1)
                src = bank_o[qt % 2][:]
                out = o_parts[:, s % 2, qt, :]
                nc.scalar.activation(out, src[:, 0:P + 1], ACT.Copy, scale=rden[:, qt:qt + 1]).then_inc(o_taken, 1)

            def take_turned(filled):
                act.wait_ge(x_filled[0], filled)
                nc.scalar.copy(o_turned[:], bank_x[0][:]).then_inc(x_taken[0], 1)

            def before():
                for n, (w, c, bank, filled) in enumerate((("q", 0, 1, 1), ("q", 1, 0, 1), ("k", 0, 1, 2), ("k", 1, 0, 2))):
                    take_part(w, c, bank, filled, n)

            def step(i, s, first=False, last=False):
                c = s % 2
                for u in range(UNITS):
                    if u == 0 and not (first and s < 2):
                        bi, bs = (i, s - 2) if s >= 2 else (i - 1, s + 2)
                        take_o(bi, bs, 3)
                    if u and u - 1 in GROUP_AT and not (first and s == 0):
                        bi, bs = (i, s - 1) if s else (i - 1, 3)
                        if GROUP_AT[u - 1] == 0 and not first:
                            act.wait_ge(o_added, 4 * i + (1 if s == 2 else s - 2))
                        take_o(bi, bs, GROUP_AT[u - 1])
                    if (s, u - 1) in PROJECT_AT:
                        w, ch, k = PROJECT_AT[s, u - 1]
                        if k == 0:
                            for g in (0, 1):
                                act.wait_ge(head_in[g], HEAD_DMAS * (i + 1))
                                act.wait_ge(tail_in[g], TAIL_DMAS * (i + 1))
                        take_part(w, ch, 1, x1_base(i) + k + 1, 4 * (i + 1) + k)
                    n = 32 * i + 8 * s + u
                    act.wait_ge(s_filled, n + 1)
                    nc.scalar.activation(probs[:, c, u, :], bank_s[u % 2][:], ACT.Exp, scale=SCALE).then_inc(exp_done, 1)
                    if not first and s < 2 and u == OT_AT + 1:
                        take_turned(x0_base(i) + 2 * s + 1)

            def after():
                i = PAIRS_ALL
                take_o(i - 1, 2, 3)
                act.wait_ge(o_added, 4 * i - 2)
                for qt in range(4):
                    take_o(i - 1, 3, qt)
                take_turned(x0_base(i) + 1)
                take_turned(x0_base(i) + 3)

            over_steps(act, step, before, after)

        @block.vector
        def _(dve):
            def reduce(j, n):
                dve.wait_ge(m_filled, n + 1)
                nc.vector.tensor_reduce(maxes[:, j // 2, j % 2:j % 2 + 1], bank_m[j % 2][:], AX.X, ALU.max).then_inc(m_reduced, 1)

            def negate(h, c, j0, n, rows):
                dve.wait_ge(m_reduced, j0)
                if not (isinstance(rows, int) and rows < 4):
                    dve.wait_ge(row_in[2 * h + c], n)
                nc.vector.tensor_reduce(negmax[:, 2 * h + c, :], maxes[:, 4 * c:4 * c + 4, :], AX.X, ALU.max,
                                        negate=True).then_inc(c_ready, 1)

            def invert(i, s, qt):
                dve.wait_ge(pv_done, 16 * i + 4 * s + qt + 1)
                nc.vector.reciprocal(rden[:, qt:qt + 1], bank_o[qt % 2][:, DEN:DEN + 1]).then_inc(rden_ready, 1)

            def add_y(i, c, filled):
                dve.wait_ge(x_filled[0], filled)
                x_flat = X[:].rearrange("p t d -> p (t d)")
                at = ((i // PAIRS) * TB + 4 * c) * P
                xs = x_flat[:, bass.ds(at, CH)]
                nc.vector.tensor_tensor(xs, xs, bank_x[0][:], ALU.add).then_inc(x_taken[0], 1)

            def before():
                for h in range(2):
                    last = nc.vector.memset(kb[h][E:E + 1, :].bitcast(F32), 1.0)
                last.then_inc(ones_ready, 1)
                for j in range(MAX_N):
                    reduce(j, j)
                negate(0, 0, MAX_N // 2, 0, 0)
                negate(0, 1, MAX_N, 0, 0)

            def step(i, s, first=False, last=False):
                h, c = s // 2, s % 2
                for u in range(UNITS):
                    if m := max_at(i, s, u, first, last):
                        reduce(m[2], MAX_N * m[1] + m[2])
                    if u == MAX_LAG:
                        if c == 0 and not (first and s == 0):
                            negate(h, 1, MAX_N * (2 * i + h) + MAX_N, 16 * i, 0 if first or (isinstance(i, int) and i == 0) else 4)
                        if c == 1 and not (last and h == 1):
                            negate(1 - h, 0, MAX_N * (2 * i + h + 1) + MAX_N // 2, 16 * (i + h), 0 if first and h == 0 else 4)
                    if u in GROUP_AT and not (first and s == 0):
                        bi, bs = (i, s - 1) if s else (i - 1, 3)
                        invert(bi, bs, GROUP_AT[u])
                    if u not in POOL_UNITS[s]:
                        n = 32 * i + 8 * s + u
                        dve.wait_ge(exp_done, n + 1)
                        p = probs[:, c, u, :]
                        hi = p.bitcast(BF16).rearrange("p (q two) -> p q two", two=2)[:, :, 1]
                        nc.vector.tensor_tensor(probs_lo[:, c, u, :], p, hi, ALU.subtract).then_inc(lo_dve, 1)
                    if not first and s < 2 and u == Y_AT + 1:
                        add_y(i - 1, s, x0_base(i) + 2 * s + 2)

            def after():
                i = PAIRS_ALL
                for qt in range(4):
                    invert(i - 1, 3, qt)
                for c in range(2):
                    add_y(i - 1, c, x0_base(i) + 2 * c + 2)
                dve.wait_ge(x_taken[0], x0_base(i) + 4)

            over_steps(dve, step, before, after)

        @block.gpsimd
        def _(pool):
            def stage(i):
                pool.wait_ge(raw_in, 32 * i + 32)
                for w in "qk":
                    last = nc.gpsimd.tensor_tensor(w_hi[w][:], w_raw[w][:], zeros[:], ALU.add)
                last.then_inc(wstep, 1)
                pool.wait_ge(wstep, i + 1)
                for w in "qk":
                    last = nc.gpsimd.tensor_tensor(w_lo[w][:], w_raw[w][:], w_hi[w][:].bitcast(F32), ALU.subtract)
                last.then_inc(staged, 1)

            def make_lo(which, c, bank, taken):
                pool.wait_ge(x_taken[bank], taken)
                cs = slice(c * CH, (c + 1) * CH)
                nc.gpsimd.tensor_tensor(t_lo[which][:, cs], full[:, c, :], t_hi[which][:, cs].bitcast(F32),
                                        ALU.subtract).then_inc(lo_made, 1)

            def add_o(i, s):
                pool.wait_ge(o_taken, 16 * i + 4 * s + 4)
                h, c = s // 2, s % 2
                nc.gpsimd.tensor_tensor(o_pair[:, c, :, h * E:(h + 1) * E], o_parts[:, c, :, 0:E], o_parts[:, c, :, E + 1:P + 1],
                                        ALU.add).then_inc(o_added, 1)

            def before():
                nc.gpsimd.memset(zeros[:], 0.0).then_inc(zeros_ready, 1)
                pool.wait_ge(zeros_ready, 1)
                stage(0)
                for w, c, bank, taken in (("q", 0, 1, 1), ("q", 1, 0, 1), ("k", 0, 1, 2), ("k", 1, 0, 2)):
                    make_lo(w, c, bank, taken)
                stage(1)

            def step(i, s, first=False, last=False):
                c = s % 2
                for u in range(UNITS):
                    if u in POOL_UNITS[s]:
                        n = 32 * i + 8 * s + u
                        pool.wait_ge(exp_done, n + 1)
                        p = probs[:, c, u, :]
                        hi = p.bitcast(BF16).rearrange("p (q two) -> p q two", two=2)[:, :, 1]
                        nc.gpsimd.tensor_tensor(probs_lo[:, c, u, :], p, hi, ALU.subtract).then_inc(lo_pool, 1)
                    if u == 1 and not (first and s < 2):
                        bi, bs = (i, s - 2) if s >= 2 else (i - 1, s + 2)
                        add_o(bi, bs)
                    if (s, u - 1) in PROJECT_AT:
                        w, ch, k = PROJECT_AT[s, u - 1]
                        make_lo(w, ch, 1, x1_base(i) + k + 1)
                    if s == 1 and u == UNITS - 1:
                        pool.wait_ge(x_filled[1], x1_base(i) + 4)
                        stage(i + 2)

            def after():
                i = PAIRS_ALL
                add_o(i - 1, 2)
                add_o(i - 1, 3)

            over_steps(pool, step, before, after)


class Normaliser:

    def __init__(self, nc, ctx, name, eps):
        sb = lambda n, s: ctx.enter_context(nc.sbuf_tensor(f"{name}_{n}", s, F32))
        sem = lambda n: ctx.enter_context(nc.semaphore(f"{name}_{n}"))
        self.nc, self.eps = nc, eps
        self.stats, self.mv = sb("stats", [P, 4, 6]), sb("mean_var", [P, 4, 2])
        self.std, self.rstd = sb("std", [P, 4]), sb("rstd", [P, 4])
        self.eps_col = sb("eps", [P, 1])
        self.eps_set = sem("eps_set")
        self.summed, self.moments, self.rooted, self.inverted, self.done = (
            sem(n) for n in ("summed", "moments", "rooted", "inverted", "done"))

    def start(self, dve):
        self.nc.vector.memset(self.eps_col[:], self.eps).then_inc(self.eps_set, 1)

    def moments_of(self, dve, src, n):
        if n:
            dve.wait_ge(self.done, n)
        for j in range(4):
            last = self.nc.vector.bn_stats(self.stats[:, j, :], src[:, j, :])
        last.then_inc(self.summed, 1)
        dve.wait_ge(self.summed, n + 1)
        for j in range(4):
            last = self.nc.vector.bn_aggr(self.mv[:, j, :], self.stats[:, j, :])
        last.then_inc(self.moments, 1)

    def root(self, act, n):
        if n == 0:
            act.wait_ge(self.eps_set, 1)
        act.wait_ge(self.moments, n + 1)
        self.nc.scalar.activation(self.std[:], self.mv[:, :, 1], ACT.Sqrt, bias=self.eps_col[:]).then_inc(self.rooted, 1)

    def apply(self, dve, src, dst, n):
        dve.wait_ge(self.rooted, n + 1)
        self.nc.vector.reciprocal(self.rstd[:], self.std[:]).then_inc(self.inverted, 1)
        dve.wait_ge(self.inverted, n + 1)
        for j in range(4):
            last = self.nc.vector.tensor_scalar(dst[:, j, :], src[:, j, :], self.mv[:, j, 0:1], self.rstd[:, j:j + 1],
                                                ALU.subtract, ALU.mult)
        last.then_inc(self.done, 1)


def quantised_ffn(nc, a, persist):
    X, ident = persist["X"], persist["ident"]
    T = X.shape[1]
    CHUNKS = T // 4
    F = a["L0_ffn_fc1_q"].shape[1]
    NF = F // P
    with ExitStack() as ctx:
        sb = lambda n, s, d=F32: ctx.enter_context(nc.sbuf_tensor(n, s, d))
        ps = lambda n: ctx.enter_context(nc.psum_tensor(n, [P, CH], F32))
        sem = lambda n: ctx.enter_context(nc.semaphore(n))
        q1, q2 = sb("q1", [P, F], I32), sb("q2", [P, NF, P], I32)
        s1, s2 = sb("s1_rows", [P, F]), sb("s2_rows", [P, NF, P])
        w1, w2 = sb("w1", [P, F]), sb("w2", [P, NF, P])
        b1_rows, b2_row = sb("b1_rows", [NF, P]), sb("b2_row", [P, P])
        b1 = sb("b1", [P, NF])
        affine_rows, affine = sb("affine_rows", [2, P]), sb("affine", [P, 2])
        half_b2 = sb("half_b2", [P, P])
        h = sb("h", [P, 2, 4, P])
        h_turned = sb("h_turned", [P, 2, CH])
        y = sb("y", [P, NF, CH])
        bank_t = [ps(f"bank_t{i}") for i in range(2)]
        bank_f = [ps(f"bank_f{i}") for i in range(2)]
        bank_z = [ps(f"bank_z{i}") for i in range(2)]
        bank_b = ps("bank_b")
        first_ln, inner_ln, last_ln = (Normaliser(nc, ctx, n, 1e-5) for n in ("ln_in", "ln_ffn", "ln_out"))
        q_in, row_in = sem("ffn_q_in"), sem("ffn_rows_in")
        w1_ready, w2_ready, b2_ready, b2_added = sem("w1_ready"), sem("w2_ready"), sem("half_b2_ready"), sem("half_b2_added")
        cols_turned, cols_ready = sem("columns_turned"), sem("columns_ready")
        turned, turned_taken, f_filled, f_taken = sem("h_turned_filled"), sem("h_turned_taken"), sem("fc1_filled"), sem("silu_done")
        z_filled, z_added = sem("fc2_filled"), sem("fc2_added")
        block = ctx.enter_context(nc.Block())
        chunk = lambda t, c: t[:, 4 * c:4 * c + 4, :]

        @block.sync
        def _(sp):
            row = lambda ap: ap.rearrange("(o n) -> o n", o=1)
            sp.dma_start(b1_rows[:], a["L0_ffn_fc1_bias"].rearrange("(f p) -> f p", p=P)).then_inc(row_in, 16)
            sp.dma_start(affine_rows[0:1, :], row(a["L0_ffn_ln_gamma"])).then_inc(row_in, 16)
            sp.dma_start(affine_rows[1:2, :], row(a["L0_ffn_ln_beta"])).then_inc(row_in, 16)
            sp.dma_start(q1[:], a["L0_ffn_fc1_q"]).then_inc(q_in, 16)
            sp.dma_start(s1[:], a["L0_ffn_fc1_scales"].broadcast_to((P, F))).then_inc(q_in, 16)
            sp.dma_start(q2[:], a["L0_ffn_fc2_q"].rearrange("(f p) n -> p f n", p=P)).then_inc(q_in, 16)
            sp.dma_start(s2[:], a["L0_ffn_fc2_scales"].rearrange("(o f) n -> o f n", o=1).broadcast_to((P, NF, P))).then_inc(q_in, 16)
            sp.dma_start(b2_row[:], row(a["L0_ffn_fc2_bias"]).broadcast_to((P, P))).then_inc(q_in, 16)

        @block.tensor
        def _(pe):
            pe.wait_ge(row_in, 48)
            nc.tensor.transpose(bank_b[:, 0:NF], b1_rows[:], ident[0:NF, 0:NF])
            nc.tensor.transpose(bank_b[:, NF:NF + 2], affine_rows[:], ident[0:2, 0:2]).then_inc(cols_turned, 1)

            def turn(c):
                pe.wait_ge(inner_ln.done, c + 1)
                if c >= 2:
                    pe.wait_ge(turned_taken, c - 1)
                for j in range(4):
                    last = nc.tensor.transpose(bank_t[c % 2][:, j * P:(j + 1) * P], h[:, c % 2, j, :], ident[:])
                last.then_inc(turned, 1)

            turn(0)
            pe.wait_ge(w1_ready, 1)
            for c in range(CHUNKS):
                pe.wait_ge(turned_taken, c + 1)
                for f in range(NF):
                    n = NF * c + f
                    if n >= 2:
                        pe.wait_ge(f_taken, n - 1)
                    nc.tensor.matmul(bank_f[n % 2][:], w1[:, f * P:(f + 1) * P], h_turned[:, c % 2, :],
                                     start=True, stop=True).then_inc(f_filled, 1)
                if c + 1 < CHUNKS:
                    turn(c + 1)
                if c == 0:
                    pe.wait_ge(w2_ready, 1)
                if c >= 2:
                    pe.wait_ge(z_added, c - 1)
                pe.wait_ge(f_taken, NF * (c + 1))
                for j in range(4):
                    for f in range(NF):
                        last = nc.tensor.matmul(bank_z[c % 2][:, j * P:(j + 1) * P], y[:, f, j * P:(j + 1) * P],
                                                w2[:, f, :], start=(f == 0), stop=(f == NF - 1))
                last.then_inc(z_filled, 1)

        @block.scalar
        def _(act):
            act.wait_ge(cols_turned, 1)
            nc.scalar.copy(b1[:], bank_b[:, 0:NF])
            nc.scalar.copy(affine[:], bank_b[:, NF:NF + 2]).then_inc(cols_ready, 1)
            act.wait_ge(cols_ready, 1)

            def silu(c):
                act.wait_ge(turned, c + 1)
                nc.scalar.activation(h_turned[:, c % 2, :], bank_t[c % 2][:], ACT.Identity, bias=affine[:, 1:2],
                                     scale=affine[:, 0:1]).then_inc(turned_taken, 1)
                for f in range(NF):
                    n = NF * c + f
                    act.wait_ge(f_filled, n + 1)
                    if c and f == 0:
                        act.wait_ge(z_filled, c)
                    nc.scalar.activation(y[:, f, :], bank_f[n % 2][:], ACT.Silu, bias=b1[:, f:f + 1]).then_inc(f_taken, 1)

            act.wait_ge(q_in, 80)
            nc.scalar.mul(half_b2[:], b2_row[:], 0.5).then_inc(b2_ready, 1)
            for c in range(CHUNKS):
                first_ln.root(act, c)
                inner_ln.root(act, c)
            for c in range(CHUNKS):
                silu(c)
            for c in range(CHUNKS):
                last_ln.root(act, c)

        @block.vector
        def _(dve):
            for ln in (first_ln, inner_ln, last_ln):
                ln.start(dve)
            for c in range(CHUNKS):
                x = chunk(X, c)
                first_ln.moments_of(dve, x, c)
                first_ln.apply(dve, x, x, c)
                dve.wait_ge(first_ln.done, c + 1)
                inner_ln.moments_of(dve, x, c)
                if c >= 2:
                    dve.wait_ge(turned, c - 1)
                inner_ln.apply(dve, x, h[:, c % 2], c)
                if c == 0:
                    dve.wait_ge(q_in, 80)
                    nc.vector.scalar_tensor_tensor(out=w1[:], in0=q1[:], scalar=-128.0, in1=s1[:], op0=ALU.add,
                                                   op1=ALU.mult).then_inc(w1_ready, 1)
                    nc.vector.scalar_tensor_tensor(out=w2[:], in0=q2[:], scalar=-128.0, in1=s2[:], op0=ALU.add,
                                                   op1=ALU.mult).then_inc(w2_ready, 1)
                    dve.wait_ge(b2_ready, 1)
                dve.wait_ge(inner_ln.done, c + 1)
                nc.vector.scalar_tensor_tensor(out=x, in0=x, scalar=2.0, in1=half_b2[:].unsqueeze(1).broadcast_to((P, 4, P)),
                                               op0=ALU.mult, op1=ALU.add).then_inc(b2_added, 1)
            for c in range(CHUNKS):
                x = chunk(X, c)
                dve.wait_ge(z_filled, c + 1)
                dve.wait_ge(b2_added, c + 1)
                nc.vector.scalar_tensor_tensor(out=x, in0=bank_z[c % 2][:].rearrange("p (t d) -> p t d", d=P), scalar=0.5,
                                               in1=x, op0=ALU.mult, op1=ALU.add).then_inc(z_added, 1)
            for c in range(CHUNKS):
                x = chunk(X, c)
                dve.wait_ge(z_added, c + 1)
                last_ln.moments_of(dve, x, c)
                last_ln.apply(dve, x, x, c)
            dve.wait_ge(last_ln.done, CHUNKS)


def attend_once(nc, a, persist):
    X, ident, B = persist["X"], persist["ident"], persist["B"]
    T = X.shape[1]
    TB = T // B
    N = TB * P
    S = B * N
    HALVES = N // CH
    INV_SCALE = float(P / 16) ** -0.5
    VW = 2 * P + 2
    STEPS = B * HALVES
    with ExitStack() as ctx:
        sb = lambda n, s, d=F32: ctx.enter_context(nc.sbuf_tensor(n, s, d))
        ps = lambda n: ctx.enter_context(nc.psum_tensor(n, [P, CH], F32))
        sem = lambda n: ctx.enter_context(nc.semaphore(n))
        w_rows, w_t = sb("w_rows", [P, 4, P]), sb("w_turned", [P, 4, P])
        xt = sb("xt", [P, S])
        hi = {w: sb(f"{w}1_hi", [P, S], F32R) for w in "qk"}
        lo = {w: sb(f"{w}1_lo", [P, S], F32R) for w in "qk"}
        V = sb("v1_parts", [P, T, VW], F16)
        ones, row = sb("ones_row", [1, P], F32R), sb("negmax_row", [1, S], F32R)
        maxes, negmax = sb("maxes1", [P, T, HALVES]), sb("negmax1", [P, T], F32R)
        probs = sb("probs1", [P, 2, TB, CH])
        probs_lo = sb("probs1_lo", [P, 2, TB, CH], F16)
        rden = sb("rden1", [P, 4])
        o_hi = sb("o_hi", [P, 2, P])
        o_new = sb("o_new", [P, S])
        bank_a = [ps(f"bank_a{i}") for i in range(4)]
        bank_m = [ps(f"bank_n{i}") for i in range(2)]
        bank_o = [ps(f"bank_p{i}") for i in range(2)]
        ln = Normaliser(nc, ctx, "ln_attn", 1e-5)
        w_in, w_turned, w_ready = sem("w1_in"), sem("w1_turned"), sem("w1t_ready")
        a_filled, xt_ready = sem("bank_a_filled"), sem("xt_ready")
        parted, parts_taken = sem("parts_hi_ready"), sem("parts_lo_ready")
        ones_ready = sem("ones1_ready")
        m_filled, m_reduced, c_ready, row_in = sem("max1_scores"), sem("max1_reduced"), sem("negmax1_ready"), sem("negmax1_in")
        exp_done, lo_done, pv_done = sem("exp1_done"), sem("probs1_lo_done"), sem("pv1_done")
        rden_ready, o_scaled, o_taken = sem("rden1_ready"), sem("o1_scaled"), sem("o1_taken")
        y_filled, y_added = sem("y1_filled"), sem("y1_added")
        block = ctx.enter_context(nc.Block())
        CK = S // CH
        X0, Q0, K0, V0, S0 = 0, CK, 2 * CK, 3 * CK, 4 * CK
        Y0 = S0 + STEPS * TB
        queries = lambda t, c: t[:, c * CH:(c + 1) * CH].rearrange("d (p t) -> d t p", t=4)

        @block.sync
        def _(sp):
            for n, w in enumerate(("wq", "wk", "wv", "wo")):
                sp.dma_start(w_rows[:, n, :], a["L1_attn_" + w]).then_inc(w_in, 16)
            for c in range(CK):
                sp.wait_ge(c_ready, c + 1)
                sp.dma_start(row[:, c * CH:(c + 1) * CH].bitcast(F32).rearrange("o (p t) -> o p t", t=4),
                             negmax[:, 4 * c:4 * c + 4].bitcast(F32)).then_inc(row_in, 16)
            sp.wait_ge(row_in, 16 * CK)

        @block.tensor
        def _(pe):
            def bank(n):
                m = n - 4
                if m >= S0:
                    pe.wait_ge(exp_done, m - S0 + 1)
                elif m >= Q0:
                    pe.wait_ge(parts_taken, m - Q0 + 1)
                elif m >= X0:
                    pe.wait_ge(xt_ready, m - X0 + 1)
                return bank_a[n % 4]

            pe.wait_ge(w_in, 64)
            for n in range(4):
                last = nc.tensor.transpose(bank_m[0][:, n * P:(n + 1) * P], w_rows[:, n, :], ident[:])
            last.then_inc(w_turned, 1)
            for c in range(CK):
                b = bank(X0 + c)
                for j in range(4):
                    last = nc.tensor.transpose(b[:, j * P:(j + 1) * P], X[:, 4 * c + j, :], ident[:])
                last.then_inc(a_filled, 1)
            pe.wait_ge(w_ready, 1)
            for w in range(2):
                for c in range(CK):
                    b = bank(Q0 + CK * w + c)
                    pe.wait_ge(xt_ready, c + 1)
                    nc.tensor.matmul(b[:], w_t[:, w, :], xt[:, c * CH:(c + 1) * CH], start=True, stop=True).then_inc(a_filled, 1)
            for c in range(CK):
                b = bank(V0 + c)
                for j in range(4):
                    t = 4 * c + j
                    last = nc.tensor.matmul(b[:, j * P:(j + 1) * P], xt[:, t * P:(t + 1) * P], w_t[:, 2, :], start=True, stop=True)
                last.then_inc(a_filled, 1)

            pe.wait_ge(parts_taken, 2 * CK)
            for n in range(T * HALVES):
                t, half = n // HALVES, n % HALVES
                b, c = t // TB, t // 4
                if n >= 2:
                    pe.wait_ge(m_reduced, n - 1)
                ks = slice(b * N + half * CH, b * N + (half + 1) * CH)
                nc.tensor.matmul(bank_m[n % 2][:], queries(hi["q"], c)[:, t % 4, :], hi["k"][:, ks],
                                 start=True, stop=True).then_inc(m_filled, 1)

            def scores(step, kt):
                b = step // HALVES
                bk = bank(S0 + TB * step + kt)
                if kt == 0:
                    pe.wait_ge(row_in, 16 * CK)
                ks, qs = slice(b * N + kt * P, b * N + (kt + 1) * P), slice(step * CH, (step + 1) * CH)
                nc.tensor.matmul(bk[:], ones[:], row[:, qs], start=True, stop=False)
                nc.tensor.matmul(bk[:], lo["k"][:, ks], hi["q"][:, qs], start=False, stop=False)
                nc.tensor.matmul(bk[:], hi["k"][:, ks], lo["q"][:, qs], start=False, stop=False)
                nc.tensor.matmul(bk[:], hi["k"][:, ks], hi["q"][:, qs], start=False, stop=True).then_inc(a_filled, 1)

            def times_v(step, qt):
                b = step // HALVES
                if qt == 0:
                    pe.wait_ge(lo_done, TB * (step + 1))
                n = 4 * step + qt
                if n >= 2:
                    pe.wait_ge(o_taken, n - 1)
                hi_of = probs[:, step % 2].bitcast(BF16).rearrange("p k (q two) -> p k q two", two=2)
                acc, qs = bank_o[n % 2], slice(qt * P, (qt + 1) * P)
                for kt in range(TB):
                    low = lambda: nc.tensor.matmul(acc[:, 0:P + 1], probs_lo[:, step % 2, kt, qs], V[:, b * TB + kt, 0:P + 1],
                                                   start=False, stop=False, skip_group_check=True)
                    if kt == TB - 1:
                        low()
                    last = nc.tensor.matmul(acc[:, 0:2 * P + 1], hi_of[:, kt, qs, 1], V[:, b * TB + kt, 0:2 * P + 1],
                                            start=(kt == 0), stop=(kt == TB - 1))
                    if kt < TB - 1:
                        low()
                last.then_inc(pv_done, 1)

            for step in range(STEPS + 1):
                for kt in range(TB):
                    if step < STEPS:
                        scores(step, kt)
                    if step and kt % 2:
                        times_v(step - 1, kt // 2)
            for c in range(CK):
                b = bank(Y0 + c)
                pe.wait_ge(o_taken, 4 * HALVES * (c // HALVES + 1))
                for j in range(4):
                    t = 4 * c + j
                    last = nc.tensor.matmul(b[:, j * P:(j + 1) * P], o_new[:, t * P:(t + 1) * P], w_t[:, 3, :], start=True, stop=True)
                last.then_inc(y_filled, 1)

        @block.scalar
        def _(act):
            act.wait_ge(w_turned, 1)
            nc.scalar.copy(w_t[:].rearrange("p n e -> p (n e)"), bank_m[0][:]).then_inc(w_ready, 1)
            for c in range(CK):
                act.wait_ge(a_filled, X0 + c + 1)
                nc.scalar.copy(xt[:, c * CH:(c + 1) * CH], bank_a[(X0 + c) % 4][:]).then_inc(xt_ready, 1)
            for n in range(2 * CK):
                w, c = "qk"[n // CK], n % CK
                act.wait_ge(a_filled, Q0 + n + 1)
                nc.scalar.copy(hi[w][:, c * CH:(c + 1) * CH], bank_a[(Q0 + n) % 4][:]).then_inc(parted, 1)
            for c in range(CK):
                act.wait_ge(a_filled, V0 + c + 1)
                nc.scalar.copy(V[:, 4 * c:4 * c + 4, 0:P], bank_a[(V0 + c) % 4][:].rearrange("p (t d) -> p t d", d=P)).then_inc(parted, 1)
            for step in range(STEPS + 1):
                for kt in range(TB):
                    if step < STEPS:
                        n = TB * step + kt
                        act.wait_ge(a_filled, S0 + n + 1)
                        nc.scalar.activation(probs[:, step % 2, kt, :], bank_a[(S0 + n) % 4][:], ACT.Exp,
                                             scale=INV_SCALE).then_inc(exp_done, 1)
                    if step and kt % 2:
                        g = 4 * (step - 1) + kt // 2
                        act.wait_ge(rden_ready, g + 1)
                        nc.scalar.activation(o_hi[:, g % 2, :], bank_o[g % 2][:, 0:P], ACT.Copy,
                                             scale=rden[:, g % 4:g % 4 + 1]).then_inc(o_scaled, 1)
            for c in range(CK):
                ln.root(act, c)

        @block.vector
        def _(dve):
            ln.start(dve)
            nc.vector.memset(ones[:].bitcast(F32), 1.0)
            nc.vector.memset(V[:, :, P:P + 1], 1.0).then_inc(ones_ready, 1)
            dve.wait_ge(ones_ready, 1)
            for n in range(2 * CK):
                w, c = "qk"[n // CK], n % CK
                cs = slice(c * CH, (c + 1) * CH)
                dve.wait_ge(parted, n + 1)
                nc.vector.tensor_tensor(lo[w][:, cs], bank_a[(Q0 + n) % 4][:], hi[w][:, cs].bitcast(F32),
                                        ALU.subtract).then_inc(parts_taken, 1)
            for c in range(CK):
                dve.wait_ge(parted, 2 * CK + c + 1)
                nc.vector.tensor_tensor(V[:, 4 * c:4 * c + 4, P + 1:2 * P + 1], bank_a[(V0 + c) % 4][:].rearrange("p (t d) -> p t d", d=P),
                                        V[:, 4 * c:4 * c + 4, 0:P], ALU.subtract).then_inc(parts_taken, 1)
            for n in range(T * HALVES):
                t, half = n // HALVES, n % HALVES
                dve.wait_ge(m_filled, n + 1)
                nc.vector.tensor_reduce(maxes[:, t, half:half + 1], bank_m[n % 2][:], AX.X, ALU.max).then_inc(m_reduced, 1)
                if n % (4 * HALVES) == 4 * HALVES - 1:
                    c = t // 4
                    dve.wait_ge(m_reduced, n + 1)
                    nc.vector.tensor_reduce(negmax[:, 4 * c:4 * c + 4], maxes[:, 4 * c:4 * c + 4, :], AX.X, ALU.max,
                                            negate=True).then_inc(c_ready, 1)
            for step in range(STEPS + 1):
                for kt in range(TB):
                    if step < STEPS:
                        n = TB * step + kt
                        dve.wait_ge(exp_done, n + 1)
                        p = probs[:, step % 2, kt, :]
                        nc.vector.tensor_tensor(probs_lo[:, step % 2, kt, :], p,
                                                p.bitcast(BF16).rearrange("p (q two) -> p q two", two=2)[:, :, 1],
                                                ALU.subtract).then_inc(lo_done, 1)
                    if step and kt % 2:
                        g = 4 * (step - 1) + kt // 2
                        dve.wait_ge(pv_done, g + 1)
                        nc.vector.reciprocal(rden[:, g % 4:g % 4 + 1], bank_o[g % 2][:, P:P + 1]).then_inc(rden_ready, 1)
                        dve.wait_ge(o_scaled, g + 1)
                        dst = o_new[:].rearrange("p (b d r) -> p b r d", b=B, r=TB)[:, g // TB, g % TB, :]
                        nc.vector.scalar_tensor_tensor(out=dst, in0=bank_o[g % 2][:, P + 1:2 * P + 1], scalar=rden[:, g % 4:g % 4 + 1],
                                                       in1=o_hi[:, g % 2, :], op0=ALU.mult, op1=ALU.add).then_inc(o_taken, 1)
            for c in range(CK):
                x = X[:, 4 * c:4 * c + 4, :]
                dve.wait_ge(y_filled, c + 1)
                nc.vector.tensor_tensor(x, x, bank_a[(Y0 + c) % 4][:].rearrange("p (t d) -> p t d", d=P), ALU.add).then_inc(y_added, 1)
                dve.wait_ge(y_added, c + 1)
                ln.moments_of(dve, x, c)
                ln.apply(dve, x, x, c)
            dve.wait_ge(ln.done, CK)


def mix_experts(nc, a, persist, out):
    X, ident, B = persist["X"], persist["ident"], persist["B"]
    T = X.shape[1]
    CK = T // 4
    S = T * P
    NE, _, F = a["L1_ffn_ew1"].shape
    NF = F // P
    FFNS = NE + 1
    with ExitStack() as ctx:
        sb = lambda n, s, d=F32: ctx.enter_context(nc.sbuf_tensor(n, s, d))
        ps = lambda n: ctx.enter_context(nc.psum_tensor(n, [P, CH], F32))
        sem = lambda n: ctx.enter_context(nc.semaphore(n))
        w1_raw = sb("e1_raw", [P, 2, F])
        w1_hi, w1_lo = sb("e1_hi", [P, F], F32R), sb("e1_lo", [P, F], F32R)
        w2 = sb("e2", [P, 2, NF, P])
        b1_rows, b1 = sb("e1_bias_rows", [FFNS * NF, P]), sb("e1_bias", [P, FFNS * NF])
        b1_now = sb("e1_bias_now", [P, NF])
        b2, shared_b2 = sb("e2_bias", [NE, P]), sb("shared_b2_rows", [P, P])
        nw_row, nw = sb("norm_w_row", [1, P]), sb("norm_w", [P, 1])
        r_rows, r_t = sb("router_rows", [NE, P]), sb("router_t", [P, NE])
        sums = sb("square_sums", [P, T])
        root, rroot, tiny = sb("rms", [P, T]), sb("rms_inv", [P, T]), sb("rms_eps", [P, 1])
        n_tok = sb("n_tokens", [P, T, P])
        nt, nt_hi, nt_lo = sb("nt", [P, S]), sb("nt_hi", [P, S], F32R), sb("nt_lo", [P, S], F32R)
        prob = sb("gates", [P, T, NE])
        top, top_at = sb("top8", [P, T, NE]), sb("top8_at", [P, T, NE], U32)
        at = sb("top2_at", [P, T, 2])
        lane_i, lane = sb("lane_i", [P, NE], I32), sb("lane", [P, NE])
        first, second = sb("is_first", [P, T, NE]), sb("is_second", [P, T, NE])
        total, share = sb("top2_sum", [P, T]), sb("top2_inv", [P, T])
        comb = sb("comb", [P, FFNS, T])
        comb_e = sb("comb_by_token", [P, T, NE])
        comb_t = sb("comb_t", [NE, S])
        h = sb("hidden", [P, 2, NF, CH])
        y = sb("y_out", [P, T, P])
        bank_h = [ps(f"bank_h{i}") for i in range(4)]
        bank_y = [ps(f"bank_y{i}") for i in range(2)]
        bank_c = [ps(f"bank_c{i}") for i in range(2)]
        ln = Normaliser(nc, ctx, "ln_moe", 1e-5)
        small_in = sem("moe_small_in")
        w_in, w1_hi_ready, w1_lo_ready = sem("expert_in"), sem("expert_hi"), sem("expert_lo")
        small_turned, small_ready = sem("moe_small_turned"), sem("moe_small_ready")
        eps_ready, squared, rooted, inverted, scaled = (sem("moe_" + n) for n in ("eps", "squared", "rooted", "inverted", "scaled"))
        turned, nt_ready, hi_ready, lo_ready = sem("n_turned"), sem("nt_ready"), sem("nt_hi_ready"), sem("nt_lo_ready")
        routed, gated, picked, pick, comb_ready = sem("router_scores"), sem("gates_ready"), sem("top_found"), sem("pick_step"), sem("comb_ready")
        lane_ready = sem("lane_ready")
        comb_turned, comb_t_ready, bias_filled, bias_added = sem("comb_turned"), sem("comb_t_ready"), sem("b2_filled"), sem("b2_added")
        h_filled, h_done, y_filled, y_added = sem("h_filled"), sem("h_done"), sem("y_filled"), sem("y_added_moe")
        b1_ready = sem("e1_bias_ready")
        stored = sem("stored")
        block = ctx.enter_context(nc.Block())
        row = lambda ap: ap.rearrange("(o n) -> o n", o=1)

        @block.sync
        def _(sp):
            def load(half, w1_src, w2_src):
                sp.dma_start(w1_raw[:].rearrange("p k f -> p (k f)")[:, bass.ds(half, F)], w1_src).then_inc(w_in, 16)
                sp.dma_start(w2[:].rearrange("p k f o -> p (k f o)")[:, bass.ds(half, F)].rearrange("p (f o) -> p f o", o=P),
                             w2_src).then_inc(w_in, 16)

            sp.dma_start(nw_row[:], row(a["L1_ffn_norm_weight"])).then_inc(small_in, 16)
            sp.dma_start(r_rows[:], a["L1_ffn_router_w"]).then_inc(small_in, 16)
            sp.dma_start(b1_rows[0:NF, :], a["L1_ffn_sb1"].rearrange("(f p) -> f p", p=P)).then_inc(small_in, 16)
            sp.dma_start(b1_rows[NF:, :], a["L1_ffn_eb1"].rearrange("e (f p) -> (e f) p", p=P)).then_inc(small_in, 16)
            sp.dma_start(b2[:], a["L1_ffn_eb2"]).then_inc(small_in, 16)
            sp.dma_start(shared_b2[:], row(a["L1_ffn_sb2"]).broadcast_to((P, P))).then_inc(small_in, 16)
            load(0, a["L1_ffn_sw1"], a["L1_ffn_sw2"].rearrange("(f p) o -> p f o", p=P))
            sp.wait_ge(w_in, 32)
            load(F, a["L1_ffn_ew1"][0], a["L1_ffn_ew2"][0].rearrange("(f p) o -> p f o", p=P))
            with sp.Fori(1, NE) as e:
                half = ((e + 1) % 2) * F
                sp.wait_ge(y_filled, CK * e)
                load(half, a["L1_ffn_ew1"][bass.ds(e, 1), :, :].rearrange("o d f -> d (o f)"),
                     a["L1_ffn_ew2"][bass.ds(e, 1), :, :].rearrange("o (f p) q -> p (o f) q", p=P))
            o = out.rearrange("b (t p) d -> p (b t) d", p=P)
            for c in range(CK):
                sp.wait_ge(ln.done, c + 1)
                sp.dma_start(o[:, 4 * c:4 * c + 4, :], y[:, 4 * c:4 * c + 4, :]).then_inc(stored, 16)
            sp.wait_ge(stored, 16 * CK)

        @block.gpsimd
        def _(pool):
            nc.gpsimd.iota(lane_i[:], [[1, NE]], base=0, channel_multiplier=0).then_inc(lane_ready, 1)

        @block.tensor
        def _(pe):
            pe.wait_ge(small_in, 96)
            nc.tensor.transpose(bank_c[0][:, 0:FFNS * NF], b1_rows[:], ident[0:FFNS * NF, 0:FFNS * NF])
            nc.tensor.transpose(bank_c[0][:, P:P + NE], r_rows[:], ident[0:NE, 0:NE])
            nc.tensor.transpose(bank_c[0][:, 2 * P:2 * P + 1], nw_row[:], ident[0:1, 0:1]).then_inc(small_turned, 1)
            for c in range(CK):
                pe.wait_ge(scaled, c + 1)
                for j in range(4):
                    last = nc.tensor.transpose(bank_h[c][:, j * P:(j + 1) * P], n_tok[:, 4 * c + j, :], ident[:])
                last.then_inc(turned, 1)
            pe.wait_ge(nt_ready, CK)
            for t in range(T):
                last = nc.tensor.matmul(bank_c[1][:, t * NE:(t + 1) * NE], nt[:, t * P:(t + 1) * P], r_t[:], start=True, stop=True)
            last.then_inc(routed, 1)

            def first_product(n, c):
                if c == 0:
                    pe.wait_ge(w1_lo_ready, n + 1)
                for f in range(NF):
                    k = NF * CK * n + NF * c + f
                    if isinstance(n, int) and n == 0 and c == 0:
                        pe.wait_ge(lo_ready, CK)
                    else:
                        pe.wait_ge(h_done, k - 3)
                    fs, xs = slice(f * P, (f + 1) * P), slice(c * CH, (c + 1) * CH)
                    nc.tensor.matmul(bank_h[f][:], w1_lo[:, fs], nt_hi[:, xs], start=True, stop=False)
                    nc.tensor.matmul(bank_h[f][:], w1_hi[:, fs], nt_lo[:, xs], start=False, stop=False)
                    nc.tensor.matmul(bank_h[f][:], w1_hi[:, fs], nt_hi[:, xs], start=False, stop=True).then_inc(h_filled, 1)

            def second_product(n, c):
                k = CK * n + c
                pe.wait_ge(h_done, NF * (k + 1))
                if not (isinstance(n, int) and n == 0 and c < 2):
                    pe.wait_ge(y_added, k - 1)
                w = w2[:].rearrange("p k f o -> p (k f o)")
                for j in range(4):
                    for f in range(NF):
                        last = nc.tensor.matmul(bank_y[c % 2][:, j * P:(j + 1) * P], h[:, c % 2, f, j * P:(j + 1) * P],
                                                w[:, bass.ds((n % 2) * F + f * P, P)], start=(f == 0), stop=(f == NF - 1))
                last.then_inc(y_filled, 1)

            first_product(0, 0)
            for c in range(1, CK):
                first_product(0, c)
                second_product(0, c - 1)
            pe.wait_ge(comb_ready, 1)
            for c in range(CK):
                if c >= 2:
                    pe.wait_ge(comb_t_ready, c - 1)
                for j in range(4):
                    last = nc.tensor.transpose(bank_c[c % 2][0:NE, j * P:(j + 1) * P], comb_e[:, 4 * c + j, :], ident[:])
                last.then_inc(comb_turned, 1)
            for c in range(CK):
                pe.wait_ge(comb_t_ready, max(c + 1, min(c + 3, CK)))
                if c >= 2:
                    pe.wait_ge(bias_added, c - 1)
                for j in range(4):
                    t = 4 * c + j
                    last = nc.tensor.matmul(bank_c[c % 2][:, j * P:(j + 1) * P], comb_t[:, t * P:(t + 1) * P], b2[:], start=True, stop=True)
                last.then_inc(bias_filled, 1)
            with pe.Fori(1, FFNS) as n:
                first_product(n, 0)
                second_product(n - 1, CK - 1)
                for c in range(1, CK):
                    first_product(n, c)
                    second_product(n, c - 1)
            second_product(FFNS - 1, CK - 1)

        @block.scalar
        def _(act):
            act.wait_ge(squared, T)
            act.wait_ge(eps_ready, 1)
            nc.scalar.activation(root[:], sums[:], ACT.Sqrt, bias=tiny[:], scale=1.0 / P).then_inc(rooted, 1)
            act.wait_ge(small_turned, 1)
            nc.scalar.copy(b1[:], bank_c[0][:, 0:FFNS * NF])
            nc.scalar.copy(r_t[:], bank_c[0][:, P:P + NE])
            nc.scalar.copy(nw[:], bank_c[0][:, 2 * P:2 * P + 1]).then_inc(small_ready, 1)
            act.wait_ge(small_ready, 1)
            for c in range(CK):
                cs = slice(c * CH, (c + 1) * CH)
                act.wait_ge(turned, c + 1)
                nc.scalar.activation(nt[:, cs], bank_h[c][:], ACT.Copy, scale=nw[:]).then_inc(nt_ready, 1)
                act.wait_ge(nt_ready, c + 1)
                nc.scalar.copy(nt_hi[:, cs], nt[:, cs]).then_inc(hi_ready, 1)

            def split_weights(n):
                act.wait_ge(w_in, 32 * n + 32)
                if not (isinstance(n, int) and n == 0):
                    act.wait_ge(h_done, NF * CK * n)
                src = w1_raw[:].rearrange("p k f -> p (k f)")[:, bass.ds((n % 2) * F, F)]
                nc.scalar.copy(w1_hi[:], src).then_inc(w1_hi_ready, 1)
                nc.scalar.copy(b1_now[:], b1[:, bass.ds(NF * n, NF)]).then_inc(b1_ready, 1)
                act.wait_ge(b1_ready, n + 1)

            def rectify(n, c):
                for f in range(NF):
                    k = NF * CK * n + NF * c + f
                    act.wait_ge(h_filled, k + 1)
                    if f == 0 and not (isinstance(n, int) and n == 0 and c < 2):
                        act.wait_ge(y_filled, CK * n + c - 1)
                    nc.scalar.activation(h[:, c % 2, f, :], bank_h[f][:], ACT.Relu,
                                         bias=b1_now[:, f:f + 1]).then_inc(h_done, 1)

            split_weights(0)
            rectify(0, 0)
            act.wait_ge(routed, 1)
            nc.scalar.activation(prob[:].rearrange("p t e -> p (t e)"), bank_c[1][:, 0:T * NE], ACT.Sigmoid).then_inc(gated, 1)
            for c in range(1, CK):
                rectify(0, c)
            for c in range(CK):
                act.wait_ge(comb_turned, c + 1)
                nc.scalar.copy(comb_t[:, c * CH:(c + 1) * CH], bank_c[c % 2][0:NE, :]).then_inc(comb_t_ready, 1)
            with act.Fori(1, FFNS) as n:
                split_weights(n)
                for c in range(CK):
                    rectify(n, c)
            for c in range(CK):
                ln.root(act, c)

        @block.vector
        def _(dve):
            ln.start(dve)
            nc.vector.memset(tiny[:], 1e-8).then_inc(eps_ready, 1)
            for t in range(T):
                nc.vector.tensor_tensor_reduce(out=n_tok[:, t, :], in0=X[:, t, :], in1=X[:, t, :], scale=1.0, scalar=0.0,
                                               op0=ALU.mult, op1=ALU.add, accum_out=sums[:, t:t + 1]).then_inc(squared, 1)
            dve.wait_ge(rooted, 1)
            nc.vector.reciprocal(rroot[:], root[:]).then_inc(inverted, 1)
            dve.wait_ge(inverted, 1)
            for c in range(CK):
                for j in range(4):
                    t = 4 * c + j
                    last = nc.vector.tensor_scalar(n_tok[:, t, :], X[:, t, :], rroot[:, t:t + 1], None, ALU.mult)
                last.then_inc(scaled, 1)
            for c in range(CK):
                cs = slice(c * CH, (c + 1) * CH)
                dve.wait_ge(hi_ready, c + 1)
                nc.vector.tensor_tensor(nt_lo[:, cs], nt[:, cs], nt_hi[:, cs].bitcast(F32), ALU.subtract).then_inc(lo_ready, 1)

            def split_weights(n):
                dve.wait_ge(w1_hi_ready, n + 1)
                src = w1_raw[:].rearrange("p k f -> p (k f)")[:, bass.ds((n % 2) * F, F)]
                nc.vector.tensor_tensor(w1_lo[:], src, w1_hi[:].bitcast(F32), ALU.subtract).then_inc(w1_lo_ready, 1)

            def add_output(n, c):
                k = CK * n + c
                dve.wait_ge(y_filled, k + 1)
                if isinstance(n, int) and n == 0:
                    x = X[:, 4 * c:4 * c + 4, :]
                    nc.vector.tensor_tensor(x, x, bank_y[c % 2][:].rearrange("p (t d) -> p t d", d=P), ALU.add).then_inc(y_added, 1)
                    return
                g = comb[:].rearrange("p n t -> p (n t)")
                if c < CK - 1 or not isinstance(n, int):
                    dve.wait_ge(y_added, k - CK + 1)
                for j in range(4):
                    t = 4 * c + j
                    last = nc.vector.scalar_tensor_tensor(out=X[:, t, :], in0=bank_y[c % 2][:, j * P:(j + 1) * P],
                                                          scalar=g[:, bass.ds(n * T + t, 1)], in1=X[:, t, :],
                                                          op0=ALU.mult, op1=ALU.add)
                last.then_inc(y_added, 1)

            split_weights(0)
            steps = 0

            def then(ins):
                nonlocal steps
                steps += 1
                ins.then_inc(pick, 1)
                dve.wait_ge(pick, steps)

            dve.wait_ge(gated, 1)
            for t in range(T):
                last = nc.vector.max(top[:, t, :], prob[:, t, :])
            last.then_inc(picked, 1)
            dve.wait_ge(picked, 1)
            for t in range(T):
                last = nc.vector.max_index(top_at[:, t, :], top[:, t, :], prob[:, t, :])
            dve.wait_ge(lane_ready, 1)
            then(last)
            wide = lambda ap: ap.broadcast_to((P, T, NE))
            then(nc.vector.tensor_copy(at[:], top_at[:, :, 0:2]))
            then(nc.vector.tensor_copy(lane[:], lane_i[:]))
            then(nc.vector.tensor_tensor(first[:], wide(lane[:].unsqueeze(1)), wide(at[:, :, 0:1]), ALU.is_equal))
            then(nc.vector.tensor_tensor(second[:], wide(lane[:].unsqueeze(1)), wide(at[:, :, 1:2]), ALU.is_equal))
            then(nc.vector.tensor_tensor(first[:], first[:], second[:], ALU.add))
            then(nc.vector.tensor_tensor(first[:], first[:], prob[:], ALU.mult))
            then(nc.vector.tensor_tensor(total[:], top[:, :, 0], top[:, :, 1], ALU.add))
            then(nc.vector.tensor_scalar(total[:], total[:], 1e-6, None, ALU.add))
            then(nc.vector.reciprocal(share[:], total[:]))
            then(nc.vector.tensor_tensor(comb_e[:], first[:], wide(share[:].unsqueeze(2)), ALU.mult))
            then(nc.vector.memset(comb[:, 0, :], 1.0))
            then(nc.vector.tensor_copy(comb[:, 1:FFNS, :].rearrange("p e t -> p t e"), comb_e[:]))
            nc.vector.tensor_tensor(X[:], X[:], shared_b2[:].unsqueeze(1).broadcast_to((P, T, P)), ALU.add).then_inc(comb_ready, 1)
            dve.wait_ge(comb_ready, 1)
            for c in range(CK - 1):
                add_output(0, c)
            for c in range(CK):
                x = X[:, 4 * c:4 * c + 4, :]
                dve.wait_ge(bias_filled, c + 1)
                if c < CK - 1:
                    dve.wait_ge(y_added, c + 1)
                nc.vector.tensor_tensor(x, x, bank_c[c % 2][:].rearrange("p (t d) -> p t d", d=P), ALU.add).then_inc(bias_added, 1)
            dve.wait_ge(bias_added, CK)
            with dve.Fori(1, FFNS) as n:
                split_weights(n)
                add_output(n - 1, CK - 1)
                for c in range(CK - 1):
                    add_output(n, c)
            add_output(FFNS - 1, CK - 1)
            dve.wait_ge(y_added, CK * FFNS)
            for c in range(CK):
                x = X[:, 4 * c:4 * c + 4, :]
                ln.moments_of(dve, x, c)
                ln.apply(dve, x, y[:, 4 * c:4 * c + 4, :], c)


def store_x(nc, persist, out):
    with ExitStack() as ctx:
        stored = ctx.enter_context(nc.semaphore("stored"))
        block = ctx.enter_context(nc.Block())

        @block.sync
        def _(sp):
            sp.dma_start(out.rearrange("b (t p) d -> p (b t) d", p=P), persist["X"][:]).then_inc(stored, 16)
            sp.wait_ge(stored, 16)


def build(nc, a, out, stop=0):
    B, S, D = a["L0_attn_query"].shape
    H, _, E = a["L0_attn_Wq"].shape
    T = B * S // P
    with ExitStack() as ctx:
        sb = lambda n, s, d: ctx.enter_context(nc.sbuf_tensor(n, s, d))
        persist = {"B": B, "Wq": a["L0_attn_Wq"], "Wk": a["L0_attn_Wk"], "Wp": a["L0_attn_Wp"],
                   "X": sb("x_tokens", [P, T, D], F32), "ident": sb("ident", [P, P], F32)}
        with ExitStack() as layer0:
            sb0 = lambda n, s, d: layer0.enter_context(nc.sbuf_tensor(n, s, d))
            persist.update(xhi=sb0("xhi", [P, B * S], F32R), xlo=sb0("xlo", [P, B * S], F32R),
                           V=sb0("v_parts", [P, H, T, 2 * E + 2], F16))
            project_values(nc, a["L0_attn_query"], a["L0_attn_Wv"], a["L0_attn_bp"], persist)
            attend_heads(nc, persist)
        if stop == 1:
            return store_x(nc, persist, out)
        quantised_ffn(nc, a, persist)
        if stop == 2:
            return store_x(nc, persist, out)
        attend_once(nc, a, persist)
        if stop == 3:
            return store_x(nc, persist, out)
        mix_experts(nc, a, persist, out)


_INS = ['L0_attn_query',
        'L0_attn_Wq',
        'L0_attn_Wk',
        'L0_attn_Wv',
        'L0_attn_Wp',
        'L0_attn_bp',
        'L0_ffn_ln_gamma',
        'L0_ffn_ln_beta',
        'L0_ffn_fc1_q',
        'L0_ffn_fc1_scales',
        'L0_ffn_fc1_bias',
        'L0_ffn_fc2_q',
        'L0_ffn_fc2_scales',
        'L0_ffn_fc2_bias',
        'L1_attn_wq',
        'L1_attn_wk',
        'L1_attn_wv',
        'L1_attn_wo',
        'L1_ffn_norm_weight',
        'L1_ffn_router_w',
        'L1_ffn_sw1',
        'L1_ffn_sb1',
        'L1_ffn_sw2',
        'L1_ffn_sb2',
        'L1_ffn_ew1',
        'L1_ffn_eb1',
        'L1_ffn_ew2',
        'L1_ffn_eb2']
_OUTS = [((2, 1024, 128), "float32")]


def kernel(**inputs):
    import numpy as _np
    import concourse.bacc as _bacc
    from concourse import mybir as _mybir
    from concourse.bass_utils import run_bass_kernel_spmd as _run

    nc = _bacc.Bacc("TRN2", target_bir_lowering=False, num_devices=1)
    arrays, args = {}, {}
    for name in _INS:
        a = _np.ascontiguousarray(inputs[name])
        arrays[f"in_{name}_dram"] = a
        args[name] = nc.dram_tensor(f"in_{name}_dram", a.shape, _mybir.dt.from_np(a.dtype), kind="ExternalInput").ap()
    shape, dtype = _OUTS[0]
    out = nc.dram_tensor("out_0_dram", shape, _mybir.dt.from_np(_np.dtype(dtype)), kind="ExternalOutput").ap()
    build(nc, args, out)
    r = _run(nc, [arrays], core_ids=[0])
    return r.results[0]["out_0_dram"]
```

```python
from contextlib import ExitStack

import concourse.bass as bass
from concourse import mybir

ALU = mybir.AluOpType
ACT = mybir.ActivationFunctionType
AX = mybir.AxisListType
F32 = mybir.dt.float32
F32R = mybir.dt.float32r
F16 = mybir.dt.float16
BF16 = mybir.dt.bfloat16
I32 = mybir.dt.int32
U32 = mybir.dt.uint32

P = 128
CH = 512


def make_identity(nc, pool, ident, zeroed, done):
    nc.gpsimd.memset(ident[:], 0.0).then_inc(zeroed, 1)
    pool.wait_ge(zeroed, 1)
    nc.gpsimd.affine_select(out=ident[:], in_=ident[:], compare_op=ALU.not_equal, fill=1.0, base=0,
                            pattern=[[-1, P]], channel_multiplier=1).then_inc(done, 1)


def project_values(nc, x, wv, bp, persist):
    X, xhi, xlo, V, ident = (persist[k] for k in ("X", "xhi", "xlo", "V", "ident"))
    T = X.shape[1]
    H = V.shape[1]
    E = P // 2
    HB = CH // E
    with ExitStack() as ctx:
        sb = lambda n, s, d: ctx.enter_context(nc.sbuf_tensor(n, s, d))
        sem = lambda n: ctx.enter_context(nc.semaphore(n))
        wv_raw = sb("wv_raw", [P, H * E], F32)
        wv_hi = sb("wv_hi", [P, H * E], F32R)
        wv_lo = sb("wv_lo", [P, H * E], F32R)
        bp_row = sb("bp_row", [P, P], F32)
        ps_t = [ctx.enter_context(nc.psum_tensor(f"ps_t{i}", [P, CH], F32)) for i in range(2)]
        ps_v = [ctx.enter_context(nc.psum_tensor(f"ps_v{i}", [P, CH], F32)) for i in range(4)]
        x_in, wv_in, bp_in = sem("x_in"), sem("wv_in"), sem("bp_in")
        zeroed, ident_ready, ones_ready = sem("ident_zeroed"), sem("ident_ready"), sem("v_ones_ready")
        turned, xhi_ready, xlo_ready = sem("x_turned"), sem("xhi_ready"), sem("xlo_ready")
        wvhi_ready, wvlo_ready = sem("wvhi_ready"), sem("wvlo_ready")
        v_ready, vhi_done, vlo_done = sem("v_ready"), sem("vhi_done"), sem("vlo_done")
        bias_added = sem("bias_added")
        block = ctx.enter_context(nc.Block())

        @block.sync
        def _(sp):
            sp.dma_start(X[:], x.rearrange("b (t p) d -> p (b t) d", p=P)).then_inc(x_in, 16)

        @block.gpsimd
        def _(pool):
            make_identity(nc, pool, ident, zeroed, ident_ready)
            nc.gpsimd.memset(V[:, :, :, 2 * E + 1:2 * E + 2], 0.0).then_inc(ones_ready, 1)
            nc.gpsimd.memset(V[:, :, :, E:E + 1], 1.0).then_inc(ones_ready, 1)
            pool.wait_ge(ones_ready, 2)

        @block.scalar
        def _(act):
            act.dma_start(wv_raw[:].rearrange("d (h e) -> d h e", e=E), wv.rearrange("h d e -> d h e")).then_inc(wv_in, 16)
            act.dma_start(bp_row[:], bp.rearrange("(o n) -> o n", o=1).broadcast_to((P, P))).then_inc(bp_in, 16)
            act.wait_ge(wv_in, 16)
            nc.scalar.copy(wv_hi[:], wv_raw[:]).then_inc(wvhi_ready, 1)
            for g in range(T // 4):
                act.wait_ge(turned, g + 1)
                nc.scalar.copy(xhi[:, g * CH:(g + 1) * CH], ps_t[g % 2][:]).then_inc(xhi_ready, 1)
            for n in range(T * H // HB):
                t, hb = n // (H // HB), n % (H // HB)
                act.wait_ge(v_ready, n + 1)
                nc.scalar.copy(V[:, hb * HB:(hb + 1) * HB, t, 0:E],
                               ps_v[n % 4][:].rearrange("p (h e) -> p h e", e=E)).then_inc(vhi_done, 1)

        @block.vector
        def _(dve):
            dve.wait_ge(wvhi_ready, 1)
            nc.vector.tensor_tensor(wv_lo[:], wv_raw[:], wv_hi[:].bitcast(F32), ALU.subtract).then_inc(wvlo_ready, 1)
            for g in range(T // 4):
                dve.wait_ge(xhi_ready, g + 1)
                nc.vector.tensor_tensor(xlo[:, g * CH:(g + 1) * CH], ps_t[g % 2][:],
                                        xhi[:, g * CH:(g + 1) * CH].bitcast(F32), ALU.subtract).then_inc(xlo_ready, 1)
            for n in range(T * H // HB):
                t, hb = n // (H // HB), n % (H // HB)
                dve.wait_ge(vhi_done, n + 1)
                nc.vector.tensor_tensor(V[:, hb * HB:(hb + 1) * HB, t, E + 1:2 * E + 1],
                                        ps_v[n % 4][:].rearrange("p (h e) -> p h e", e=E),
                                        V[:, hb * HB:(hb + 1) * HB, t, 0:E], ALU.subtract).then_inc(vlo_done, 1)
            dve.wait_ge(bp_in, 16)
            dve.wait_ge(turned, T // 4)
            nc.vector.tensor_tensor(X[:], X[:], bp_row[:].unsqueeze(1).broadcast_to((P, T, P)), ALU.add).then_inc(bias_added, 1)
            dve.wait_ge(bias_added, 1)

        @block.tensor
        def _(pe):
            pe.wait_ge(x_in, 16)
            pe.wait_ge(ident_ready, 1)
            for g in range(T // 4):
                if g >= 2:
                    pe.wait_ge(xlo_ready, g - 1)
                for j in range(4):
                    last = nc.tensor.transpose(ps_t[g % 2][:, j * P:(j + 1) * P], X[:, 4 * g + j, :], ident[:])
                last.then_inc(turned, 1)
            pe.wait_ge(wvlo_ready, 1)
            for n in range(T * H // HB):
                t, hb = n // (H // HB), n % (H // HB)
                if hb == 0:
                    pe.wait_ge(xlo_ready, t // 4 + 1)
                if n >= 4:
                    pe.wait_ge(vlo_done, n - 3)
                out, ws = ps_v[n % 4][:], slice(hb * CH, (hb + 1) * CH)
                xs = slice(t * P, (t + 1) * P)
                nc.tensor.matmul(out, xlo[:, xs], wv_hi[:, ws], start=True, stop=False)
                nc.tensor.matmul(out, xhi[:, xs], wv_lo[:, ws], start=False, stop=False)
                nc.tensor.matmul(out, xhi[:, xs], wv_hi[:, ws], start=False, stop=True).then_inc(v_ready, 1)


def attend_heads(nc, persist):
    X, xhi, xlo, V, ident = (persist[k] for k in ("X", "xhi", "xlo", "V", "ident"))
    E = P // 2
    T, H, VW = X.shape[1], V.shape[1], V.shape[3]
    PAIRS = H // 2
    TB = T // persist["B"]
    N = TB * P
    PAIRS_ALL = PAIRS * persist["B"]
    UNITS = N // P
    SCALE = float(E) ** -0.5
    DEN = E
    MAX_N = 2 * UNITS
    MAX_LAG = 4
    PV_TO = [0, 4, 9, 14, 18, 23, 28, 32]
    GROUP_AT = {2: 0, 4: 1, 6: 2, 7: 3}
    POOL_UNITS = [(0, 2, 4, 6), (0, 2, 4, 6), (0, 2, 3, 5, 6), (0, 2, 3, 5, 6)]
    OT_AT, Y_AT = 3, 6
    PROJECT_AT = {(0, 4): ("q", 0, 0), (0, 6): ("q", 1, 1), (1, 1): ("k", 0, 2), (1, 4): ("k", 1, 3)}
    by_pool = [sum(len(POOL_UNITS[j]) for j in range(s + 1)) for s in range(4)]
    by_dve = [UNITS * (s + 1) - by_pool[s] for s in range(4)]

    with ExitStack() as ctx:
        sb = lambda n, s, d: ctx.enter_context(nc.sbuf_tensor(n, s, d))
        ps = lambda n: ctx.enter_context(nc.psum_tensor(n, [P, CH], F32))
        sem = lambda n: ctx.enter_context(nc.semaphore(n))
        probs = sb("probs", [P, 2, UNITS, CH], F32)
        probs_lo = sb("probs_lo", [P, 2, UNITS, CH], F16)
        ka = [sb(f"ka{i}", [P, N], F32R) for i in range(2)]
        kb = [sb(f"kb{i}", [P, N], F32R) for i in range(2)]
        qa = [sb(f"qa{i}", [P, N], F32R) for i in range(2)]
        qb = [sb(f"qb{i}", [P, N], F32R) for i in range(2)]
        t_hi = {w: sb(f"t{w}_hi", [P, N], F32R) for w in "qk"}
        t_lo = {w: sb(f"t{w}_lo", [P, N], F32R) for w in "qk"}
        full = sb("full", [P, 2, CH], F32)
        v_now = [sb(f"v_now{i}", [P, UNITS, VW], F16) for i in range(2)]
        w_raw = {w: sb(f"w{w}_raw", [P, P], F32) for w in "qk"}
        w_hi = {w: sb(f"w{w}_hi", [P, P], F32R) for w in "qk"}
        w_lo = {w: sb(f"w{w}_lo", [P, P], F32R) for w in "qk"}
        o_parts = sb("o_parts", [P, 2, 4, P + 1], F32)
        o_pair = sb("o_pair", [P, 2, 4, P], F32)
        o_turned = sb("o_turned", [P, CH], F32)
        wp_pair = sb("wp_pair", [P, P], F32)
        rden = sb("rden", [P, 4], F32)
        maxes = sb("maxes", [P, UNITS, 2], F32)
        negmax = sb("negmax", [P, 4, 4], F32R)
        bank_s = [ps(f"bank_s{i}") for i in range(2)]
        bank_m = [ps(f"bank_m{i}") for i in range(2)]
        bank_o = [ps(f"bank_o{i}") for i in range(2)]
        bank_x = [ps(f"bank_x{i}") for i in range(2)]

        ones_ready = sem("kb_ones_ready")
        staged = sem("weights_staged")
        x_filled = [sem(f"bank_x{i}_filled") for i in range(2)]
        x_taken = [sem(f"bank_x{i}_taken") for i in range(2)]
        lo_made = sem("qk_lo_ready")
        head_in = [sem(f"head{i}_in") for i in range(2)]
        tail_in = [sem(f"tail{i}_in") for i in range(2)]
        v_in = [sem(f"v_now{i}_in") for i in range(2)]
        wp_in = sem("wp_pair_in")
        row_in = [sem(f"negmax_row{i}_in") for i in range(4)]
        m_filled, m_reduced = sem("max_scores_ready"), sem("max_reduced")
        c_ready = sem("negmax_ready")
        s_filled, exp_done = sem("scores_ready"), sem("exp_done")
        lo_dve, lo_pool = sem("probs_lo_by_vector"), sem("probs_lo_by_gpsimd")
        pv_done, rden_ready, o_taken, o_added = sem("pv_done"), sem("rden_ready"), sem("o_taken"), sem("o_added")
        y_added = sem("y_added")
        raw_in = sem("weights_raw_in")
        zeros, zeros_ready = sb("zeros", [P, P], F32), sem("zeros_ready")
        wstep = sem("weights_hi_staged")
        block = ctx.enter_context(nc.Block())

        HEAD_DMAS, TAIL_DMAS = 16 * 4, 16 * 2

        def over_steps(eng, step, before, after):
            before()
            step(0, 0, first=True)
            step(0, 1, first=True)
            with eng.Fori(0, PAIRS_ALL - 1) as i:
                step(i, 2)
                step(i, 3)
                step(i + 1, 0)
                step(i + 1, 1)
            step(PAIRS_ALL - 1, 2, last=True)
            step(PAIRS_ALL - 1, 3, last=True)
            after()

        def max_at(i, s, u, first, last):
            h, c = s // 2, s % 2
            j = c * UNITS + u - MAX_LAG
            if j < 0:
                return None if first and s == 0 else (h, 2 * i + h, j + MAX_N)
            return None if last and h == 1 else (1 - h, 2 * i + h + 1, j)

        x0_base = lambda i: 4 * i - 2
        x1_base = lambda i: 4 * i + 2

        @block.sync
        def _(sp):
            value = lambda v: v if isinstance(v, int) else sp.snap(v)

            def load_head(h, i, used_up=0):
                parts, used_up = value(4 * i + 4), value(used_up)
                if not (isinstance(used_up, int) and used_up == 0):
                    sp.wait_ge(s_filled, used_up)
                sp.wait_ge(lo_made, parts)
                rows = slice(h * E, (h + 1) * E)
                f = lambda a: a.bitcast(F32)
                for dst, src in ((ka[h][0:E, :], t_hi["k"]), (qa[h][0:E, :], t_hi["q"]), (qa[h][E:P, :], t_hi["q"]),
                                 (ka[h][E:P, :], t_lo["k"])):
                    sp.dma_start(f(dst), f(src[rows, :])).then_inc(head_in[h], 16)
                for dst, src in ((kb[h][0:E, :], t_hi["k"]), (qb[h][0:E, :], t_lo["q"])):
                    sp.dma_start(f(dst), f(src[rows, :])).then_inc(tail_in[h], 16)

            def load_row(h, c, n):
                sp.wait_ge(c_ready, n + 1)
                dst = qb[h][E:E + 1, c * CH:(c + 1) * CH].bitcast(F32).rearrange("o (p t) -> o p t", t=4)
                sp.dma_start(dst, negmax[:, 2 * h + c, :].bitcast(F32)).then_inc(row_in[2 * h + c], 16)

            def load_weights(i):
                first_head = value((i % PAIRS) * 2)
                if not (isinstance(i, int) and i == 0):
                    sp.wait_ge(staged, i)
                for w in "qk":
                    src = persist["W" + w][bass.ds(first_head, 2), :, :].rearrange("h d e -> d h e")
                    sp.dma_start(w_raw[w][:].rearrange("d (h e) -> d h e", e=E), src).then_inc(raw_in, 16)

            def load_v(h, i, used_up=0):
                at = (((i % PAIRS) * 2 + h) * T + (i // PAIRS) * TB) * VW
                if not (isinstance(used_up, int) and used_up == 0):
                    sp.wait_ge(pv_done, used_up)
                src = V[:].rearrange("p h t v -> p (h t v)")[:, bass.ds(at, UNITS * VW)]
                sp.dma_start(v_now[h][:].rearrange("p t v -> p (t v)"), src).then_inc(v_in[h], 16)

            def load_wp(i, first):
                head = value((i % PAIRS) * 2)
                if not first:
                    sp.wait_ge(x_taken[0], x0_base(i) + 4)
                rows_of = persist["Wp"].rearrange("(e h) o -> h e o", h=H)
                src = rows_of[bass.ds(head, 2), :, :]
                sp.dma_start(wp_pair[0:E, :], src[0]).then_inc(wp_in, 16)
                sp.dma_start(wp_pair[E:P, :], src[1]).then_inc(wp_in, 16)

            def before():
                load_weights(0)
                load_weights(1)
                load_head(0, 0)
                load_row(0, 0, 0)
                load_row(0, 1, 1)
                load_v(0, 0)

            def step(i, s, first=False, last=False):
                if s == 0:
                    load_head(1, i, 0 if first else 32 * i)
                    load_weights(i + 2)
                    if not first:
                        load_row(0, 1, 4 * i + 1)
                if s == 1:
                    load_v(1, i, 0 if first else 16 * i)
                    load_row(1, 0, 4 * i + 2)
                if s == 2:
                    if not last:
                        load_head(0, i + 1, 32 * i + 16)
                    load_row(1, 1, 4 * i + 3)
                    load_wp(i, isinstance(i, int) and i == 0)
                if s == 3 and not last:
                    load_v(0, i + 1, 16 * i + 8)
                    load_row(0, 0, 4 * i + 4)

            over_steps(sp, step, before, lambda: None)

        @block.tensor
        def _(pe):
            def project(which, c, i, bank, use):
                pe.wait_ge(staged, i + 1)
                if not (isinstance(use, int) and use == 0):
                    pe.wait_ge(x_taken[bank], use)
                col = ((i // PAIRS) % persist["B"]) * N + c * CH
                out, xs = bank_x[bank][:], bass.ds(col, CH)
                nc.tensor.matmul(out, w_lo[which][:], xhi[:, xs], start=True, stop=False)
                nc.tensor.matmul(out, w_hi[which][:], xlo[:, xs], start=False, stop=False)
                nc.tensor.matmul(out, w_hi[which][:], xhi[:, xs], start=False, stop=True).then_inc(x_filled[bank], 1)

            def max_scores(h, j, n):
                if not (isinstance(n, int) and n < 2):
                    pe.wait_ge(m_reduced, n - 1)
                qt, half = j // 2, j % 2
                qs = qa[h][:, (qt // 4) * CH:(qt // 4 + 1) * CH].rearrange("d (p t) -> d t p", t=4)[:, qt % 4, :]
                nc.tensor.matmul(bank_m[j % 2][:], qs, ka[h][:, half * CH:(half + 1) * CH],
                                 start=True, stop=True).then_inc(m_filled, 1)

            def times_v(i, s, done, upto):
                v = v_now[s // 2]
                hi_of = probs[:, s % 2].bitcast(BF16).rearrange("p k (q two) -> p k q two", two=2)
                for n in range(done, upto):
                    qt, kt = n // UNITS, n % UNITS
                    if n == 0 and s % 2 == 0:
                        pe.wait_ge(v_in[s // 2], 16 * (i + 1))
                    if kt == 0 and not (isinstance(i, int) and i == 0 and s == 0 and qt < 2):
                        pe.wait_ge(o_taken, 16 * i + 4 * s + qt - 1)
                    if n == 0:
                        pe.wait_ge(lo_pool, by_pool[3] * i + by_pool[s])
                        pe.wait_ge(lo_dve, by_dve[3] * i + by_dve[s])
                    qs = slice(qt * P, (qt + 1) * P)
                    acc = bank_o[qt % 2]
                    low = lambda: nc.tensor.matmul(acc[:, 0:E + 1], probs_lo[:, s % 2, kt, qs], v[:, kt, 0:E + 1],
                                                   start=False, stop=False, skip_group_check=True)
                    if kt == UNITS - 1:
                        low()
                    last = nc.tensor.matmul(acc[:, 0:2 * E + 1], hi_of[:, kt, qs, 1], v[:, kt, 0:2 * E + 1],
                                            start=(kt == 0), stop=(kt == UNITS - 1))
                    if kt < UNITS - 1:
                        low()
                    else:
                        last.then_inc(pv_done, 1)

            def turn_o(i, c, use):
                pe.wait_ge(o_added, 4 * i + c + 3)
                pe.wait_ge(x_taken[0], use)
                for t in range(4):
                    last = nc.tensor.transpose(bank_x[0][:, t * P:(t + 1) * P], o_pair[:, c, t, :], ident[:])
                last.then_inc(x_filled[0], 1)

            def times_wp(i, c, use):
                pe.wait_ge(x_taken[0], use)
                pe.wait_ge(wp_in, 32 * (i + 1))
                for t in range(4):
                    last = nc.tensor.matmul(bank_x[0][:, t * P:(t + 1) * P], o_turned[:, t * P:(t + 1) * P],
                                            wp_pair[:], start=True, stop=True)
                last.then_inc(x_filled[0], 1)

            def before():
                for n, (w, c, bank, use) in enumerate((("q", 0, 1, 0), ("q", 1, 0, 0), ("k", 0, 1, 1), ("k", 1, 0, 1))):
                    project(w, c, 0, bank, use)
                pe.wait_ge(head_in[0], HEAD_DMAS)
                for j in range(MAX_N):
                    max_scores(0, j, j)

            def step(i, s, first=False, last=False):
                h, c = s // 2, s % 2
                for u in range(UNITS):
                    n = 32 * i + 8 * s + u
                    if u == 0:
                        pe.wait_ge(row_in[s], 16 * (i + 1))
                        if s == 0 and first:
                            pe.wait_ge(ones_ready, 1)
                        if c == 0:
                            pe.wait_ge(tail_in[h], TAIL_DMAS * (i + 1))
                    if not (first and s == 0 and u < 2):
                        pe.wait_ge(exp_done, n - 1)
                    ks, qs = slice(u * P, (u + 1) * P), slice(c * CH, (c + 1) * CH)
                    nc.tensor.matmul(bank_s[u % 2][:], kb[h][0:E + 1, ks], qb[h][0:E + 1, qs], start=True, stop=False)
                    nc.tensor.matmul(bank_s[u % 2][:], ka[h][:, ks], qa[h][:, qs], start=False, stop=True).then_inc(s_filled, 1)
                    if m := max_at(i, s, u, first, last):
                        if m[2] == 0:
                            pe.wait_ge(head_in[1 - h], HEAD_DMAS * (i + 1 + h))
                        max_scores(m[0], m[2], MAX_N * m[1] + m[2])
                    if not (first and s == 0):
                        pi, psn = (i, s - 1) if s else (i - 1, 3)
                        times_v(pi, psn, PV_TO[u - 1] if u else 0, PV_TO[u])
                    if (s, u) in PROJECT_AT:
                        w, ch, k = PROJECT_AT[s, u]
                        project(w, ch, i + 1, 1, x1_base(i) + k)
                    if not first and s < 2:
                        if u == OT_AT:
                            turn_o(i - 1, s, x0_base(i) + 2 * s)
                        if u == Y_AT:
                            times_wp(i - 1, s, x0_base(i) + 2 * s + 1)

            def after():
                i = PAIRS_ALL
                times_v(i - 1, 3, 0, 4 * UNITS)
                for c in range(2):
                    turn_o(i - 1, c, x0_base(i) + 2 * c)
                    times_wp(i - 1, c, x0_base(i) + 2 * c + 1)

            over_steps(pe, step, before, after)

        @block.scalar
        def _(act):
            def take_part(which, c, bank, filled, n):
                act.wait_ge(x_filled[bank], filled)
                cs = slice(c * CH, (c + 1) * CH)
                if not (isinstance(n, int) and n < 2):
                    act.wait_ge(lo_made, n - 1)
                nc.scalar.copy(full[:, c, :], bank_x[bank][:])
                nc.scalar.copy(t_hi[which][:, cs], bank_x[bank][:]).then_inc(x_taken[bank], 1)

            def take_o(i, s, qt):
                act.wait_ge(rden_ready, 16 * i + 4 * s + qt + 1)
                src = bank_o[qt % 2][:]
                out = o_parts[:, s % 2, qt, :]
                nc.scalar.activation(out, src[:, 0:P + 1], ACT.Copy, scale=rden[:, qt:qt + 1]).then_inc(o_taken, 1)

            def take_turned(filled):
                act.wait_ge(x_filled[0], filled)
                nc.scalar.copy(o_turned[:], bank_x[0][:]).then_inc(x_taken[0], 1)

            def before():
                for n, (w, c, bank, filled) in enumerate((("q", 0, 1, 1), ("q", 1, 0, 1), ("k", 0, 1, 2), ("k", 1, 0, 2))):
                    take_part(w, c, bank, filled, n)

            def step(i, s, first=False, last=False):
                c = s % 2
                for u in range(UNITS):
                    if u == 0 and not (first and s < 2):
                        bi, bs = (i, s - 2) if s >= 2 else (i - 1, s + 2)
                        take_o(bi, bs, 3)
                    if u and u - 1 in GROUP_AT and not (first and s == 0):
                        bi, bs = (i, s - 1) if s else (i - 1, 3)
                        if GROUP_AT[u - 1] == 0 and not first:
                            act.wait_ge(o_added, 4 * i + (1 if s == 2 else s - 2))
                        take_o(bi, bs, GROUP_AT[u - 1])
                    if (s, u - 1) in PROJECT_AT:
                        w, ch, k = PROJECT_AT[s, u - 1]
                        if k == 0:
                            for g in (0, 1):
                                act.wait_ge(head_in[g], HEAD_DMAS * (i + 1))
                                act.wait_ge(tail_in[g], TAIL_DMAS * (i + 1))
                        take_part(w, ch, 1, x1_base(i) + k + 1, 4 * (i + 1) + k)
                    n = 32 * i + 8 * s + u
                    act.wait_ge(s_filled, n + 1)
                    nc.scalar.activation(probs[:, c, u, :], bank_s[u % 2][:], ACT.Exp, scale=SCALE).then_inc(exp_done, 1)
                    if not first and s < 2 and u == OT_AT + 1:
                        take_turned(x0_base(i) + 2 * s + 1)

            def after():
                i = PAIRS_ALL
                take_o(i - 1, 2, 3)
                act.wait_ge(o_added, 4 * i - 2)
                for qt in range(4):
                    take_o(i - 1, 3, qt)
                take_turned(x0_base(i) + 1)
                take_turned(x0_base(i) + 3)

            over_steps(act, step, before, after)

        @block.vector
        def _(dve):
            def reduce(j, n):
                dve.wait_ge(m_filled, n + 1)
                nc.vector.tensor_reduce(maxes[:, j // 2, j % 2:j % 2 + 1], bank_m[j % 2][:], AX.X, ALU.max).then_inc(m_reduced, 1)

            def negate(h, c, j0, n, rows):
                dve.wait_ge(m_reduced, j0)
                if not (isinstance(rows, int) and rows < 4):
                    dve.wait_ge(row_in[2 * h + c], n)
                nc.vector.tensor_reduce(negmax[:, 2 * h + c, :], maxes[:, 4 * c:4 * c + 4, :], AX.X, ALU.max,
                                        negate=True).then_inc(c_ready, 1)

            def invert(i, s, qt):
                dve.wait_ge(pv_done, 16 * i + 4 * s + qt + 1)
                nc.vector.reciprocal(rden[:, qt:qt + 1], bank_o[qt % 2][:, DEN:DEN + 1]).then_inc(rden_ready, 1)

            def add_y(i, c, filled):
                dve.wait_ge(x_filled[0], filled)
                x_flat = X[:].rearrange("p t d -> p (t d)")
                at = ((i // PAIRS) * TB + 4 * c) * P
                xs = x_flat[:, bass.ds(at, CH)]
                nc.vector.tensor_tensor(xs, xs, bank_x[0][:], ALU.add).then_inc(x_taken[0], 1)

            def before():
                for h in range(2):
                    last = nc.vector.memset(kb[h][E:E + 1, :].bitcast(F32), 1.0)
                last.then_inc(ones_ready, 1)
                for j in range(MAX_N):
                    reduce(j, j)
                negate(0, 0, MAX_N // 2, 0, 0)
                negate(0, 1, MAX_N, 0, 0)

            def step(i, s, first=False, last=False):
                h, c = s // 2, s % 2
                for u in range(UNITS):
                    if m := max_at(i, s, u, first, last):
                        reduce(m[2], MAX_N * m[1] + m[2])
                    if u == MAX_LAG:
                        if c == 0 and not (first and s == 0):
                            negate(h, 1, MAX_N * (2 * i + h) + MAX_N, 16 * i, 0 if first or (isinstance(i, int) and i == 0) else 4)
                        if c == 1 and not (last and h == 1):
                            negate(1 - h, 0, MAX_N * (2 * i + h + 1) + MAX_N // 2, 16 * (i + h), 0 if first and h == 0 else 4)
                    if u in GROUP_AT and not (first and s == 0):
                        bi, bs = (i, s - 1) if s else (i - 1, 3)
                        invert(bi, bs, GROUP_AT[u])
                    if u not in POOL_UNITS[s]:
                        n = 32 * i + 8 * s + u
                        dve.wait_ge(exp_done, n + 1)
                        p = probs[:, c, u, :]
                        hi = p.bitcast(BF16).rearrange("p (q two) -> p q two", two=2)[:, :, 1]
                        nc.vector.tensor_tensor(probs_lo[:, c, u, :], p, hi, ALU.subtract).then_inc(lo_dve, 1)
                    if not first and s < 2 and u == Y_AT + 1:
                        add_y(i - 1, s, x0_base(i) + 2 * s + 2)

            def after():
                i = PAIRS_ALL
                for qt in range(4):
                    invert(i - 1, 3, qt)
                for c in range(2):
                    add_y(i - 1, c, x0_base(i) + 2 * c + 2)
                dve.wait_ge(x_taken[0], x0_base(i) + 4)

            over_steps(dve, step, before, after)

        @block.gpsimd
        def _(pool):
            def stage(i):
                pool.wait_ge(raw_in, 32 * i + 32)
                for w in "qk":
                    last = nc.gpsimd.tensor_tensor(w_hi[w][:], w_raw[w][:], zeros[:], ALU.add)
                last.then_inc(wstep, 1)
                pool.wait_ge(wstep, i + 1)
                for w in "qk":
                    last = nc.gpsimd.tensor_tensor(w_lo[w][:], w_raw[w][:], w_hi[w][:].bitcast(F32), ALU.subtract)
                last.then_inc(staged, 1)

            def make_lo(which, c, bank, taken):
                pool.wait_ge(x_taken[bank], taken)
                cs = slice(c * CH, (c + 1) * CH)
                nc.gpsimd.tensor_tensor(t_lo[which][:, cs], full[:, c, :], t_hi[which][:, cs].bitcast(F32),
                                        ALU.subtract).then_inc(lo_made, 1)

            def add_o(i, s):
                pool.wait_ge(o_taken, 16 * i + 4 * s + 4)
                h, c = s // 2, s % 2
                nc.gpsimd.tensor_tensor(o_pair[:, c, :, h * E:(h + 1) * E], o_parts[:, c, :, 0:E], o_parts[:, c, :, E + 1:P + 1],
                                        ALU.add).then_inc(o_added, 1)

            def before():
                nc.gpsimd.memset(zeros[:], 0.0).then_inc(zeros_ready, 1)
                pool.wait_ge(zeros_ready, 1)
                stage(0)
                for w, c, bank, taken in (("q", 0, 1, 1), ("q", 1, 0, 1), ("k", 0, 1, 2), ("k", 1, 0, 2)):
                    make_lo(w, c, bank, taken)
                stage(1)

            def step(i, s, first=False, last=False):
                c = s % 2
                for u in range(UNITS):
                    if u in POOL_UNITS[s]:
                        n = 32 * i + 8 * s + u
                        pool.wait_ge(exp_done, n + 1)
                        p = probs[:, c, u, :]
                        hi = p.bitcast(BF16).rearrange("p (q two) -> p q two", two=2)[:, :, 1]
                        nc.gpsimd.tensor_tensor(probs_lo[:, c, u, :], p, hi, ALU.subtract).then_inc(lo_pool, 1)
                    if u == 1 and not (first and s < 2):
                        bi, bs = (i, s - 2) if s >= 2 else (i - 1, s + 2)
                        add_o(bi, bs)
                    if (s, u - 1) in PROJECT_AT:
                        w, ch, k = PROJECT_AT[s, u - 1]
                        make_lo(w, ch, 1, x1_base(i) + k + 1)
                    if s == 1 and u == UNITS - 1:
                        pool.wait_ge(x_filled[1], x1_base(i) + 4)
                        stage(i + 2)

            def after():
                i = PAIRS_ALL
                add_o(i - 1, 2)
                add_o(i - 1, 3)

            over_steps(pool, step, before, after)


class Normaliser:

    def __init__(self, nc, ctx, name, eps):
        sb = lambda n, s: ctx.enter_context(nc.sbuf_tensor(f"{name}_{n}", s, F32))
        sem = lambda n: ctx.enter_context(nc.semaphore(f"{name}_{n}"))
        self.nc, self.eps = nc, eps
        self.stats, self.mv = sb("stats", [P, 4, 6]), sb("mean_var", [P, 4, 2])
        self.std, self.rstd = sb("std", [P, 4]), sb("rstd", [P, 4])
        self.eps_col = sb("eps", [P, 1])
        self.eps_set = sem("eps_set")
        self.summed, self.moments, self.rooted, self.inverted, self.done = (
            sem(n) for n in ("summed", "moments", "rooted", "inverted", "done"))

    def start(self, dve):
        self.nc.vector.memset(self.eps_col[:], self.eps).then_inc(self.eps_set, 1)

    def moments_of(self, dve, src, n):
        if n:
            dve.wait_ge(self.done, n)
        for j in range(4):
            last = self.nc.vector.bn_stats(self.stats[:, j, :], src[:, j, :])
        last.then_inc(self.summed, 1)
        dve.wait_ge(self.summed, n + 1)
        for j in range(4):
            last = self.nc.vector.bn_aggr(self.mv[:, j, :], self.stats[:, j, :])
        last.then_inc(self.moments, 1)

    def root(self, act, n):
        if n == 0:
            act.wait_ge(self.eps_set, 1)
        act.wait_ge(self.moments, n + 1)
        self.nc.scalar.activation(self.std[:], self.mv[:, :, 1], ACT.Sqrt, bias=self.eps_col[:]).then_inc(self.rooted, 1)

    def apply(self, dve, src, dst, n):
        dve.wait_ge(self.rooted, n + 1)
        self.nc.vector.reciprocal(self.rstd[:], self.std[:]).then_inc(self.inverted, 1)
        dve.wait_ge(self.inverted, n + 1)
        for j in range(4):
            last = self.nc.vector.tensor_scalar(dst[:, j, :], src[:, j, :], self.mv[:, j, 0:1], self.rstd[:, j:j + 1],
                                                ALU.subtract, ALU.mult)
        last.then_inc(self.done, 1)


def quantised_ffn(nc, a, persist):
    X, ident = persist["X"], persist["ident"]
    T = X.shape[1]
    CHUNKS = T // 4
    F = a["L0_ffn_fc1_q"].shape[1]
    NF = F // P
    with ExitStack() as ctx:
        sb = lambda n, s, d=F32: ctx.enter_context(nc.sbuf_tensor(n, s, d))
        ps = lambda n: ctx.enter_context(nc.psum_tensor(n, [P, CH], F32))
        sem = lambda n: ctx.enter_context(nc.semaphore(n))
        q1, q2 = sb("q1", [P, F], I32), sb("q2", [P, NF, P], I32)
        s1, s2 = sb("s1_rows", [P, F]), sb("s2_rows", [P, NF, P])
        w1, w2 = sb("w1", [P, F]), sb("w2", [P, NF, P])
        b1_rows, b2_row = sb("b1_rows", [NF, P]), sb("b2_row", [P, P])
        b1 = sb("b1", [P, NF])
        affine_rows, affine = sb("affine_rows", [2, P]), sb("affine", [P, 2])
        half_b2 = sb("half_b2", [P, P])
        h = sb("h", [P, 2, 4, P])
        h_turned = sb("h_turned", [P, 2, CH])
        y = sb("y", [P, NF, CH])
        bank_t = [ps(f"bank_t{i}") for i in range(2)]
        bank_f = [ps(f"bank_f{i}") for i in range(2)]
        bank_z = [ps(f"bank_z{i}") for i in range(2)]
        bank_b = ps("bank_b")
        first_ln, inner_ln, last_ln = (Normaliser(nc, ctx, n, 1e-5) for n in ("ln_in", "ln_ffn", "ln_out"))
        q_in, row_in = sem("ffn_q_in"), sem("ffn_rows_in")
        w1_ready, w2_ready, b2_ready, b2_added = sem("w1_ready"), sem("w2_ready"), sem("half_b2_ready"), sem("half_b2_added")
        cols_turned, cols_ready = sem("columns_turned"), sem("columns_ready")
        turned, turned_taken, f_filled, f_taken = sem("h_turned_filled"), sem("h_turned_taken"), sem("fc1_filled"), sem("silu_done")
        z_filled, z_added = sem("fc2_filled"), sem("fc2_added")
        block = ctx.enter_context(nc.Block())
        chunk = lambda t, c: t[:, 4 * c:4 * c + 4, :]

        @block.sync
        def _(sp):
            row = lambda ap: ap.rearrange("(o n) -> o n", o=1)
            sp.dma_start(b1_rows[:], a["L0_ffn_fc1_bias"].rearrange("(f p) -> f p", p=P)).then_inc(row_in, 16)
            sp.dma_start(affine_rows[0:1, :], row(a["L0_ffn_ln_gamma"])).then_inc(row_in, 16)
            sp.dma_start(affine_rows[1:2, :], row(a["L0_ffn_ln_beta"])).then_inc(row_in, 16)
            sp.dma_start(q1[:], a["L0_ffn_fc1_q"]).then_inc(q_in, 16)
            sp.dma_start(s1[:], a["L0_ffn_fc1_scales"].broadcast_to((P, F))).then_inc(q_in, 16)
            sp.dma_start(q2[:], a["L0_ffn_fc2_q"].rearrange("(f p) n -> p f n", p=P)).then_inc(q_in, 16)
            sp.dma_start(s2[:], a["L0_ffn_fc2_scales"].rearrange("(o f) n -> o f n", o=1).broadcast_to((P, NF, P))).then_inc(q_in, 16)
            sp.dma_start(b2_row[:], row(a["L0_ffn_fc2_bias"]).broadcast_to((P, P))).then_inc(q_in, 16)

        @block.tensor
        def _(pe):
            pe.wait_ge(row_in, 48)
            nc.tensor.transpose(bank_b[:, 0:NF], b1_rows[:], ident[0:NF, 0:NF])
            nc.tensor.transpose(bank_b[:, NF:NF + 2], affine_rows[:], ident[0:2, 0:2]).then_inc(cols_turned, 1)

            def turn(c):
                pe.wait_ge(inner_ln.done, c + 1)
                if c >= 2:
                    pe.wait_ge(turned_taken, c - 1)
                for j in range(4):
                    last = nc.tensor.transpose(bank_t[c % 2][:, j * P:(j + 1) * P], h[:, c % 2, j, :], ident[:])
                last.then_inc(turned, 1)

            turn(0)
            pe.wait_ge(w1_ready, 1)
            for c in range(CHUNKS):
                pe.wait_ge(turned_taken, c + 1)
                for f in range(NF):
                    n = NF * c + f
                    if n >= 2:
                        pe.wait_ge(f_taken, n - 1)
                    nc.tensor.matmul(bank_f[n % 2][:], w1[:, f * P:(f + 1) * P], h_turned[:, c % 2, :],
                                     start=True, stop=True).then_inc(f_filled, 1)
                if c + 1 < CHUNKS:
                    turn(c + 1)
                if c == 0:
                    pe.wait_ge(w2_ready, 1)
                if c >= 2:
                    pe.wait_ge(z_added, c - 1)
                pe.wait_ge(f_taken, NF * (c + 1))
                for j in range(4):
                    for f in range(NF):
                        last = nc.tensor.matmul(bank_z[c % 2][:, j * P:(j + 1) * P], y[:, f, j * P:(j + 1) * P],
                                                w2[:, f, :], start=(f == 0), stop=(f == NF - 1))
                last.then_inc(z_filled, 1)

        @block.scalar
        def _(act):
            act.wait_ge(cols_turned, 1)
            nc.scalar.copy(b1[:], bank_b[:, 0:NF])
            nc.scalar.copy(affine[:], bank_b[:, NF:NF + 2]).then_inc(cols_ready, 1)
            act.wait_ge(cols_ready, 1)

            def silu(c):
                act.wait_ge(turned, c + 1)
                nc.scalar.activation(h_turned[:, c % 2, :], bank_t[c % 2][:], ACT.Identity, bias=affine[:, 1:2],
                                     scale=affine[:, 0:1]).then_inc(turned_taken, 1)
                for f in range(NF):
                    n = NF * c + f
                    act.wait_ge(f_filled, n + 1)
                    if c and f == 0:
                        act.wait_ge(z_filled, c)
                    nc.scalar.activation(y[:, f, :], bank_f[n % 2][:], ACT.Silu, bias=b1[:, f:f + 1]).then_inc(f_taken, 1)

            act.wait_ge(q_in, 80)
            nc.scalar.mul(half_b2[:], b2_row[:], 0.5).then_inc(b2_ready, 1)
            for c in range(CHUNKS):
                first_ln.root(act, c)
                inner_ln.root(act, c)
            for c in range(CHUNKS):
                silu(c)
            for c in range(CHUNKS):
                last_ln.root(act, c)

        @block.vector
        def _(dve):
            for ln in (first_ln, inner_ln, last_ln):
                ln.start(dve)
            for c in range(CHUNKS):
                x = chunk(X, c)
                first_ln.moments_of(dve, x, c)
                first_ln.apply(dve, x, x, c)
                dve.wait_ge(first_ln.done, c + 1)
                inner_ln.moments_of(dve, x, c)
                if c >= 2:
                    dve.wait_ge(turned, c - 1)
                inner_ln.apply(dve, x, h[:, c % 2], c)
                if c == 0:
                    dve.wait_ge(q_in, 80)
                    nc.vector.scalar_tensor_tensor(out=w1[:], in0=q1[:], scalar=-128.0, in1=s1[:], op0=ALU.add,
                                                   op1=ALU.mult).then_inc(w1_ready, 1)
                    nc.vector.scalar_tensor_tensor(out=w2[:], in0=q2[:], scalar=-128.0, in1=s2[:], op0=ALU.add,
                                                   op1=ALU.mult).then_inc(w2_ready, 1)
                    dve.wait_ge(b2_ready, 1)
                dve.wait_ge(inner_ln.done, c + 1)
                nc.vector.scalar_tensor_tensor(out=x, in0=x, scalar=2.0, in1=half_b2[:].unsqueeze(1).broadcast_to((P, 4, P)),
                                               op0=ALU.mult, op1=ALU.add).then_inc(b2_added, 1)
            for c in range(CHUNKS):
                x = chunk(X, c)
                dve.wait_ge(z_filled, c + 1)
                dve.wait_ge(b2_added, c + 1)
                nc.vector.scalar_tensor_tensor(out=x, in0=bank_z[c % 2][:].rearrange("p (t d) -> p t d", d=P), scalar=0.5,
                                               in1=x, op0=ALU.mult, op1=ALU.add).then_inc(z_added, 1)
            for c in range(CHUNKS):
                x = chunk(X, c)
                dve.wait_ge(z_added, c + 1)
                last_ln.moments_of(dve, x, c)
                last_ln.apply(dve, x, x, c)
            dve.wait_ge(last_ln.done, CHUNKS)


def attend_once(nc, a, persist):
    X, ident, B = persist["X"], persist["ident"], persist["B"]
    T = X.shape[1]
    TB = T // B
    N = TB * P
    S = B * N
    HALVES = N // CH
    INV_SCALE = float(P / 16) ** -0.5
    VW = 2 * P + 2
    STEPS = B * HALVES
    with ExitStack() as ctx:
        sb = lambda n, s, d=F32: ctx.enter_context(nc.sbuf_tensor(n, s, d))
        ps = lambda n: ctx.enter_context(nc.psum_tensor(n, [P, CH], F32))
        sem = lambda n: ctx.enter_context(nc.semaphore(n))
        w_rows, w_t = sb("w_rows", [P, 4, P]), sb("w_turned", [P, 4, P])
        xt = sb("xt", [P, S])
        hi = {w: sb(f"{w}1_hi", [P, S], F32R) for w in "qk"}
        lo = {w: sb(f"{w}1_lo", [P, S], F32R) for w in "qk"}
        V = sb("v1_parts", [P, T, VW], F16)
        ones, row = sb("ones_row", [1, P], F32R), sb("negmax_row", [1, S], F32R)
        maxes, negmax = sb("maxes1", [P, T, HALVES]), sb("negmax1", [P, T], F32R)
        probs = sb("probs1", [P, 2, TB, CH])
        probs_lo = sb("probs1_lo", [P, 2, TB, CH], F16)
        rden = sb("rden1", [P, 4])
        o_hi = sb("o_hi", [P, 2, P])
        o_new = sb("o_new", [P, S])
        bank_a = [ps(f"bank_a{i}") for i in range(4)]
        bank_m = [ps(f"bank_n{i}") for i in range(2)]
        bank_o = [ps(f"bank_p{i}") for i in range(2)]
        ln = Normaliser(nc, ctx, "ln_attn", 1e-5)
        w_in, w_turned, w_ready = sem("w1_in"), sem("w1_turned"), sem("w1t_ready")
        a_filled, xt_ready = sem("bank_a_filled"), sem("xt_ready")
        parted, parts_taken = sem("parts_hi_ready"), sem("parts_lo_ready")
        ones_ready = sem("ones1_ready")
        m_filled, m_reduced, c_ready, row_in = sem("max1_scores"), sem("max1_reduced"), sem("negmax1_ready"), sem("negmax1_in")
        exp_done, lo_done, pv_done = sem("exp1_done"), sem("probs1_lo_done"), sem("pv1_done")
        rden_ready, o_scaled, o_taken = sem("rden1_ready"), sem("o1_scaled"), sem("o1_taken")
        y_filled, y_added = sem("y1_filled"), sem("y1_added")
        block = ctx.enter_context(nc.Block())
        CK = S // CH
        X0, Q0, K0, V0, S0 = 0, CK, 2 * CK, 3 * CK, 4 * CK
        Y0 = S0 + STEPS * TB
        queries = lambda t, c: t[:, c * CH:(c + 1) * CH].rearrange("d (p t) -> d t p", t=4)

        @block.sync
        def _(sp):
            for n, w in enumerate(("wq", "wk", "wv", "wo")):
                sp.dma_start(w_rows[:, n, :], a["L1_attn_" + w]).then_inc(w_in, 16)
            for c in range(CK):
                sp.wait_ge(c_ready, c + 1)
                sp.dma_start(row[:, c * CH:(c + 1) * CH].bitcast(F32).rearrange("o (p t) -> o p t", t=4),
                             negmax[:, 4 * c:4 * c + 4].bitcast(F32)).then_inc(row_in, 16)
            sp.wait_ge(row_in, 16 * CK)

        @block.tensor
        def _(pe):
            def bank(n):
                m = n - 4
                if m >= S0:
                    pe.wait_ge(exp_done, m - S0 + 1)
                elif m >= Q0:
                    pe.wait_ge(parts_taken, m - Q0 + 1)
                elif m >= X0:
                    pe.wait_ge(xt_ready, m - X0 + 1)
                return bank_a[n % 4]

            pe.wait_ge(w_in, 64)
            for n in range(4):
                last = nc.tensor.transpose(bank_m[0][:, n * P:(n + 1) * P], w_rows[:, n, :], ident[:])
            last.then_inc(w_turned, 1)
            for c in range(CK):
                b = bank(X0 + c)
                for j in range(4):
                    last = nc.tensor.transpose(b[:, j * P:(j + 1) * P], X[:, 4 * c + j, :], ident[:])
                last.then_inc(a_filled, 1)
            pe.wait_ge(w_ready, 1)
            for w in range(2):
                for c in range(CK):
                    b = bank(Q0 + CK * w + c)
                    pe.wait_ge(xt_ready, c + 1)
                    nc.tensor.matmul(b[:], w_t[:, w, :], xt[:, c * CH:(c + 1) * CH], start=True, stop=True).then_inc(a_filled, 1)
            for c in range(CK):
                b = bank(V0 + c)
                for j in range(4):
                    t = 4 * c + j
                    last = nc.tensor.matmul(b[:, j * P:(j + 1) * P], xt[:, t * P:(t + 1) * P], w_t[:, 2, :], start=True, stop=True)
                last.then_inc(a_filled, 1)

            pe.wait_ge(parts_taken, 2 * CK)
            for n in range(T * HALVES):
                t, half = n // HALVES, n % HALVES
                b, c = t // TB, t // 4
                if n >= 2:
                    pe.wait_ge(m_reduced, n - 1)
                ks = slice(b * N + half * CH, b * N + (half + 1) * CH)
                nc.tensor.matmul(bank_m[n % 2][:], queries(hi["q"], c)[:, t % 4, :], hi["k"][:, ks],
                                 start=True, stop=True).then_inc(m_filled, 1)

            def scores(step, kt):
                b = step // HALVES
                bk = bank(S0 + TB * step + kt)
                if kt == 0:
                    pe.wait_ge(row_in, 16 * CK)
                ks, qs = slice(b * N + kt * P, b * N + (kt + 1) * P), slice(step * CH, (step + 1) * CH)
                nc.tensor.matmul(bk[:], ones[:], row[:, qs], start=True, stop=False)
                nc.tensor.matmul(bk[:], lo["k"][:, ks], hi["q"][:, qs], start=False, stop=False)
                nc.tensor.matmul(bk[:], hi["k"][:, ks], lo["q"][:, qs], start=False, stop=False)
                nc.tensor.matmul(bk[:], hi["k"][:, ks], hi["q"][:, qs], start=False, stop=True).then_inc(a_filled, 1)

            def times_v(step, qt):
                b = step // HALVES
                if qt == 0:
                    pe.wait_ge(lo_done, TB * (step + 1))
                n = 4 * step + qt
                if n >= 2:
                    pe.wait_ge(o_taken, n - 1)
                hi_of = probs[:, step % 2].bitcast(BF16).rearrange("p k (q two) -> p k q two", two=2)
                acc, qs = bank_o[n % 2], slice(qt * P, (qt + 1) * P)
                for kt in range(TB):
                    low = lambda: nc.tensor.matmul(acc[:, 0:P + 1], probs_lo[:, step % 2, kt, qs], V[:, b * TB + kt, 0:P + 1],
                                                   start=False, stop=False, skip_group_check=True)
                    if kt == TB - 1:
                        low()
                    last = nc.tensor.matmul(acc[:, 0:2 * P + 1], hi_of[:, kt, qs, 1], V[:, b * TB + kt, 0:2 * P + 1],
                                            start=(kt == 0), stop=(kt == TB - 1))
                    if kt < TB - 1:
                        low()
                last.then_inc(pv_done, 1)

            for step in range(STEPS + 1):
                for kt in range(TB):
                    if step < STEPS:
                        scores(step, kt)
                    if step and kt % 2:
                        times_v(step - 1, kt // 2)
            for c in range(CK):
                b = bank(Y0 + c)
                pe.wait_ge(o_taken, 4 * HALVES * (c // HALVES + 1))
                for j in range(4):
                    t = 4 * c + j
                    last = nc.tensor.matmul(b[:, j * P:(j + 1) * P], o_new[:, t * P:(t + 1) * P], w_t[:, 3, :], start=True, stop=True)
                last.then_inc(y_filled, 1)

        @block.scalar
        def _(act):
            act.wait_ge(w_turned, 1)
            nc.scalar.copy(w_t[:].rearrange("p n e -> p (n e)"), bank_m[0][:]).then_inc(w_ready, 1)
            for c in range(CK):
                act.wait_ge(a_filled, X0 + c + 1)
                nc.scalar.copy(xt[:, c * CH:(c + 1) * CH], bank_a[(X0 + c) % 4][:]).then_inc(xt_ready, 1)
            for n in range(2 * CK):
                w, c = "qk"[n // CK], n % CK
                act.wait_ge(a_filled, Q0 + n + 1)
                nc.scalar.copy(hi[w][:, c * CH:(c + 1) * CH], bank_a[(Q0 + n) % 4][:]).then_inc(parted, 1)
            for c in range(CK):
                act.wait_ge(a_filled, V0 + c + 1)
                nc.scalar.copy(V[:, 4 * c:4 * c + 4, 0:P], bank_a[(V0 + c) % 4][:].rearrange("p (t d) -> p t d", d=P)).then_inc(parted, 1)
            for step in range(STEPS + 1):
                for kt in range(TB):
                    if step < STEPS:
                        n = TB * step + kt
                        act.wait_ge(a_filled, S0 + n + 1)
                        nc.scalar.activation(probs[:, step % 2, kt, :], bank_a[(S0 + n) % 4][:], ACT.Exp,
                                             scale=INV_SCALE).then_inc(exp_done, 1)
                    if step and kt % 2:
                        g = 4 * (step - 1) + kt // 2
                        act.wait_ge(rden_ready, g + 1)
                        nc.scalar.activation(o_hi[:, g % 2, :], bank_o[g % 2][:, 0:P], ACT.Copy,
                                             scale=rden[:, g % 4:g % 4 + 1]).then_inc(o_scaled, 1)
            for c in range(CK):
                ln.root(act, c)

        @block.vector
        def _(dve):
            ln.start(dve)
            nc.vector.memset(ones[:].bitcast(F32), 1.0)
            nc.vector.memset(V[:, :, P:P + 1], 1.0).then_inc(ones_ready, 1)
            dve.wait_ge(ones_ready, 1)
            for n in range(2 * CK):
                w, c = "qk"[n // CK], n % CK
                cs = slice(c * CH, (c + 1) * CH)
                dve.wait_ge(parted, n + 1)
                nc.vector.tensor_tensor(lo[w][:, cs], bank_a[(Q0 + n) % 4][:], hi[w][:, cs].bitcast(F32),
                                        ALU.subtract).then_inc(parts_taken, 1)
            for c in range(CK):
                dve.wait_ge(parted, 2 * CK + c + 1)
                nc.vector.tensor_tensor(V[:, 4 * c:4 * c + 4, P + 1:2 * P + 1], bank_a[(V0 + c) % 4][:].rearrange("p (t d) -> p t d", d=P),
                                        V[:, 4 * c:4 * c + 4, 0:P], ALU.subtract).then_inc(parts_taken, 1)
            for n in range(T * HALVES):
                t, half = n // HALVES, n % HALVES
                dve.wait_ge(m_filled, n + 1)
                nc.vector.tensor_reduce(maxes[:, t, half:half + 1], bank_m[n % 2][:], AX.X, ALU.max).then_inc(m_reduced, 1)
                if n % (4 * HALVES) == 4 * HALVES - 1:
                    c = t // 4
                    dve.wait_ge(m_reduced, n + 1)
                    nc.vector.tensor_reduce(negmax[:, 4 * c:4 * c + 4], maxes[:, 4 * c:4 * c + 4, :], AX.X, ALU.max,
                                            negate=True).then_inc(c_ready, 1)
            for step in range(STEPS + 1):
                for kt in range(TB):
                    if step < STEPS:
                        n = TB * step + kt
                        dve.wait_ge(exp_done, n + 1)
                        p = probs[:, step % 2, kt, :]
                        nc.vector.tensor_tensor(probs_lo[:, step % 2, kt, :], p,
                                                p.bitcast(BF16).rearrange("p (q two) -> p q two", two=2)[:, :, 1],
                                                ALU.subtract).then_inc(lo_done, 1)
                    if step and kt % 2:
                        g = 4 * (step - 1) + kt // 2
                        dve.wait_ge(pv_done, g + 1)
                        nc.vector.reciprocal(rden[:, g % 4:g % 4 + 1], bank_o[g % 2][:, P:P + 1]).then_inc(rden_ready, 1)
                        dve.wait_ge(o_scaled, g + 1)
                        dst = o_new[:].rearrange("p (b d r) -> p b r d", b=B, r=TB)[:, g // TB, g % TB, :]
                        nc.vector.scalar_tensor_tensor(out=dst, in0=bank_o[g % 2][:, P + 1:2 * P + 1], scalar=rden[:, g % 4:g % 4 + 1],
                                                       in1=o_hi[:, g % 2, :], op0=ALU.mult, op1=ALU.add).then_inc(o_taken, 1)
            for c in range(CK):
                x = X[:, 4 * c:4 * c + 4, :]
                dve.wait_ge(y_filled, c + 1)
                nc.vector.tensor_tensor(x, x, bank_a[(Y0 + c) % 4][:].rearrange("p (t d) -> p t d", d=P), ALU.add).then_inc(y_added, 1)
                dve.wait_ge(y_added, c + 1)
                ln.moments_of(dve, x, c)
                ln.apply(dve, x, x, c)
            dve.wait_ge(ln.done, CK)


def mix_experts(nc, a, persist, out):
    X, ident, B = persist["X"], persist["ident"], persist["B"]
    T = X.shape[1]
    CK = T // 4
    S = T * P
    NE, _, F = a["L1_ffn_ew1"].shape
    NF = F // P
    FFNS = NE + 1
    with ExitStack() as ctx:
        sb = lambda n, s, d=F32: ctx.enter_context(nc.sbuf_tensor(n, s, d))
        ps = lambda n: ctx.enter_context(nc.psum_tensor(n, [P, CH], F32))
        sem = lambda n: ctx.enter_context(nc.semaphore(n))
        w_raw = [sb("e1_raw", [P, F]), sb("e2_raw", [P, F])]
        w_hi = [[sb(f"e{w + 1}_hi{i}", [P, F], F32R) for w in range(2)] for i in range(2)]
        w_lo = [[sb(f"e{w + 1}_lo{i}", [P, F], F32R) for w in range(2)] for i in range(2)]
        b1_rows, b1 = sb("e1_bias_rows", [FFNS * NF, P]), sb("e1_bias", [P, FFNS * NF])
        b1_now = sb("e1_bias_now", [P, 2, NF])
        b2, shared_b2 = sb("e2_bias", [NE, P]), sb("shared_b2_rows", [P, P])
        nw_row, nw = sb("norm_w_row", [1, P]), sb("norm_w", [P, 1])
        r_rows, r_t = sb("router_rows", [NE, P]), sb("router_t", [P, NE])
        sums = sb("square_sums", [P, T])
        root, rroot, tiny = sb("rms", [P, T]), sb("rms_inv", [P, T]), sb("rms_eps", [P, 1])
        n_tok = sb("n_tokens", [P, T, P])
        nt, nt_hi, nt_lo = sb("nt", [P, S]), sb("nt_hi", [P, S], F32R), sb("nt_lo", [P, S], F32R)
        prob = sb("gates", [P, T, NE])
        top, top_at = sb("top8", [P, T, NE]), sb("top8_at", [P, T, NE], U32)
        at = sb("top2_at", [P, T, 2])
        lane_i, lane = sb("lane_i", [P, NE], I32), sb("lane", [P, NE])
        first, second = sb("is_first", [P, T, NE]), sb("is_second", [P, T, NE])
        total, share = sb("top2_sum", [P, T]), sb("top2_inv", [P, T])
        comb_e = sb("comb_by_token", [P, T, NE])
        comb_t = sb("comb_t", [NE, S])
        gates = [sb(f"gates_on_all{i}", [P, S]) for i in range(2)]
        gate_rows = nc.dram_tensor("gate_rows", [NE, S], F32).ap()
        r = sb("rectified", [P, 2, CH])
        h = sb("hidden", [P, NF, CH])
        h_hi, h_lo = sb("hidden_hi", [P, NF, CH], F32R), sb("hidden_lo", [P, NF, CH], F32R)
        y_t = sb("y_by_width", [P, 2, CH])
        y = sb("y_out", [P, T, P])
        bank_h = [ps(f"bank_h{i}") for i in range(2)]
        bank_y = [ps(f"bank_y{i}") for i in range(CK)]
        bank_c = [ps(f"bank_c{i}") for i in range(2)]
        ln = Normaliser(nc, ctx, "ln_moe", 1e-5)
        small_in = sem("moe_small_in")
        w_in, w_hi_ready, w_lo_ready = sem("expert_in"), sem("expert_hi"), sem("expert_lo")
        small_turned, small_ready = sem("moe_small_turned"), sem("moe_small_ready")
        eps_ready, squared, rooted, inverted, scaled = (sem("moe_" + n) for n in ("eps", "squared", "rooted", "inverted", "scaled"))
        turned, nt_ready, hi_ready, lo_ready = sem("n_turned"), sem("nt_ready"), sem("nt_hi_ready"), sem("nt_lo_ready")
        routed, gated, picked, pick, comb_ready = sem("router_scores"), sem("gates_ready"), sem("top_found"), sem("pick_step"), sem("comb_ready")
        lane_ready = sem("lane_ready")
        comb_turned, comb_t_ready, rows_stored = sem("comb_turned"), sem("comb_t_ready"), sem("gate_rows_stored")
        gates_in = [sem(f"gates_on_all{i}_in") for i in range(2)]
        h_filled, rectified, h_gated, h_hi_ready = sem("h_filled"), sem("rectified"), sem("h_gated"), sem("h_hi_ready")
        lo_pool, lo_dve = sem("h_lo_by_gpsimd"), sem("h_lo_by_vector")
        h_used = sem("h_used")
        y_copied, y_turned, y_added = sem("y_copied"), sem("y_turned"), sem("y_added_moe")
        b1_ready = sem("e1_bias_ready")
        stored = sem("stored")
        block = ctx.enter_context(nc.Block())
        row = lambda ap: ap.rearrange("(o n) -> o n", o=1)
        TILES = NF * CK
        LO_POOL = NF - 1

        def over_ffns(eng, ffn):
            ffn(0, 0)
            with eng.Fori(0, NE // 2 - 1) as m:
                ffn(2 * m + 1, 1, m)
                ffn(2 * m + 2, 0, m)
            ffn(NE - 1, 1, NE // 2 - 1)
            ffn(NE, 0, NE // 2 - 1)

        @block.sync
        def _(sp):
            def load(e):
                sp.dma_start(w_raw[0][:], a["L1_ffn_ew1"][bass.ds(e, 1), :, :].rearrange("o d f -> d (o f)")).then_inc(w_in, 16)
                sp.dma_start(w_raw[1][:].rearrange("p (f q) -> p f q", q=P),
                             a["L1_ffn_ew2"][bass.ds(e, 1), :, :].rearrange("o (f p) q -> p (o f) q", p=P)).then_inc(w_in, 16)

            def load_gates(e, i):
                sp.dma_start(gates[i][:], gate_rows[bass.ds(e, 1), :].broadcast_to((P, S))).then_inc(gates_in[i], 16)

            sp.dma_start(nw_row[:], row(a["L1_ffn_norm_weight"])).then_inc(small_in, 16)
            sp.dma_start(r_rows[:], a["L1_ffn_router_w"]).then_inc(small_in, 16)
            sp.dma_start(b1_rows[0:NF, :], a["L1_ffn_sb1"].rearrange("(f p) -> f p", p=P)).then_inc(small_in, 16)
            sp.dma_start(b1_rows[NF:, :], a["L1_ffn_eb1"].rearrange("e (f p) -> (e f) p", p=P)).then_inc(small_in, 16)
            sp.dma_start(b2[:], a["L1_ffn_eb2"]).then_inc(small_in, 16)
            sp.dma_start(shared_b2[:], row(a["L1_ffn_sb2"]).broadcast_to((P, P))).then_inc(small_in, 16)
            sp.dma_start(w_raw[0][:], a["L1_ffn_sw1"]).then_inc(w_in, 16)
            sp.dma_start(w_raw[1][:].rearrange("p (f q) -> p f q", q=P), a["L1_ffn_sw2"].rearrange("(f p) o -> p f o", p=P)).then_inc(w_in, 16)
            sp.wait_ge(w_lo_ready, 1)
            load(0)
            sp.wait_ge(comb_t_ready, CK)
            sp.dma_start(gate_rows, comb_t[:]).then_inc(rows_stored, 16)
            sp.wait_ge(rows_stored, 16)
            load_gates(0, 1)
            load_gates(1, 0)
            sp.wait_ge(w_lo_ready, 2)
            load(1)
            with sp.Fori(1, NE // 2) as m:
                for d in range(2):
                    sp.wait_ge(h_gated, TILES * (2 * m + d - 1))
                    load_gates(2 * m + d, 1 - d)
                    sp.wait_ge(w_lo_ready, 2 * m + d + 1)
                    load(2 * m + d)
            o = out.rearrange("b (t p) d -> p (b t) d", p=P)
            for c in range(CK):
                sp.wait_ge(ln.done, c + 1)
                sp.dma_start(o[:, 4 * c:4 * c + 4, :], y[:, 4 * c:4 * c + 4, :]).then_inc(stored, 16)
            sp.wait_ge(stored, 16 * CK)

        @block.gpsimd
        def _(pool):
            nc.gpsimd.iota(lane_i[:], [[1, NE]], base=0, channel_multiplier=0).then_inc(lane_ready, 1)

            def ffn(n, half, m=None):
                for c in range(CK):
                    for f in range(NF if isinstance(n, int) and n == 0 and c < CK - 1 else LO_POOL):
                        pool.wait_ge(h_hi_ready, TILES * n + NF * c + f + 1)
                        nc.gpsimd.tensor_tensor(h_lo[:, f, :], h[:, f, :], h_hi[:, f, :].bitcast(F32), ALU.subtract).then_inc(lo_pool, 1)

            over_ffns(pool, ffn)

        @block.tensor
        def _(pe):
            pe.wait_ge(small_in, 96)
            nc.tensor.transpose(bank_c[0][:, 0:FFNS * NF], b1_rows[:], ident[0:FFNS * NF, 0:FFNS * NF])
            nc.tensor.transpose(bank_c[0][:, P:P + NE], r_rows[:], ident[0:NE, 0:NE])
            nc.tensor.transpose(bank_c[0][:, 2 * P:2 * P + 1], nw_row[:], ident[0:1, 0:1]).then_inc(small_turned, 1)
            for c in range(CK):
                pe.wait_ge(scaled, c + 1)
                for j in range(4):
                    last = nc.tensor.transpose(bank_y[c][:, j * P:(j + 1) * P], n_tok[:, 4 * c + j, :], ident[:])
                last.then_inc(turned, 1)
            pe.wait_ge(nt_ready, CK)
            for t in range(T):
                last = nc.tensor.matmul(bank_c[1][:, t * NE:(t + 1) * NE], nt[:, t * P:(t + 1) * P], r_t[:], start=True, stop=True)
            last.then_inc(routed, 1)

            def first_product(n, half, c, f):
                k = TILES * n + NF * c + f
                if c == 0 and f == 0:
                    pe.wait_ge(w_lo_ready, n + 1)
                if isinstance(n, int) and n == 0 and f == 0:
                    pe.wait_ge(lo_ready, c + 1)
                if not (isinstance(n, int) and k < 2):
                    pe.wait_ge(rectified, k - 1)
                fs, xs = slice(f * P, (f + 1) * P), slice(c * CH, (c + 1) * CH)
                out = bank_h[f % 2][:]
                nc.tensor.matmul(out, w_lo[half][0][:, fs], nt_hi[:, xs], start=True, stop=False)
                nc.tensor.matmul(out, w_hi[half][0][:, fs], nt_lo[:, xs], start=False, stop=False)
                nc.tensor.matmul(out, w_hi[half][0][:, fs], nt_hi[:, xs], start=False, stop=True).then_inc(h_filled, 1)

            def add_biases(c, start):
                nc.tensor.matmul(bank_y[c][:], b2[:], comb_t[:, c * CH:(c + 1) * CH], start=start, stop=False)

            def second_product(n, half, c, f):
                first_ffn, last_ffn = (isinstance(n, int) and n == v for v in (0, NE))
                if last_ffn and f == 0 and c < CK - 1:
                    add_biases(c, False)
                if first_ffn:
                    pe.wait_ge(lo_pool, NF * c + f + 1)
                elif f < LO_POOL:
                    pe.wait_ge(lo_pool, LO_POOL * CK * (n - 1) + TILES - 1 + LO_POOL * c + f + 1)
                else:
                    pe.wait_ge(lo_dve, CK * (n - 1) + c + 2)
                fs = slice(f * P, (f + 1) * P)
                out = bank_y[c][:]
                nc.tensor.matmul(out, w_lo[half][1][:, fs], h_hi[:, f, :], start=first_ffn and f == 0, stop=False)
                nc.tensor.matmul(out, w_hi[half][1][:, fs], h_lo[:, f, :], start=False, stop=False)
                nc.tensor.matmul(out, w_hi[half][1][:, fs], h_hi[:, f, :], start=False,
                                 stop=last_ffn and f == NF - 1).then_inc(h_used, 1)

            def turn_gates():
                pe.wait_ge(comb_ready, 1)
                for c in range(CK):
                    if c >= 2:
                        pe.wait_ge(comb_t_ready, c - 1)
                    for j in range(4):
                        last = nc.tensor.transpose(bank_c[c % 2][0:NE, j * P:(j + 1) * P], comb_e[:, 4 * c + j, :], ident[:])
                    last.then_inc(comb_turned, 1)

            def turn_output(c):
                pe.wait_ge(y_copied, c + 1)
                pe.wait_ge(comb_t_ready, CK) if c < 2 else pe.wait_ge(y_added, c - 1)
                for j in range(4):
                    last = nc.tensor.transpose(bank_c[c % 2][:, j * P:(j + 1) * P], y_t[:, c % 2, j * P:(j + 1) * P], ident[:])
                last.then_inc(y_turned, 1)

            def ffn(n, half, m=None):
                first_ffn, last_ffn = (isinstance(n, int) and n == v for v in (0, NE))
                for c in range(CK):
                    for f in range(NF):
                        first_product(n, half, c, f)
                        if c:
                            second_product(n, half, c - 1, f)
                        elif not first_ffn:
                            second_product(n - 1, 1 - half, CK - 1, f)
                        if last_ffn and c >= 2 and f == 1:
                            turn_output(c - 2)
                    if first_ffn and c == 2:
                        turn_gates()
                if first_ffn:
                    pe.wait_ge(comb_t_ready, CK)
                    add_biases(CK - 1, True)

            over_ffns(pe, ffn)
            for f in range(NF):
                second_product(NE, 0, CK - 1, f)
            for c in range(CK - 2, CK):
                turn_output(c)

        @block.scalar
        def _(act):
            act.wait_ge(squared, T)
            act.wait_ge(eps_ready, 1)
            nc.scalar.activation(root[:], sums[:], ACT.Sqrt, bias=tiny[:], scale=1.0 / P).then_inc(rooted, 1)
            act.wait_ge(small_turned, 1)
            nc.scalar.copy(b1[:], bank_c[0][:, 0:FFNS * NF])
            nc.scalar.copy(r_t[:], bank_c[0][:, P:P + NE])
            nc.scalar.copy(nw[:], bank_c[0][:, 2 * P:2 * P + 1]).then_inc(small_ready, 1)
            act.wait_ge(small_ready, 1)
            for c in range(CK):
                cs = slice(c * CH, (c + 1) * CH)
                act.wait_ge(turned, c + 1)
                nc.scalar.activation(nt[:, cs], bank_y[c][:], ACT.Copy, scale=nw[:]).then_inc(nt_ready, 1)
                act.wait_ge(nt_ready, c + 1)
                nc.scalar.copy(nt_hi[:, cs], nt[:, cs]).then_inc(hi_ready, 1)

            def split_weights(n, half):
                act.wait_ge(w_in, 32 * n + 32)
                if not (isinstance(n, int) and n < 2):
                    act.wait_ge(h_used, TILES * (n - 1))
                for w in range(2):
                    nc.scalar.copy(w_hi[half][w][:], w_raw[w][:]).then_inc(w_hi_ready, 1)
                nc.scalar.copy(b1_now[:, half, :], b1[:, bass.ds(NF * n, NF)]).then_inc(b1_ready, 1)

            def rectify(n, half, c, f):
                k = TILES * n + NF * c + f
                act.wait_ge(h_filled, k + 1)
                if isinstance(n, int) and n == 0:
                    if c:
                        act.wait_ge(lo_pool, k - 3)
                    dst = h[:, f, :]
                else:
                    dst = r[:, f % 2, :]
                nc.scalar.activation(dst, bank_h[f % 2][:], ACT.Relu, bias=b1_now[:, half, f:f + 1]).then_inc(rectified, 1)

            def lead(n, c, f):
                k = TILES * n + NF * c + f
                if isinstance(n, int) and n == 0:
                    act.wait_ge(rectified, k + 1)
                else:
                    act.wait_ge(h_gated, TILES * (n - 1) + NF * c + f + 1)
                if not (isinstance(n, int) and k < NF):
                    act.wait_ge(h_used, k - NF + 1)
                nc.scalar.copy(h_hi[:, f, :], h[:, f, :]).then_inc(h_hi_ready, 1)

            def copy_output(c):
                act.wait_ge(h_used, TILES * NE + NF * (c + 1))
                if c >= 2:
                    act.wait_ge(y_turned, c - 1)
                nc.scalar.copy(y_t[:, c % 2, :], bank_y[c][:]).then_inc(y_copied, 1)

            def ffn(n, half, m=None):
                first_ffn, last_ffn = (isinstance(n, int) and n == v for v in (0, NE))
                act.wait_ge(b1_ready, n + 1)
                for c in range(CK):
                    for f in range(NF):
                        rectify(n, half, c, f)
                        if first_ffn:
                            lead(n, c, f)
                        elif c or f:
                            lead(n, c if f else c - 1, (f - 1) % NF)
                        if c == 2 and f == 0 and not last_ffn:
                            split_weights(n + 1, 1 - half)
                        if last_ffn and c >= 2 and f == 0:
                            copy_output(c - 2)
                        if last_ffn and c >= 2 and f == NF - 1:
                            ln.root(act, c - 2)
                    if first_ffn and c == 0:
                        act.wait_ge(routed, 1)
                        nc.scalar.activation(prob[:].rearrange("p t e -> p (t e)"), bank_c[1][:, 0:T * NE], ACT.Sigmoid).then_inc(gated, 1)
                    if first_ffn and c == 2:
                        for g in range(CK):
                            act.wait_ge(comb_turned, g + 1)
                            nc.scalar.copy(comb_t[:, g * CH:(g + 1) * CH], bank_c[g % 2][0:NE, :]).then_inc(comb_t_ready, 1)
                if not first_ffn:
                    lead(n, CK - 1, NF - 1)

            split_weights(0, 0)
            over_ffns(act, ffn)
            for c in range(CK - 2, CK):
                copy_output(c)
            for c in range(CK - 2, CK):
                ln.root(act, c)

        @block.vector
        def _(dve):
            ln.start(dve)
            nc.vector.memset(tiny[:], 1e-8).then_inc(eps_ready, 1)
            for t in range(T):
                nc.vector.tensor_tensor_reduce(out=n_tok[:, t, :], in0=X[:, t, :], in1=X[:, t, :], scale=1.0, scalar=0.0,
                                               op0=ALU.mult, op1=ALU.add, accum_out=sums[:, t:t + 1]).then_inc(squared, 1)
            dve.wait_ge(rooted, 1)
            nc.vector.reciprocal(rroot[:], root[:]).then_inc(inverted, 1)
            dve.wait_ge(inverted, 1)
            for c in range(CK):
                for j in range(4):
                    t = 4 * c + j
                    last = nc.vector.tensor_scalar(n_tok[:, t, :], X[:, t, :], rroot[:, t:t + 1], None, ALU.mult)
                last.then_inc(scaled, 1)
            for c in range(CK):
                cs = slice(c * CH, (c + 1) * CH)
                dve.wait_ge(hi_ready, c + 1)
                nc.vector.tensor_tensor(nt_lo[:, cs], nt[:, cs], nt_hi[:, cs].bitcast(F32), ALU.subtract).then_inc(lo_ready, 1)

            def split_weights(n, half):
                dve.wait_ge(w_hi_ready, 2 * n + 2)
                for w in range(2):
                    last = nc.vector.tensor_tensor(w_lo[half][w][:], w_raw[w][:], w_hi[half][w][:].bitcast(F32), ALU.subtract)
                last.then_inc(w_lo_ready, 1)

            def gate(n, half, c, f):
                dve.wait_ge(rectified, TILES * n + NF * c + f + 1)
                if f < LO_POOL:
                    dve.wait_ge(lo_pool, LO_POOL * CK * (n - 1) + TILES - 1 + LO_POOL * (c - 1) + f + 1)
                nc.vector.tensor_tensor(h[:, f, :], r[:, f % 2, :], gates[half][:, c * CH:(c + 1) * CH], ALU.mult).then_inc(h_gated, 1)

            def rest(n, c):
                dve.wait_ge(h_hi_ready, TILES * n + NF * (c + 1))
                nc.vector.tensor_tensor(h_lo[:, NF - 1, :], h[:, NF - 1, :], h_hi[:, NF - 1, :].bitcast(F32),
                                        ALU.subtract).then_inc(lo_dve, 1)

            def add_output(c):
                x = X[:, 4 * c:4 * c + 4, :]
                dve.wait_ge(y_turned, c + 1)
                nc.vector.tensor_tensor(x, x, bank_c[c % 2][:].rearrange("p (t d) -> p t d", d=P), ALU.add).then_inc(y_added, 1)
                dve.wait_ge(y_added, c + 1)
                ln.moments_of(dve, x, c)

            def normalise(c):
                ln.apply(dve, X[:, 4 * c:4 * c + 4, :], y[:, 4 * c:4 * c + 4, :], c)

            def ffn(n, half, m=None):
                first_ffn, last_ffn = (isinstance(n, int) and n == v for v in (0, NE))
                if first_ffn:
                    choose_gates()
                    split_weights(1, 1)
                    rest(0, CK - 1)
                    return
                dve.wait_ge(gates_in[half], 16 * (m + 1))
                for c in range(CK):
                    for f in range(NF):
                        gate(n, half, c, f)
                        if f == 0 and c:
                            rest(n, c - 1)
                        if c == 2 and f == 1 and not last_ffn:
                            split_weights(n + 1, 1 - half)
                        if last_ffn and c >= 2 and f == 2:
                            add_output(c - 2)
                    if last_ffn and c >= 2:
                        normalise(c - 2)
                rest(n, CK - 1)

            def choose_gates():
                steps = 0

                def then(ins):
                    nonlocal steps
                    steps += 1
                    ins.then_inc(pick, 1)
                    dve.wait_ge(pick, steps)

                dve.wait_ge(gated, 1)
                for t in range(T):
                    last = nc.vector.max(top[:, t, :], prob[:, t, :])
                last.then_inc(picked, 1)
                dve.wait_ge(picked, 1)
                for t in range(T):
                    last = nc.vector.max_index(top_at[:, t, :], top[:, t, :], prob[:, t, :])
                dve.wait_ge(lane_ready, 1)
                then(last)
                wide = lambda ap: ap.broadcast_to((P, T, NE))
                then(nc.vector.tensor_copy(at[:], top_at[:, :, 0:2]))
                then(nc.vector.tensor_copy(lane[:], lane_i[:]))
                then(nc.vector.tensor_tensor(first[:], wide(lane[:].unsqueeze(1)), wide(at[:, :, 0:1]), ALU.is_equal))
                then(nc.vector.tensor_tensor(second[:], wide(lane[:].unsqueeze(1)), wide(at[:, :, 1:2]), ALU.is_equal))
                then(nc.vector.tensor_tensor(first[:], first[:], second[:], ALU.add))
                then(nc.vector.tensor_tensor(first[:], first[:], prob[:], ALU.mult))
                then(nc.vector.tensor_tensor(total[:], top[:, :, 0], top[:, :, 1], ALU.add))
                then(nc.vector.tensor_scalar(total[:], total[:], 1e-6, None, ALU.add))
                then(nc.vector.reciprocal(share[:], total[:]))
                then(nc.vector.tensor_tensor(comb_e[:], first[:], wide(share[:].unsqueeze(2)), ALU.mult))
                nc.vector.tensor_tensor(X[:], X[:], shared_b2[:].unsqueeze(1).broadcast_to((P, T, P)), ALU.add).then_inc(comb_ready, 1)
                dve.wait_ge(comb_ready, 1)

            split_weights(0, 0)
            over_ffns(dve, ffn)
            for c in range(CK - 2, CK):
                add_output(c)
                normalise(c)


def store_x(nc, persist, out):
    with ExitStack() as ctx:
        stored = ctx.enter_context(nc.semaphore("stored"))
        block = ctx.enter_context(nc.Block())

        @block.sync
        def _(sp):
            sp.dma_start(out.rearrange("b (t p) d -> p (b t) d", p=P), persist["X"][:]).then_inc(stored, 16)
            sp.wait_ge(stored, 16)


def build(nc, a, out, stop=0):
    B, S, D = a["L0_attn_query"].shape
    H, _, E = a["L0_attn_Wq"].shape
    T = B * S // P
    with ExitStack() as ctx:
        sb = lambda n, s, d: ctx.enter_context(nc.sbuf_tensor(n, s, d))
        persist = {"B": B, "Wq": a["L0_attn_Wq"], "Wk": a["L0_attn_Wk"], "Wp": a["L0_attn_Wp"],
                   "X": sb("x_tokens", [P, T, D], F32), "ident": sb("ident", [P, P], F32)}
        with ExitStack() as layer0:
            sb0 = lambda n, s, d: layer0.enter_context(nc.sbuf_tensor(n, s, d))
            persist.update(xhi=sb0("xhi", [P, B * S], F32R), xlo=sb0("xlo", [P, B * S], F32R),
                           V=sb0("v_parts", [P, H, T, 2 * E + 2], F16))
            project_values(nc, a["L0_attn_query"], a["L0_attn_Wv"], a["L0_attn_bp"], persist)
            attend_heads(nc, persist)
        if stop == 1:
            return store_x(nc, persist, out)
        quantised_ffn(nc, a, persist)
        if stop == 2:
            return store_x(nc, persist, out)
        attend_once(nc, a, persist)
        if stop == 3:
            return store_x(nc, persist, out)
        mix_experts(nc, a, persist, out)


_INS = ['L0_attn_query',
        'L0_attn_Wq',
        'L0_attn_Wk',
        'L0_attn_Wv',
        'L0_attn_Wp',
        'L0_attn_bp',
        'L0_ffn_ln_gamma',
        'L0_ffn_ln_beta',
        'L0_ffn_fc1_q',
        'L0_ffn_fc1_scales',
        'L0_ffn_fc1_bias',
        'L0_ffn_fc2_q',
        'L0_ffn_fc2_scales',
        'L0_ffn_fc2_bias',
        'L1_attn_wq',
        'L1_attn_wk',
        'L1_attn_wv',
        'L1_attn_wo',
        'L1_ffn_norm_weight',
        'L1_ffn_router_w',
        'L1_ffn_sw1',
        'L1_ffn_sb1',
        'L1_ffn_sw2',
        'L1_ffn_sb2',
        'L1_ffn_ew1',
        'L1_ffn_eb1',
        'L1_ffn_ew2',
        'L1_ffn_eb2']
_OUTS = [((2, 1024, 128), "float32")]


def kernel(**inputs):
    import numpy as _np
    import concourse.bacc as _bacc
    from concourse import mybir as _mybir
    from concourse.bass_utils import run_bass_kernel_spmd as _run

    nc = _bacc.Bacc("TRN2", target_bir_lowering=False, num_devices=1)
    arrays, args = {}, {}
    for name in _INS:
        a = _np.ascontiguousarray(inputs[name])
        arrays[f"in_{name}_dram"] = a
        args[name] = nc.dram_tensor(f"in_{name}_dram", a.shape, _mybir.dt.from_np(a.dtype), kind="ExternalInput").ap()
    shape, dtype = _OUTS[0]
    out = nc.dram_tensor("out_0_dram", shape, _mybir.dt.from_np(_np.dtype(dtype)), kind="ExternalOutput").ap()
    build(nc, args, out)
    r = _run(nc, [arrays], core_ids=[0])
    return r.results[0]["out_0_dram"]
```

```python
from contextlib import ExitStack

import concourse.bass as bass
from concourse import mybir

ALU = mybir.AluOpType
ACT = mybir.ActivationFunctionType
AX = mybir.AxisListType
F32 = mybir.dt.float32
F32R = mybir.dt.float32r
F16 = mybir.dt.float16
BF16 = mybir.dt.bfloat16
I32 = mybir.dt.int32
U32 = mybir.dt.uint32

P = 128
CH = 512


def make_identity(nc, pool, ident, zeroed, done):
    nc.gpsimd.memset(ident[:], 0.0).then_inc(zeroed, 1)
    pool.wait_ge(zeroed, 1)
    nc.gpsimd.affine_select(out=ident[:], in_=ident[:], compare_op=ALU.not_equal, fill=1.0, base=0,
                            pattern=[[-1, P]], channel_multiplier=1).then_inc(done, 1)


def attend_heads(nc, a, persist):
    X, xhi, xlo, V, ident = (persist[k] for k in ("X", "xhi", "xlo", "V", "ident"))
    E = P // 2
    T, H, VW = X.shape[1], V.shape[1], V.shape[3]
    PAIRS = H // 2
    TB = T // persist["B"]
    N = TB * P
    PAIRS_ALL = PAIRS * persist["B"]
    UNITS = N // P
    SCALE = float(E) ** -0.5
    DEN = E
    MAX_N = 2 * UNITS
    MAX_LAG = 4
    FIRST_MAX = MAX_N - MAX_LAG
    FIRST_MAX_AT = 9
    HB = CH // E
    V_N = T * H // HB
    PV_TO = [0, 4, 9, 13, 18, 22, 27, 32]
    GROUP_AT = {2: 0, 4: 1, 6: 2, 7: 3}
    POOL_UNITS = [(0, 2, 4, 6), (0, 2, 4, 6), (0, 2, 3, 5, 6), (0, 2, 3, 5, 6)]
    OT_AT, Y_AT = 3, 6
    PROJECT_AT = {(0, 4): ("q", 0, 0), (0, 6): ("q", 1, 1), (1, 1): ("k", 0, 2), (1, 4): ("k", 1, 3)}
    by_pool = [sum(len(POOL_UNITS[j]) for j in range(s + 1)) for s in range(4)]
    by_dve = [UNITS * (s + 1) - by_pool[s] for s in range(4)]

    with ExitStack() as ctx:
        sb = lambda n, s, d: ctx.enter_context(nc.sbuf_tensor(n, s, d))
        ps = lambda n: ctx.enter_context(nc.psum_tensor(n, [P, CH], F32))
        sem = lambda n: ctx.enter_context(nc.semaphore(n))
        probs = sb("probs", [P, 2, UNITS, CH], F32)
        probs_lo = sb("probs_lo", [P, 2, UNITS, CH], F16)
        ka = [sb(f"ka{i}", [P, N], F32R) for i in range(2)]
        kb = [sb(f"kb{i}", [P, N], F32R) for i in range(2)]
        qa = [sb(f"qa{i}", [P, N], F32R) for i in range(2)]
        qb = [sb(f"qb{i}", [P, N], F32R) for i in range(2)]
        t_hi = {w: sb(f"t{w}_hi", [P, N], F32R) for w in "qk"}
        t_lo = {w: sb(f"t{w}_lo", [P, N], F32R) for w in "qk"}
        full = sb("full", [P, 2, CH], F32)
        v_now = [sb(f"v_now{i}", [P, UNITS, VW], F16) for i in range(2)]
        w_raw = {w: sb(f"w{w}_raw", [P, P], F32) for w in "qk"}
        w_hi = {w: sb(f"w{w}_hi", [P, P], F32R) for w in "qk"}
        w_lo = {w: sb(f"w{w}_lo", [P, P], F32R) for w in "qk"}
        o_parts = sb("o_parts", [P, 2, 4, P + 1], F32)
        o_pair = sb("o_pair", [P, 2, 4, P], F32)
        o_turned = sb("o_turned", [P, CH], F32)
        wp_pair = sb("wp_pair", [P, P], F32)
        rden = sb("rden", [P, 4], F32)
        maxes = sb("maxes", [P, UNITS, 2], F32)
        negmax = sb("negmax", [P, 4, 4], F32R)
        bank_s = [ps(f"bank_s{i}") for i in range(2)]
        bank_m = [ps(f"bank_m{i}") for i in range(2)]
        bank_o = [ps(f"bank_o{i}") for i in range(2)]
        bank_x = [ps(f"bank_x{i}") for i in range(2)]

        ones_ready = sem("kb_ones_ready")
        staged = sem("weights_staged")
        x_filled = [sem(f"bank_x{i}_filled") for i in range(2)]
        x_taken = [sem(f"bank_x{i}_taken") for i in range(2)]
        lo_made = sem("qk_lo_ready")
        head_in = [sem(f"head{i}_in") for i in range(2)]
        tail_in = [sem(f"tail{i}_in") for i in range(2)]
        v_in = [sem(f"v_now{i}_in") for i in range(2)]
        wp_in = sem("wp_pair_in")
        row_in = [sem(f"negmax_row{i}_in") for i in range(4)]
        m_filled, m_reduced = sem("max_scores_ready"), sem("max_reduced")
        c_ready = sem("negmax_ready")
        s_filled, exp_done = sem("scores_ready"), sem("exp_done")
        lo_dve, lo_pool = sem("probs_lo_by_vector"), sem("probs_lo_by_gpsimd")
        pv_done, rden_ready, o_taken, o_added = sem("pv_done"), sem("rden_ready"), sem("o_taken"), sem("o_added")
        raw_in = sem("weights_raw_in")
        zeros, zeros_ready = sb("zeros", [P, P], F32), sem("zeros_ready")
        wstep = sem("weights_hi_staged")
        wv_raw = probs[:, 1, 0:H * E // CH, :].rearrange("p k n -> p (k n)")
        wv_hi, wv_lo = ka[1][:, 0:H * E], qa[1][:, 0:H * E]
        bp_rows = o_turned[:, 0:P]
        bank_t = [bank_m[0], bank_m[1], bank_s[0], bank_s[1]]
        bank_v = [bank_o[0], bank_o[1], bank_s[0], bank_s[1]]
        x_in = [sem(f"x{g}_in") for g in range(T // 4)]
        wv_in, bp_in = sem("wv_in"), sem("bp_in")
        zeroed, ident_ready, v_ones_ready = sem("ident_zeroed"), sem("ident_ready"), sem("v_ones_ready")
        turned, xhi_ready, xlo_ready = sem("x_turned"), sem("xhi_ready"), sem("xlo_ready")
        wvhi_ready, wvlo_ready = sem("wvhi_ready"), sem("wvlo_ready")
        v_filled, vhi_done, vlo_done = sem("v_filled"), sem("vhi_done"), sem("vlo_done")
        block = ctx.enter_context(nc.Block())

        HEAD_DMAS, TAIL_DMAS = 16 * 4, 16 * 2

        def over_steps(eng, step, before, after):
            before()
            step(0, 0, first=True)
            step(0, 1, first=True)
            with eng.Fori(0, PAIRS_ALL - 1) as i:
                step(i, 2)
                step(i, 3)
                step(i + 1, 0)
                step(i + 1, 1)
            step(PAIRS_ALL - 1, 2, last=True)
            step(PAIRS_ALL - 1, 3, last=True)
            after()

        def max_at(i, s, u, first, last):
            h, c = s // 2, s % 2
            j = c * UNITS + u - MAX_LAG
            if j < 0:
                return h, 2 * i + h, j + MAX_N
            return None if last and h == 1 else (1 - h, 2 * i + h + 1, j)

        x0_base = lambda i: 4 * i - 2
        x1_base = lambda i: 4 * i + 2

        @block.sync
        def _(sp):
            value = lambda v: v if isinstance(v, int) else sp.snap(v)

            def load_head(h, i, used_up=0):
                parts, used_up = value(4 * i + 4), value(used_up)
                if not (isinstance(used_up, int) and used_up == 0):
                    sp.wait_ge(s_filled, used_up)
                sp.wait_ge(lo_made, parts)
                rows = slice(h * E, (h + 1) * E)
                f = lambda a: a.bitcast(F32)
                for dst, src in ((ka[h][0:E, :], t_hi["k"]), (qa[h][0:E, :], t_hi["q"]), (qa[h][E:P, :], t_hi["q"]),
                                 (ka[h][E:P, :], t_lo["k"])):
                    sp.dma_start(f(dst), f(src[rows, :])).then_inc(head_in[h], 16)
                for dst, src in ((kb[h][0:E, :], t_hi["k"]), (qb[h][0:E, :], t_lo["q"])):
                    sp.dma_start(f(dst), f(src[rows, :])).then_inc(tail_in[h], 16)

            def load_row(h, c, n):
                sp.wait_ge(c_ready, n + 1)
                dst = qb[h][E:E + 1, c * CH:(c + 1) * CH].bitcast(F32).rearrange("o (p t) -> o p t", t=4)
                sp.dma_start(dst, negmax[:, 2 * h + c, :].bitcast(F32)).then_inc(row_in[2 * h + c], 16)

            def load_weights(i):
                first_head = value((i % PAIRS) * 2)
                if not (isinstance(i, int) and i == 0):
                    sp.wait_ge(staged, i)
                for w in "qk":
                    src = persist["W" + w][bass.ds(first_head, 2), :, :].rearrange("h d e -> d h e")
                    sp.dma_start(w_raw[w][:].rearrange("d (h e) -> d h e", e=E), src).then_inc(raw_in, 16)

            def load_v(h, i, used_up=0):
                at = (((i % PAIRS) * 2 + h) * T + (i // PAIRS) * TB) * VW
                if not (isinstance(used_up, int) and used_up == 0):
                    sp.wait_ge(pv_done, used_up)
                src = V[:].rearrange("p h t v -> p (h t v)")[:, bass.ds(at, UNITS * VW)]
                sp.dma_start(v_now[h][:].rearrange("p t v -> p (t v)"), src).then_inc(v_in[h], 16)

            def load_wp(i, first):
                head = value((i % PAIRS) * 2)
                if not first:
                    sp.wait_ge(x_taken[0], x0_base(i) + 4)
                rows_of = persist["Wp"].rearrange("(e h) o -> h e o", h=H)
                src = rows_of[bass.ds(head, 2), :, :]
                sp.dma_start(wp_pair[0:E, :], src[0]).then_inc(wp_in, 16)
                sp.dma_start(wp_pair[E:P, :], src[1]).then_inc(wp_in, 16)

            def before():
                x = a["L0_attn_query"].rearrange("b (t p) d -> p (b t) d", p=P)
                for g in range(T // 4):
                    sp.dma_start(X[:, 4 * g:4 * g + 4, :], x[:, 4 * g:4 * g + 4, :]).then_inc(x_in[g], 16)
                    if g == 0:
                        load_weights(0)
                load_weights(1)
                load_head(0, 0)
                load_row(0, 0, 0)
                sp.wait_ge(v_ones_ready, 2)
                sp.wait_ge(vlo_done, V_N)
                load_v(0, 0)

            def step(i, s, first=False, last=False):
                if s == 0:
                    load_head(1, i, 0 if first else 32 * i)
                    load_weights(i + 2)
                    load_row(0, 1, 4 * i + 1)
                if s == 1:
                    load_v(1, i, 0 if first else 16 * i)
                    load_row(1, 0, 4 * i + 2)
                if s == 2:
                    if not last:
                        load_head(0, i + 1, 32 * i + 16)
                    load_row(1, 1, 4 * i + 3)
                    load_wp(i, isinstance(i, int) and i == 0)
                if s == 3 and not last:
                    load_v(0, i + 1, 16 * i + 8)
                    load_row(0, 0, 4 * i + 4)

            over_steps(sp, step, before, lambda: None)

        @block.tensor
        def _(pe):
            def project(which, c, i, bank, use):
                pe.wait_ge(staged, i + 1)
                if not (isinstance(use, int) and use == 0):
                    pe.wait_ge(x_taken[bank], use)
                col = ((i // PAIRS) % persist["B"]) * N + c * CH
                out, xs = bank_x[bank][:], bass.ds(col, CH)
                nc.tensor.matmul(out, w_lo[which][:], xhi[:, xs], start=True, stop=False)
                nc.tensor.matmul(out, w_hi[which][:], xlo[:, xs], start=False, stop=False)
                nc.tensor.matmul(out, w_hi[which][:], xhi[:, xs], start=False, stop=True).then_inc(x_filled[bank], 1)

            def max_scores(h, j, n):
                if not (isinstance(n, int) and n < 2):
                    pe.wait_ge(m_reduced, n - 1)
                qt, half = j // 2, j % 2
                qs = qa[h][:, (qt // 4) * CH:(qt // 4 + 1) * CH].rearrange("d (p t) -> d t p", t=4)[:, qt % 4, :]
                nc.tensor.matmul(bank_m[j % 2][:], qs, ka[h][:, half * CH:(half + 1) * CH],
                                 start=True, stop=True).then_inc(m_filled, 1)

            def times_v(i, s, done, upto):
                v = v_now[s // 2]
                hi_of = probs[:, s % 2].bitcast(BF16).rearrange("p k (q two) -> p k q two", two=2)
                for n in range(done, upto):
                    qt, kt = n // UNITS, n % UNITS
                    if n == 0 and s % 2 == 0:
                        pe.wait_ge(v_in[s // 2], 16 * (i + 1))
                    if kt == 0 and not (isinstance(i, int) and i == 0 and s == 0 and qt < 2):
                        pe.wait_ge(o_taken, 16 * i + 4 * s + qt - 1)
                    if n == 0:
                        pe.wait_ge(lo_pool, by_pool[3] * i + by_pool[s])
                        pe.wait_ge(lo_dve, by_dve[3] * i + by_dve[s])
                    qs = slice(qt * P, (qt + 1) * P)
                    acc = bank_o[qt % 2]
                    low = lambda: nc.tensor.matmul(acc[:, 0:E + 1], probs_lo[:, s % 2, kt, qs], v[:, kt, 0:E + 1],
                                                   start=False, stop=False, skip_group_check=True)
                    if kt == UNITS - 1:
                        low()
                    last = nc.tensor.matmul(acc[:, 0:2 * E + 1], hi_of[:, kt, qs, 1], v[:, kt, 0:2 * E + 1],
                                            start=(kt == 0), stop=(kt == UNITS - 1))
                    if kt < UNITS - 1:
                        low()
                    else:
                        last.then_inc(pv_done, 1)

            def turn_o(i, c, use):
                pe.wait_ge(o_added, 4 * i + c + 3)
                pe.wait_ge(x_taken[0], use)
                for t in range(4):
                    last = nc.tensor.transpose(bank_x[0][:, t * P:(t + 1) * P], o_pair[:, c, t, :], ident[:])
                last.then_inc(x_filled[0], 1)

            def times_wp(i, c, use):
                pe.wait_ge(x_taken[0], use)
                pe.wait_ge(wp_in, 32 * (i + 1))
                for t in range(4):
                    last = nc.tensor.matmul(bank_x[0][:, t * P:(t + 1) * P], o_turned[:, t * P:(t + 1) * P],
                                            wp_pair[:], start=True, stop=True)
                last.then_inc(x_filled[0], 1)

            def before():
                pe.wait_ge(ident_ready, 1)
                for g in range(T // 4):
                    pe.wait_ge(x_in[g], 16)
                    for j in range(4):
                        last = nc.tensor.transpose(bank_t[g][:, j * P:(j + 1) * P], X[:, 4 * g + j, :], ident[:])
                    last.then_inc(turned, 1)
                pe.wait_ge(xlo_ready, TB // 4)
                for w, c, bank, use in (("q", 0, 1, 0), ("q", 1, 0, 0), ("k", 0, 1, 1), ("k", 1, 0, 1)):
                    project(w, c, 0, bank, use)
                pe.wait_ge(xlo_ready, T // 4)
                pe.wait_ge(wvlo_ready, 1)
                for n in range(V_N):
                    t, hb = n // (H // HB), n % (H // HB)
                    if n >= 4:
                        pe.wait_ge(vlo_done, n - 3)
                    out, ws, xs = bank_v[n % 4][:], slice(hb * CH, (hb + 1) * CH), slice(t * P, (t + 1) * P)
                    nc.tensor.matmul(out, xlo[:, xs], wv_hi[:, ws], start=True, stop=False)
                    nc.tensor.matmul(out, xhi[:, xs], wv_lo[:, ws], start=False, stop=False)
                    nc.tensor.matmul(out, xhi[:, xs], wv_hi[:, ws], start=False, stop=True).then_inc(v_filled, 1)
                    j = (n - FIRST_MAX_AT) // 2
                    if n == FIRST_MAX_AT:
                        pe.wait_ge(head_in[0], HEAD_DMAS)
                    if (n - FIRST_MAX_AT) % 2 == 0 and 0 <= j < FIRST_MAX:
                        max_scores(0, j, j)
                pe.wait_ge(vlo_done, V_N)

            def step(i, s, first=False, last=False):
                h, c = s // 2, s % 2
                for u in range(UNITS):
                    n = 32 * i + 8 * s + u
                    if u == 0:
                        pe.wait_ge(row_in[s], 16 * (i + 1))
                        if s == 0 and first:
                            pe.wait_ge(ones_ready, 1)
                        if c == 0:
                            pe.wait_ge(tail_in[h], TAIL_DMAS * (i + 1))
                    if not (first and s == 0 and u < 2):
                        pe.wait_ge(exp_done, n - 1)
                    ks, qs = slice(u * P, (u + 1) * P), slice(c * CH, (c + 1) * CH)
                    nc.tensor.matmul(bank_s[u % 2][:], kb[h][0:E + 1, ks], qb[h][0:E + 1, qs], start=True, stop=False)
                    nc.tensor.matmul(bank_s[u % 2][:], ka[h][:, ks], qa[h][:, qs], start=False, stop=True).then_inc(s_filled, 1)
                    if m := max_at(i, s, u, first, last):
                        if m[2] == 0:
                            pe.wait_ge(head_in[1 - h], HEAD_DMAS * (i + 1 + h))
                        max_scores(m[0], m[2], MAX_N * m[1] + m[2])
                    if not (first and s == 0):
                        pi, psn = (i, s - 1) if s else (i - 1, 3)
                        times_v(pi, psn, PV_TO[u - 1] if u else 0, PV_TO[u])
                    if (s, u) in PROJECT_AT:
                        w, ch, k = PROJECT_AT[s, u]
                        project(w, ch, i + 1, 1, x1_base(i) + k)
                    if not first and s < 2:
                        if u == OT_AT:
                            turn_o(i - 1, s, x0_base(i) + 2 * s)
                        if u == Y_AT:
                            times_wp(i - 1, s, x0_base(i) + 2 * s + 1)

            def after():
                i = PAIRS_ALL
                times_v(i - 1, 3, 0, 4 * UNITS)
                for c in range(2):
                    turn_o(i - 1, c, x0_base(i) + 2 * c)
                    times_wp(i - 1, c, x0_base(i) + 2 * c + 1)

            over_steps(pe, step, before, after)

        @block.scalar
        def _(act):
            def take_part(which, c, bank, filled, n):
                act.wait_ge(x_filled[bank], filled)
                cs = slice(c * CH, (c + 1) * CH)
                if not (isinstance(n, int) and n < 2):
                    act.wait_ge(lo_made, n - 1)
                nc.scalar.copy(full[:, c, :], bank_x[bank][:])
                nc.scalar.copy(t_hi[which][:, cs], bank_x[bank][:]).then_inc(x_taken[bank], 1)

            def take_o(i, s, qt):
                act.wait_ge(rden_ready, 16 * i + 4 * s + qt + 1)
                src = bank_o[qt % 2][:]
                out = o_parts[:, s % 2, qt, :]
                nc.scalar.activation(out, src[:, 0:P + 1], ACT.Copy, scale=rden[:, qt:qt + 1]).then_inc(o_taken, 1)

            def take_turned(filled):
                act.wait_ge(x_filled[0], filled)
                nc.scalar.copy(o_turned[:], bank_x[0][:]).then_inc(x_taken[0], 1)

            def before():
                act.dma_start(wv_raw.rearrange("d (h e) -> d h e", e=E), a["L0_attn_Wv"].rearrange("h d e -> d h e")).then_inc(wv_in, 16)
                act.dma_start(bp_rows, a["L0_attn_bp"].rearrange("(o n) -> o n", o=1).broadcast_to((P, P))).then_inc(bp_in, 16)
                for g in range(T // 4):
                    act.wait_ge(turned, g + 1)
                    nc.scalar.copy(xhi[:, g * CH:(g + 1) * CH], bank_t[g][:]).then_inc(xhi_ready, 1)
                act.wait_ge(wv_in, 16)
                nc.scalar.copy(wv_hi, wv_raw).then_inc(wvhi_ready, 1)
                for n, (w, c, bank, filled) in enumerate((("q", 0, 1, 1), ("q", 1, 0, 1), ("k", 0, 1, 2), ("k", 1, 0, 2))):
                    take_part(w, c, bank, filled, n)
                for n in range(V_N):
                    t, hb = n // (H // HB), n % (H // HB)
                    act.wait_ge(v_filled, n + 1)
                    nc.scalar.copy(V[:, hb * HB:(hb + 1) * HB, t, 0:E],
                                   bank_v[n % 4][:].rearrange("p (h e) -> p h e", e=E)).then_inc(vhi_done, 1)

            def step(i, s, first=False, last=False):
                c = s % 2
                for u in range(UNITS):
                    if u == 0 and not (first and s < 2):
                        bi, bs = (i, s - 2) if s >= 2 else (i - 1, s + 2)
                        take_o(bi, bs, 3)
                    if u and u - 1 in GROUP_AT and not (first and s == 0):
                        bi, bs = (i, s - 1) if s else (i - 1, 3)
                        if GROUP_AT[u - 1] == 0 and not first:
                            act.wait_ge(o_added, 4 * i + (1 if s == 2 else s - 2))
                        take_o(bi, bs, GROUP_AT[u - 1])
                    if (s, u - 1) in PROJECT_AT:
                        w, ch, k = PROJECT_AT[s, u - 1]
                        if k == 0:
                            for g in (0, 1):
                                act.wait_ge(head_in[g], HEAD_DMAS * (i + 1))
                                act.wait_ge(tail_in[g], TAIL_DMAS * (i + 1))
                        take_part(w, ch, 1, x1_base(i) + k + 1, 4 * (i + 1) + k)
                    n = 32 * i + 8 * s + u
                    act.wait_ge(s_filled, n + 1)
                    nc.scalar.activation(probs[:, c, u, :], bank_s[u % 2][:], ACT.Exp, scale=SCALE).then_inc(exp_done, 1)
                    if not first and s < 2 and u == OT_AT + 1:
                        take_turned(x0_base(i) + 2 * s + 1)

            def after():
                i = PAIRS_ALL
                take_o(i - 1, 2, 3)
                act.wait_ge(o_added, 4 * i - 2)
                for qt in range(4):
                    take_o(i - 1, 3, qt)
                take_turned(x0_base(i) + 1)
                take_turned(x0_base(i) + 3)

            over_steps(act, step, before, after)

        @block.vector
        def _(dve):
            def reduce(j, n):
                dve.wait_ge(m_filled, n + 1)
                nc.vector.tensor_reduce(maxes[:, j // 2, j % 2:j % 2 + 1], bank_m[j % 2][:], AX.X, ALU.max).then_inc(m_reduced, 1)

            def negate(h, c, j0, n, rows):
                dve.wait_ge(m_reduced, j0)
                if not (isinstance(rows, int) and rows < 4):
                    dve.wait_ge(row_in[2 * h + c], n)
                nc.vector.tensor_reduce(negmax[:, 2 * h + c, :], maxes[:, 4 * c:4 * c + 4, :], AX.X, ALU.max,
                                        negate=True).then_inc(c_ready, 1)

            def invert(i, s, qt):
                dve.wait_ge(pv_done, 16 * i + 4 * s + qt + 1)
                nc.vector.reciprocal(rden[:, qt:qt + 1], bank_o[qt % 2][:, DEN:DEN + 1]).then_inc(rden_ready, 1)

            def add_y(i, c, filled):
                dve.wait_ge(x_filled[0], filled)
                x_flat = X[:].rearrange("p t d -> p (t d)")
                at = ((i // PAIRS) * TB + 4 * c) * P
                xs = x_flat[:, bass.ds(at, CH)]
                nc.vector.tensor_tensor(xs, xs, bank_x[0][:], ALU.add).then_inc(x_taken[0], 1)

            def before():
                for h in range(2):
                    last = nc.vector.memset(kb[h][E:E + 1, :].bitcast(F32), 1.0)
                last.then_inc(ones_ready, 1)
                for g in range(T // 4):
                    dve.wait_ge(xhi_ready, g + 1)
                    nc.vector.tensor_tensor(xlo[:, g * CH:(g + 1) * CH], bank_t[g][:],
                                            xhi[:, g * CH:(g + 1) * CH].bitcast(F32), ALU.subtract).then_inc(xlo_ready, 1)
                dve.wait_ge(wvhi_ready, 1)
                nc.vector.tensor_tensor(wv_lo, wv_raw, wv_hi.bitcast(F32), ALU.subtract).then_inc(wvlo_ready, 1)
                for n in range(V_N):
                    t, hb = n // (H // HB), n % (H // HB)
                    dve.wait_ge(vhi_done, n + 1)
                    nc.vector.tensor_tensor(V[:, hb * HB:(hb + 1) * HB, t, E + 1:2 * E + 1],
                                            bank_v[n % 4][:].rearrange("p (h e) -> p h e", e=E),
                                            V[:, hb * HB:(hb + 1) * HB, t, 0:E], ALU.subtract).then_inc(vlo_done, 1)
                    j = (n - FIRST_MAX_AT) // 2
                    if (n - FIRST_MAX_AT) % 2 == 0 and 0 <= j < FIRST_MAX:
                        reduce(j, j)
                        if j == MAX_N // 2:
                            negate(0, 0, MAX_N // 2, 0, 0)

            def step(i, s, first=False, last=False):
                h, c = s // 2, s % 2
                for u in range(UNITS):
                    if m := max_at(i, s, u, first, last):
                        reduce(m[2], MAX_N * m[1] + m[2])
                    if u == MAX_LAG:
                        if c == 0:
                            negate(h, 1, MAX_N * (2 * i + h) + MAX_N, 16 * i, 0 if first or (isinstance(i, int) and i == 0) else 4)
                        if c == 1 and not (last and h == 1):
                            negate(1 - h, 0, MAX_N * (2 * i + h + 1) + MAX_N // 2, 16 * (i + h), 0 if first and h == 0 else 4)
                    if u in GROUP_AT and not (first and s == 0):
                        bi, bs = (i, s - 1) if s else (i - 1, 3)
                        invert(bi, bs, GROUP_AT[u])
                    if u not in POOL_UNITS[s]:
                        n = 32 * i + 8 * s + u
                        dve.wait_ge(exp_done, n + 1)
                        p = probs[:, c, u, :]
                        hi = p.bitcast(BF16).rearrange("p (q two) -> p q two", two=2)[:, :, 1]
                        nc.vector.tensor_tensor(probs_lo[:, c, u, :], p, hi, ALU.subtract).then_inc(lo_dve, 1)
                    if not first and s < 2 and u == Y_AT + 1:
                        add_y(i - 1, s, x0_base(i) + 2 * s + 2)

            def after():
                i = PAIRS_ALL
                for qt in range(4):
                    invert(i - 1, 3, qt)
                for c in range(2):
                    add_y(i - 1, c, x0_base(i) + 2 * c + 2)
                dve.wait_ge(x_taken[0], x0_base(i) + 4)

            over_steps(dve, step, before, after)

        @block.gpsimd
        def _(pool):
            def stage(i):
                pool.wait_ge(raw_in, 32 * i + 32)
                for w in "qk":
                    last = nc.gpsimd.tensor_tensor(w_hi[w][:], w_raw[w][:], zeros[:], ALU.add)
                last.then_inc(wstep, 1)
                pool.wait_ge(wstep, i + 1)
                for w in "qk":
                    last = nc.gpsimd.tensor_tensor(w_lo[w][:], w_raw[w][:], w_hi[w][:].bitcast(F32), ALU.subtract)
                last.then_inc(staged, 1)

            def make_lo(which, c, bank, taken):
                pool.wait_ge(x_taken[bank], taken)
                cs = slice(c * CH, (c + 1) * CH)
                nc.gpsimd.tensor_tensor(t_lo[which][:, cs], full[:, c, :], t_hi[which][:, cs].bitcast(F32),
                                        ALU.subtract).then_inc(lo_made, 1)

            def add_o(i, s):
                pool.wait_ge(o_taken, 16 * i + 4 * s + 4)
                h, c = s // 2, s % 2
                nc.gpsimd.tensor_tensor(o_pair[:, c, :, h * E:(h + 1) * E], o_parts[:, c, :, 0:E], o_parts[:, c, :, E + 1:P + 1],
                                        ALU.add).then_inc(o_added, 1)

            def before():
                make_identity(nc, pool, ident, zeroed, ident_ready)
                nc.gpsimd.memset(zeros[:], 0.0).then_inc(zeros_ready, 1)
                pool.wait_ge(zeros_ready, 1)
                stage(0)
                for w, c, bank, taken in (("q", 0, 1, 1), ("q", 1, 0, 1), ("k", 0, 1, 2), ("k", 1, 0, 2)):
                    make_lo(w, c, bank, taken)
                stage(1)
                nc.gpsimd.memset(V[:, :, :, 2 * E + 1:2 * E + 2], 0.0).then_inc(v_ones_ready, 1)
                nc.gpsimd.memset(V[:, :, :, E:E + 1], 1.0).then_inc(v_ones_ready, 1)
                pool.wait_ge(bp_in, 16)
                pool.wait_ge(turned, T // 4)
                nc.gpsimd.tensor_tensor(X[:], X[:], bp_rows.unsqueeze(1).broadcast_to((P, T, P)), ALU.add)

            def step(i, s, first=False, last=False):
                c = s % 2
                for u in range(UNITS):
                    if u in POOL_UNITS[s]:
                        n = 32 * i + 8 * s + u
                        pool.wait_ge(exp_done, n + 1)
                        p = probs[:, c, u, :]
                        hi = p.bitcast(BF16).rearrange("p (q two) -> p q two", two=2)[:, :, 1]
                        nc.gpsimd.tensor_tensor(probs_lo[:, c, u, :], p, hi, ALU.subtract).then_inc(lo_pool, 1)
                    if u == 1 and not (first and s < 2):
                        bi, bs = (i, s - 2) if s >= 2 else (i - 1, s + 2)
                        add_o(bi, bs)
                    if (s, u - 1) in PROJECT_AT:
                        w, ch, k = PROJECT_AT[s, u - 1]
                        make_lo(w, ch, 1, x1_base(i) + k + 1)
                    if s == 1 and u == UNITS - 1:
                        pool.wait_ge(x_filled[1], x1_base(i) + 4)
                        stage(i + 2)

            def after():
                i = PAIRS_ALL
                add_o(i - 1, 2)
                add_o(i - 1, 3)

            over_steps(pool, step, before, after)


class Normaliser:

    def __init__(self, nc, ctx, name, eps):
        sb = lambda n, s: ctx.enter_context(nc.sbuf_tensor(f"{name}_{n}", s, F32))
        sem = lambda n: ctx.enter_context(nc.semaphore(f"{name}_{n}"))
        self.nc, self.eps = nc, eps
        self.stats, self.mv = sb("stats", [P, 4, 6]), sb("mean_var", [P, 4, 2])
        self.std, self.rstd = sb("std", [P, 4]), sb("rstd", [P, 4])
        self.eps_col = sb("eps", [P, 1])
        self.eps_set = sem("eps_set")
        self.summed, self.moments, self.rooted, self.inverted, self.done = (
            sem(n) for n in ("summed", "moments", "rooted", "inverted", "done"))

    def start(self, dve):
        self.nc.vector.memset(self.eps_col[:], self.eps).then_inc(self.eps_set, 1)

    def moments_of(self, dve, src, n):
        if n:
            dve.wait_ge(self.done, n)
        for j in range(4):
            last = self.nc.vector.bn_stats(self.stats[:, j, :], src[:, j, :])
        last.then_inc(self.summed, 1)
        dve.wait_ge(self.summed, n + 1)
        for j in range(4):
            last = self.nc.vector.bn_aggr(self.mv[:, j, :], self.stats[:, j, :])
        last.then_inc(self.moments, 1)

    def root(self, act, n):
        if n == 0:
            act.wait_ge(self.eps_set, 1)
        act.wait_ge(self.moments, n + 1)
        self.nc.scalar.activation(self.std[:], self.mv[:, :, 1], ACT.Sqrt, bias=self.eps_col[:]).then_inc(self.rooted, 1)

    def apply(self, dve, src, dst, n):
        dve.wait_ge(self.rooted, n + 1)
        self.nc.vector.reciprocal(self.rstd[:], self.std[:]).then_inc(self.inverted, 1)
        dve.wait_ge(self.inverted, n + 1)
        for j in range(4):
            last = self.nc.vector.tensor_scalar(dst[:, j, :], src[:, j, :], self.mv[:, j, 0:1], self.rstd[:, j:j + 1],
                                                ALU.subtract, ALU.mult)
        last.then_inc(self.done, 1)


def quantised_ffn(nc, a, persist):
    X, ident = persist["X"], persist["ident"]
    T = X.shape[1]
    CHUNKS = T // 4
    F = a["L0_ffn_fc1_q"].shape[1]
    NF = F // P
    with ExitStack() as ctx:
        sb = lambda n, s, d=F32: ctx.enter_context(nc.sbuf_tensor(n, s, d))
        ps = lambda n: ctx.enter_context(nc.psum_tensor(n, [P, CH], F32))
        sem = lambda n: ctx.enter_context(nc.semaphore(n))
        q1, q2 = sb("q1", [P, F], I32), sb("q2", [P, NF, P], I32)
        s1, s2 = sb("s1_rows", [P, F]), sb("s2_rows", [P, NF, P])
        w1, w2 = sb("w1", [P, F]), sb("w2", [P, NF, P])
        b1_rows, b2_row = sb("b1_rows", [NF, P]), sb("b2_row", [P, P])
        b1 = sb("b1", [P, NF])
        affine_rows, affine = sb("affine_rows", [2, P]), sb("affine", [P, 2])
        half_b2 = sb("half_b2", [P, P])
        h = sb("h", [P, 2, 4, P])
        h_turned = sb("h_turned", [P, 2, CH])
        y = sb("y", [P, NF, CH])
        bank_t = [ps(f"bank_t{i}") for i in range(2)]
        bank_f = [ps(f"bank_f{i}") for i in range(2)]
        bank_z = [ps(f"bank_z{i}") for i in range(2)]
        bank_b = ps("bank_b")
        first_ln, inner_ln, last_ln = (Normaliser(nc, ctx, n, 1e-5) for n in ("ln_in", "ln_ffn", "ln_out"))
        q_in, row_in = sem("ffn_q_in"), sem("ffn_rows_in")
        w1_ready, w2_ready, b2_ready, b2_added = sem("w1_ready"), sem("w2_ready"), sem("half_b2_ready"), sem("half_b2_added")
        cols_turned, cols_ready = sem("columns_turned"), sem("columns_ready")
        turned, turned_taken, f_filled, f_taken = sem("h_turned_filled"), sem("h_turned_taken"), sem("fc1_filled"), sem("silu_done")
        z_filled, z_added = sem("fc2_filled"), sem("fc2_added")
        doubled, next_in = sem("x_doubled"), sem("attention_weights_in")
        block = ctx.enter_context(nc.Block())
        chunk = lambda t, c: t[:, 4 * c:4 * c + 4, :]

        @block.sync
        def _(sp):
            row = lambda ap: ap.rearrange("(o n) -> o n", o=1)
            sp.dma_start(b1_rows[:], a["L0_ffn_fc1_bias"].rearrange("(f p) -> f p", p=P)).then_inc(row_in, 16)
            sp.dma_start(affine_rows[0:1, :], row(a["L0_ffn_ln_gamma"])).then_inc(row_in, 16)
            sp.dma_start(affine_rows[1:2, :], row(a["L0_ffn_ln_beta"])).then_inc(row_in, 16)
            sp.dma_start(q1[:], a["L0_ffn_fc1_q"]).then_inc(q_in, 16)
            sp.dma_start(s1[:], a["L0_ffn_fc1_scales"].broadcast_to((P, F))).then_inc(q_in, 16)
            sp.dma_start(q2[:], a["L0_ffn_fc2_q"].rearrange("(f p) n -> p f n", p=P)).then_inc(q_in, 16)
            sp.dma_start(s2[:], a["L0_ffn_fc2_scales"].rearrange("(o f) n -> o f n", o=1).broadcast_to((P, NF, P))).then_inc(q_in, 16)
            sp.dma_start(b2_row[:], row(a["L0_ffn_fc2_bias"]).broadcast_to((P, P))).then_inc(q_in, 16)
            for n, w in enumerate(("wq", "wk", "wv", "wo")):
                sp.dma_start(persist["w_rows"][:, n, :], a["L1_attn_" + w]).then_inc(next_in, 16)
            sp.wait_ge(next_in, 64)

        @block.gpsimd
        def _(pool):
            pool.wait_ge(b2_ready, 1)
            for c in range(CHUNKS):
                x = chunk(X, c)
                pool.wait_ge(inner_ln.done, c + 1)
                nc.gpsimd.tensor_tensor(x, x, x, ALU.add).then_inc(doubled, 1)
                pool.wait_ge(doubled, c + 1)
                nc.gpsimd.tensor_tensor(x, x, half_b2[:].unsqueeze(1).broadcast_to((P, 4, P)), ALU.add).then_inc(b2_added, 1)

        @block.tensor
        def _(pe):
            pe.wait_ge(row_in, 48)
            nc.tensor.transpose(bank_b[:, 0:NF], b1_rows[:], ident[0:NF, 0:NF])
            nc.tensor.transpose(bank_b[:, NF:NF + 2], affine_rows[:], ident[0:2, 0:2]).then_inc(cols_turned, 1)

            def turn(c):
                pe.wait_ge(inner_ln.done, c + 1)
                if c >= 2:
                    pe.wait_ge(turned_taken, c - 1)
                for j in range(4):
                    last = nc.tensor.transpose(bank_t[c % 2][:, j * P:(j + 1) * P], h[:, c % 2, j, :], ident[:])
                last.then_inc(turned, 1)

            turn(0)
            pe.wait_ge(w1_ready, 1)
            for c in range(CHUNKS):
                pe.wait_ge(turned_taken, c + 1)
                for f in range(NF):
                    n = NF * c + f
                    if n >= 2:
                        pe.wait_ge(f_taken, n - 1)
                    nc.tensor.matmul(bank_f[n % 2][:], w1[:, f * P:(f + 1) * P], h_turned[:, c % 2, :],
                                     start=True, stop=True).then_inc(f_filled, 1)
                if c == 0:
                    pe.wait_ge(w2_ready, 1)
                if c >= 2:
                    pe.wait_ge(z_added, c - 1)
                pe.wait_ge(f_taken, NF * (c + 1))
                for j in range(4):
                    for f in range(NF):
                        last = nc.tensor.matmul(bank_z[c % 2][:, j * P:(j + 1) * P], y[:, f, j * P:(j + 1) * P],
                                                w2[:, f, :], start=(f == 0), stop=(f == NF - 1))
                last.then_inc(z_filled, 1)
                if c + 1 < CHUNKS:
                    turn(c + 1)

        @block.scalar
        def _(act):
            first_ln.root(act, 0)
            act.wait_ge(cols_turned, 1)
            nc.scalar.copy(b1[:], bank_b[:, 0:NF])
            nc.scalar.copy(affine[:], bank_b[:, NF:NF + 2]).then_inc(cols_ready, 1)
            act.wait_ge(cols_ready, 1)

            def silu(c):
                act.wait_ge(turned, c + 1)
                nc.scalar.activation(h_turned[:, c % 2, :], bank_t[c % 2][:], ACT.Identity, bias=affine[:, 1:2],
                                     scale=affine[:, 0:1]).then_inc(turned_taken, 1)
                for f in range(NF):
                    n = NF * c + f
                    act.wait_ge(f_filled, n + 1)
                    if c and f == 0:
                        act.wait_ge(z_filled, c)
                    nc.scalar.activation(y[:, f, :], bank_f[n % 2][:], ACT.Silu, bias=b1[:, f:f + 1]).then_inc(f_taken, 1)

            inner_ln.root(act, 0)
            act.wait_ge(q_in, 80)
            nc.scalar.mul(half_b2[:], b2_row[:], 0.5).then_inc(b2_ready, 1)
            for c in range(CHUNKS):
                if c + 1 < CHUNKS:
                    first_ln.root(act, c + 1)
                silu(c)
                if c + 1 < CHUNKS:
                    inner_ln.root(act, c + 1)
                if c:
                    last_ln.root(act, c - 1)
            last_ln.root(act, CHUNKS - 1)

        @block.vector
        def _(dve):
            for ln in (first_ln, inner_ln, last_ln):
                ln.start(dve)
            for c in range(CHUNKS + 2):
                enters, leaves = c < CHUNKS, c >= 2
                if enters:
                    x = chunk(X, c)
                    first_ln.moments_of(dve, x, c)
                    first_ln.apply(dve, x, x, c)
                    dve.wait_ge(first_ln.done, c + 1)
                    inner_ln.moments_of(dve, x, c)
                if leaves:
                    out = chunk(X, c - 2)
                    dve.wait_ge(z_filled, c - 1)
                    dve.wait_ge(b2_added, c - 1)
                    nc.vector.scalar_tensor_tensor(out=out, in0=bank_z[c % 2][:].rearrange("p (t d) -> p t d", d=P), scalar=0.5,
                                                   in1=out, op0=ALU.mult, op1=ALU.add).then_inc(z_added, 1)
                    dve.wait_ge(z_added, c - 1)
                    last_ln.moments_of(dve, out, c - 2)
                if enters:
                    if leaves:
                        dve.wait_ge(turned, c - 1)
                    inner_ln.apply(dve, x, h[:, c % 2], c)
                if leaves:
                    last_ln.apply(dve, out, out, c - 2)
                if c == 0:
                    dve.wait_ge(q_in, 80)
                    nc.vector.scalar_tensor_tensor(out=w1[:], in0=q1[:], scalar=-128.0, in1=s1[:], op0=ALU.add,
                                                   op1=ALU.mult).then_inc(w1_ready, 1)
                    nc.vector.scalar_tensor_tensor(out=w2[:], in0=q2[:], scalar=-128.0, in1=s2[:], op0=ALU.add,
                                                   op1=ALU.mult).then_inc(w2_ready, 1)
            dve.wait_ge(last_ln.done, CHUNKS)


def attend_once(nc, a, persist):
    X, ident, B = persist["X"], persist["ident"], persist["B"]
    T = X.shape[1]
    TB = T // B
    N = TB * P
    S = B * N
    HALVES = N // CH
    INV_SCALE = float(P / 16) ** -0.5
    VW = 2 * P + 2
    STEPS = B * HALVES
    with ExitStack() as ctx:
        sb = lambda n, s, d=F32: ctx.enter_context(nc.sbuf_tensor(n, s, d))
        ps = lambda n: ctx.enter_context(nc.psum_tensor(n, [P, CH], F32))
        sem = lambda n: ctx.enter_context(nc.semaphore(n))
        w_rows, w_t = persist["w_rows"], sb("w_turned", [P, 4, P])
        xt = sb("xt", [P, S])
        hi = {w: sb(f"{w}1_hi", [P, S], F32R) for w in "qk"}
        lo = {w: sb(f"{w}1_lo", [P, S], F32R) for w in "qk"}
        V = sb("v1_parts", [P, T, VW], F16)
        ones, row = sb("ones_row", [1, P], F32R), sb("negmax_row", [1, S], F32R)
        maxes, negmax = sb("maxes1", [P, T, HALVES]), sb("negmax1", [P, T], F32R)
        probs = sb("probs1", [P, 2, TB, CH])
        probs_lo = sb("probs1_lo", [P, 2, TB, CH], F16)
        rden = sb("rden1", [P, 4])
        o_hi = sb("o_hi", [P, 2, P])
        o_new = sb("o_new", [P, S])
        bank_a = [ps(f"bank_a{i}") for i in range(4)]
        bank_m = [ps(f"bank_n{i}") for i in range(2)]
        bank_o = [ps(f"bank_p{i}") for i in range(2)]
        ln = Normaliser(nc, ctx, "ln_attn", 1e-5)
        w_turned, w_ready = sem("w1_turned"), sem("w1t_ready")
        a_filled, xt_ready = sem("bank_a_filled"), sem("xt_ready")
        parted, parts_taken = sem("parts_hi_ready"), sem("parts_lo_ready")
        ones_ready = sem("ones1_ready")
        m_filled, m_reduced, c_ready = sem("max1_scores"), sem("max1_reduced"), sem("negmax1_ready")
        row_in = [sem(f"negmax1_in{c}") for c in range(S // CH)]
        exp_done, pv_done = sem("exp1_done"), sem("pv1_done")
        lo_pool, lo_dve = sem("probs1_lo_by_gpsimd"), sem("probs1_lo_by_vector")
        rden_ready, o_scaled, o_taken = sem("rden1_ready"), sem("o1_scaled"), sem("o1_taken")
        y_filled, y_added = sem("y1_filled"), sem("y1_added")
        block = ctx.enter_context(nc.Block())
        CK = S // CH
        X0, Q0, K0, V0, S0 = 0, CK, 2 * CK, 3 * CK, 4 * CK
        MAX_N = T * HALVES
        AHEAD = 4 * HALVES + 3
        FINISH_AT = {(STEPS - 1, 0): 0, (STEPS - 1, 4): 1}
        queries = lambda t, c: t[:, c * CH:(c + 1) * CH].rearrange("d (p t) -> d t p", t=4)

        def make_lo(unit, eng, step, kt, made):
            eng.wait_ge(exp_done, TB * step + kt + 1)
            p = probs[:, step % 2, kt, :]
            if step >= 2:
                eng.wait_ge(pv_done, 4 * (step - 1))
            unit.tensor_tensor(probs_lo[:, step % 2, kt, :], p, p.bitcast(BF16).rearrange("p (q two) -> p q two", two=2)[:, :, 1],
                               ALU.subtract).then_inc(made, 1)

        @block.gpsimd
        def _(pool):
            for step in range(STEPS):
                for kt in range(0, TB, 2):
                    make_lo(nc.gpsimd, pool, step, kt, lo_pool)

        @block.sync
        def _(sp):
            for c in range(CK):
                sp.wait_ge(c_ready, c + 1)
                sp.dma_start(row[:, c * CH:(c + 1) * CH].bitcast(F32).rearrange("o (p t) -> o p t", t=4),
                             negmax[:, 4 * c:4 * c + 4].bitcast(F32)).then_inc(row_in[c], 16)

        @block.tensor
        def _(pe):
            def bank(n):
                m = n - 4
                if m >= S0:
                    pe.wait_ge(exp_done, m - S0 + 1)
                elif m >= Q0:
                    pe.wait_ge(parts_taken, m - Q0 + 1)
                elif m >= X0:
                    pe.wait_ge(xt_ready, m - X0 + 1)
                return bank_a[n % 4]

            for n in range(4):
                last = nc.tensor.transpose(bank_m[0][:, n * P:(n + 1) * P], w_rows[:, n, :], ident[:])
            last.then_inc(w_turned, 1)
            for c in range(CK):
                b = bank(X0 + c)
                for j in range(4):
                    last = nc.tensor.transpose(b[:, j * P:(j + 1) * P], X[:, 4 * c + j, :], ident[:])
                last.then_inc(a_filled, 1)
            pe.wait_ge(w_ready, 1)
            for w in range(2):
                for c in range(CK):
                    b = bank(Q0 + CK * w + c)
                    pe.wait_ge(xt_ready, c + 1)
                    nc.tensor.matmul(b[:], w_t[:, w, :], xt[:, c * CH:(c + 1) * CH], start=True, stop=True).then_inc(a_filled, 1)
            for c in range(CK):
                b = bank(V0 + c)
                for j in range(4):
                    t = 4 * c + j
                    last = nc.tensor.matmul(b[:, j * P:(j + 1) * P], xt[:, t * P:(t + 1) * P], w_t[:, 2, :], start=True, stop=True)
                last.then_inc(a_filled, 1)

            pe.wait_ge(parts_taken, 2 * CK)
            def max_scores(n):
                t, half = n // HALVES, n % HALVES
                b, c = t // TB, t // 4
                if n >= 2:
                    pe.wait_ge(m_reduced, n - 1)
                ks = slice(b * N + half * CH, b * N + (half + 1) * CH)
                nc.tensor.matmul(bank_m[n % 2][:], queries(hi["q"], c)[:, t % 4, :], hi["k"][:, ks],
                                 start=True, stop=True).then_inc(m_filled, 1)

            def scores(step, kt):
                b = step // HALVES
                bk = bank(S0 + TB * step + kt)
                if kt == 0:
                    pe.wait_ge(row_in[step], 16)
                ks, qs = slice(b * N + kt * P, b * N + (kt + 1) * P), slice(step * CH, (step + 1) * CH)
                nc.tensor.matmul(bk[:], ones[:], row[:, qs], start=True, stop=False)
                nc.tensor.matmul(bk[:], lo["k"][:, ks], hi["q"][:, qs], start=False, stop=False)
                nc.tensor.matmul(bk[:], hi["k"][:, ks], lo["q"][:, qs], start=False, stop=False)
                nc.tensor.matmul(bk[:], hi["k"][:, ks], hi["q"][:, qs], start=False, stop=True).then_inc(a_filled, 1)

            def times_v(step, qt):
                b = step // HALVES
                if qt == 0:
                    pe.wait_ge(lo_pool, TB // 2 * (step + 1))
                    pe.wait_ge(lo_dve, TB // 2 * (step + 1))
                n = 4 * step + qt
                if n >= 2:
                    pe.wait_ge(o_taken, n - 1)
                hi_of = probs[:, step % 2].bitcast(BF16).rearrange("p k (q two) -> p k q two", two=2)
                acc, qs = bank_o[n % 2], slice(qt * P, (qt + 1) * P)
                for kt in range(TB):
                    low = lambda: nc.tensor.matmul(acc[:, 0:P + 1], probs_lo[:, step % 2, kt, qs], V[:, b * TB + kt, 0:P + 1],
                                                   start=False, stop=False, skip_group_check=True)
                    if kt == TB - 1:
                        low()
                    last = nc.tensor.matmul(acc[:, 0:2 * P + 1], hi_of[:, kt, qs, 1], V[:, b * TB + kt, 0:2 * P + 1],
                                            start=(kt == 0), stop=(kt == TB - 1))
                    if kt < TB - 1:
                        low()
                last.then_inc(pv_done, 1)

            def times_wo(c):
                pe.wait_ge(o_taken, 4 * HALVES * (c // HALVES + 1))
                if c < 2:
                    pe.wait_ge(m_reduced, MAX_N)
                else:
                    pe.wait_ge(y_added, c - 1)
                for j in range(4):
                    t = 4 * c + j
                    last = nc.tensor.matmul(bank_m[c % 2][:, j * P:(j + 1) * P], o_new[:, t * P:(t + 1) * P], w_t[:, 3, :], start=True, stop=True)
                last.then_inc(y_filled, 1)

            for n in range(AHEAD):
                max_scores(n)
            for step in range(STEPS + 1):
                for kt in range(TB):
                    if step < STEPS:
                        scores(step, kt)
                    n = AHEAD + TB * step + kt
                    if n < MAX_N:
                        max_scores(n)
                    if step and kt % 2:
                        times_v(step - 1, kt // 2)
                    if (step, kt) in FINISH_AT:
                        times_wo(FINISH_AT[step, kt])
            for c in range(CK // 2, CK):
                times_wo(c)

        @block.scalar
        def _(act):
            act.wait_ge(w_turned, 1)
            nc.scalar.copy(w_t[:].rearrange("p n e -> p (n e)"), bank_m[0][:]).then_inc(w_ready, 1)
            for c in range(CK):
                act.wait_ge(a_filled, X0 + c + 1)
                nc.scalar.copy(xt[:, c * CH:(c + 1) * CH], bank_a[(X0 + c) % 4][:]).then_inc(xt_ready, 1)
            for n in range(2 * CK):
                w, c = "qk"[n // CK], n % CK
                act.wait_ge(a_filled, Q0 + n + 1)
                nc.scalar.copy(hi[w][:, c * CH:(c + 1) * CH], bank_a[(Q0 + n) % 4][:]).then_inc(parted, 1)
            for c in range(CK):
                act.wait_ge(a_filled, V0 + c + 1)
                nc.scalar.copy(V[:, 4 * c:4 * c + 4, 0:P], bank_a[(V0 + c) % 4][:].rearrange("p (t d) -> p t d", d=P)).then_inc(parted, 1)
            for step in range(STEPS + 1):
                for kt in range(TB):
                    if step < STEPS:
                        n = TB * step + kt
                        act.wait_ge(a_filled, S0 + n + 1)
                        nc.scalar.activation(probs[:, step % 2, kt, :], bank_a[(S0 + n) % 4][:], ACT.Exp,
                                             scale=INV_SCALE).then_inc(exp_done, 1)
                    if step and kt % 2:
                        g = 4 * (step - 1) + kt // 2
                        act.wait_ge(rden_ready, g + 1)
                        nc.scalar.activation(o_hi[:, g % 2, :], bank_o[g % 2][:, 0:P], ACT.Copy,
                                             scale=rden[:, g % 4:g % 4 + 1]).then_inc(o_scaled, 1)
                    if (step, kt - 1) in FINISH_AT:
                        ln.root(act, FINISH_AT[step, kt - 1])
            for c in range(CK // 2, CK):
                ln.root(act, c)

        @block.vector
        def _(dve):
            ln.start(dve)
            nc.vector.memset(ones[:].bitcast(F32), 1.0)
            nc.vector.memset(V[:, :, P:P + 1], 1.0).then_inc(ones_ready, 1)
            dve.wait_ge(ones_ready, 1)
            for n in range(2 * CK):
                w, c = "qk"[n // CK], n % CK
                cs = slice(c * CH, (c + 1) * CH)
                dve.wait_ge(parted, n + 1)
                nc.vector.tensor_tensor(lo[w][:, cs], bank_a[(Q0 + n) % 4][:], hi[w][:, cs].bitcast(F32),
                                        ALU.subtract).then_inc(parts_taken, 1)
            for c in range(CK):
                dve.wait_ge(parted, 2 * CK + c + 1)
                nc.vector.tensor_tensor(V[:, 4 * c:4 * c + 4, P + 1:2 * P + 1], bank_a[(V0 + c) % 4][:].rearrange("p (t d) -> p t d", d=P),
                                        V[:, 4 * c:4 * c + 4, 0:P], ALU.subtract).then_inc(parts_taken, 1)
            def reduce(n):
                t, half = n // HALVES, n % HALVES
                dve.wait_ge(m_filled, n + 1)
                nc.vector.tensor_reduce(maxes[:, t, half:half + 1], bank_m[n % 2][:], AX.X, ALU.max).then_inc(m_reduced, 1)
                if n % (4 * HALVES) == 4 * HALVES - 1:
                    c = t // 4
                    dve.wait_ge(m_reduced, n + 1)
                    nc.vector.tensor_reduce(negmax[:, 4 * c:4 * c + 4], maxes[:, 4 * c:4 * c + 4, :], AX.X, ALU.max,
                                            negate=True).then_inc(c_ready, 1)
            def finish(c):
                x = X[:, 4 * c:4 * c + 4, :]
                dve.wait_ge(y_filled, c + 1)
                nc.vector.tensor_tensor(x, x, bank_m[c % 2][:].rearrange("p (t d) -> p t d", d=P), ALU.add).then_inc(y_added, 1)
                dve.wait_ge(y_added, c + 1)
                ln.moments_of(dve, x, c)
                ln.apply(dve, x, x, c)

            for n in range(AHEAD):
                reduce(n)
            for step in range(STEPS + 1):
                for kt in range(TB):
                    n = AHEAD + TB * step + kt
                    if n < MAX_N:
                        reduce(n)
                    if step < STEPS and kt % 2:
                        make_lo(nc.vector, dve, step, kt, lo_dve)
                    if step and kt % 2:
                        g = 4 * (step - 1) + kt // 2
                        dve.wait_ge(pv_done, g + 1)
                        nc.vector.reciprocal(rden[:, g % 4:g % 4 + 1], bank_o[g % 2][:, P:P + 1]).then_inc(rden_ready, 1)
                        dve.wait_ge(o_scaled, g + 1)
                        dst = o_new[:].rearrange("p (b d r) -> p b r d", b=B, r=TB)[:, g // TB, g % TB, :]
                        nc.vector.scalar_tensor_tensor(out=dst, in0=bank_o[g % 2][:, P + 1:2 * P + 1], scalar=rden[:, g % 4:g % 4 + 1],
                                                       in1=o_hi[:, g % 2, :], op0=ALU.mult, op1=ALU.add).then_inc(o_taken, 1)
                    if (step, kt - 1) in FINISH_AT:
                        finish(FINISH_AT[step, kt - 1])
            for c in range(CK // 2, CK):
                finish(c)
            dve.wait_ge(ln.done, CK)


def mix_experts(nc, a, persist, out):
    X, ident, B = persist["X"], persist["ident"], persist["B"]
    T = X.shape[1]
    CK = T // 4
    S = T * P
    NE, _, F = a["L1_ffn_ew1"].shape
    NF = F // P
    FFNS = NE + 1
    with ExitStack() as ctx:
        sb = lambda n, s, d=F32: ctx.enter_context(nc.sbuf_tensor(n, s, d))
        ps = lambda n: ctx.enter_context(nc.psum_tensor(n, [P, CH], F32))
        sem = lambda n: ctx.enter_context(nc.semaphore(n))
        w_raw = [sb("e1_raw", [P, F]), sb("e2_raw", [P, F])]
        w_hi = [[sb(f"e{w + 1}_hi{i}", [P, F], F32R) for w in range(2)] for i in range(2)]
        w_lo = [[sb(f"e{w + 1}_lo{i}", [P, F], F32R) for w in range(2)] for i in range(2)]
        b1_rows, b1 = sb("e1_bias_rows", [FFNS * NF, P]), sb("e1_bias", [P, FFNS * NF])
        b1_now = sb("e1_bias_now", [P, 2, NF])
        b2, shared_b2 = sb("e2_bias", [NE, P]), sb("shared_b2_rows", [P, P])
        nw_row, nw = sb("norm_w_row", [1, P]), sb("norm_w", [P, 1])
        r_rows, r_t = sb("router_rows", [NE, P]), sb("router_t", [P, NE])
        sums = sb("square_sums", [P, T])
        root, rroot, tiny = sb("rms", [P, T]), sb("rms_inv", [P, T]), sb("rms_eps", [P, 1])
        n_tok = sb("n_tokens", [P, T, P])
        nt, nt_hi, nt_lo = sb("nt", [P, S]), sb("nt_hi", [P, S], F32R), sb("nt_lo", [P, S], F32R)
        prob = sb("gates", [P, T, NE])
        top, top_at = sb("top8", [P, T, NE]), sb("top8_at", [P, T, NE], U32)
        at = sb("top2_at", [P, T, 2])
        lane_i, lane = sb("lane_i", [P, NE], I32), sb("lane", [P, NE])
        first, second = sb("is_first", [P, T, NE]), sb("is_second", [P, T, NE])
        total, share = sb("top2_sum", [P, T]), sb("top2_inv", [P, T])
        comb_e = sb("comb_by_token", [P, T, NE])
        comb_t = sb("comb_t", [NE, S])
        gates = [sb(f"gates_on_all{i}", [P, S]) for i in range(2)]
        gate_rows = nc.dram_tensor("gate_rows", [NE, S], F32).ap()
        r = sb("rectified", [P, 2, CH])
        h = sb("hidden", [P, NF, CH])
        h_hi, h_lo = sb("hidden_hi", [P, NF, CH], F32R), sb("hidden_lo", [P, NF, CH], F32R)
        y_t = sb("y_by_width", [P, 2, CH])
        y = sb("y_out", [P, T, P])
        bank_h = [ps(f"bank_h{i}") for i in range(2)]
        bank_y = [ps(f"bank_y{i}") for i in range(CK)]
        bank_c = [ps(f"bank_c{i}") for i in range(2)]
        ln = Normaliser(nc, ctx, "ln_moe", 1e-5)
        small_in = sem("moe_small_in")
        w_in, w_hi_ready, w_lo_ready = sem("expert_in"), sem("expert_hi"), sem("expert_lo")
        small_turned, small_ready = sem("moe_small_turned"), sem("moe_small_ready")
        eps_ready, squared, rooted, inverted, scaled = (sem("moe_" + n) for n in ("eps", "squared", "rooted", "inverted", "scaled"))
        turned, nt_ready, hi_ready, lo_ready = sem("n_turned"), sem("nt_ready"), sem("nt_hi_ready"), sem("nt_lo_ready")
        routed, gated, picked, pick, comb_ready = sem("router_scores"), sem("gates_ready"), sem("top_found"), sem("pick_step"), sem("comb_ready")
        lane_ready, b2_added = sem("lane_ready"), sem("shared_b2_added")
        comb_turned, comb_t_ready, rows_stored = sem("comb_turned"), sem("comb_t_ready"), sem("gate_rows_stored")
        gates_in = [sem(f"gates_on_all{i}_in") for i in range(2)]
        h_filled, rectified, h_gated, h_hi_ready = sem("h_filled"), sem("rectified"), sem("h_gated"), sem("h_hi_ready")
        lo_pool, lo_dve = sem("h_lo_by_gpsimd"), sem("h_lo_by_vector")
        h_used = sem("h_used")
        y_copied, y_turned, y_added = sem("y_copied"), sem("y_turned"), sem("y_added_moe")
        b1_ready = sem("e1_bias_ready")
        stored = sem("stored")
        block = ctx.enter_context(nc.Block())
        row = lambda ap: ap.rearrange("(o n) -> o n", o=1)
        TILES = NF * CK
        GATES_AT = 1
        LO_POOL = NF - 1

        def over_ffns(eng, ffn):
            ffn(0, 0)
            with eng.Fori(0, NE // 2 - 1) as m:
                ffn(2 * m + 1, 1, m)
                ffn(2 * m + 2, 0, m)
            ffn(NE - 1, 1, NE // 2 - 1)
            ffn(NE, 0, NE // 2 - 1)

        @block.sync
        def _(sp):
            def load(e):
                sp.dma_start(w_raw[0][:], a["L1_ffn_ew1"][bass.ds(e, 1), :, :].rearrange("o d f -> d (o f)")).then_inc(w_in, 16)
                sp.dma_start(w_raw[1][:].rearrange("p (f q) -> p f q", q=P),
                             a["L1_ffn_ew2"][bass.ds(e, 1), :, :].rearrange("o (f p) q -> p (o f) q", p=P)).then_inc(w_in, 16)

            def load_gates(e, i):
                sp.dma_start(gates[i][:], gate_rows[bass.ds(e, 1), :].broadcast_to((P, S))).then_inc(gates_in[i], 16)

            sp.dma_start(nw_row[:], row(a["L1_ffn_norm_weight"])).then_inc(small_in, 16)
            sp.dma_start(r_rows[:], a["L1_ffn_router_w"]).then_inc(small_in, 16)
            sp.dma_start(b1_rows[0:NF, :], a["L1_ffn_sb1"].rearrange("(f p) -> f p", p=P)).then_inc(small_in, 16)
            sp.dma_start(b1_rows[NF:, :], a["L1_ffn_eb1"].rearrange("e (f p) -> (e f) p", p=P)).then_inc(small_in, 16)
            sp.dma_start(b2[:], a["L1_ffn_eb2"]).then_inc(small_in, 16)
            sp.dma_start(shared_b2[:], row(a["L1_ffn_sb2"]).broadcast_to((P, P))).then_inc(small_in, 16)
            sp.dma_start(w_raw[0][:], a["L1_ffn_sw1"]).then_inc(w_in, 16)
            sp.dma_start(w_raw[1][:].rearrange("p (f q) -> p f q", q=P), a["L1_ffn_sw2"].rearrange("(f p) o -> p f o", p=P)).then_inc(w_in, 16)
            sp.wait_ge(w_lo_ready, 1)
            load(0)
            sp.wait_ge(comb_t_ready, CK)
            sp.dma_start(gate_rows, comb_t[:]).then_inc(rows_stored, 16)
            sp.wait_ge(rows_stored, 16)
            load_gates(0, 1)
            sp.wait_ge(gates_in[1], 16)
            load_gates(1, 0)
            sp.wait_ge(w_lo_ready, 2)
            load(1)
            with sp.Fori(1, NE // 2) as m:
                for d in range(2):
                    sp.wait_ge(h_gated, TILES * (2 * m + d - 1))
                    load_gates(2 * m + d, 1 - d)
                    sp.wait_ge(w_lo_ready, 2 * m + d + 1)
                    load(2 * m + d)
            o = out.rearrange("b (t p) d -> p (b t) d", p=P)
            for c in range(CK):
                sp.wait_ge(ln.done, c + 1)
                sp.dma_start(o[:, 4 * c:4 * c + 4, :], y[:, 4 * c:4 * c + 4, :]).then_inc(stored, 16)
            sp.wait_ge(stored, 16 * CK)

        @block.gpsimd
        def _(pool):
            nc.gpsimd.iota(lane_i[:], [[1, NE]], base=0, channel_multiplier=0).then_inc(lane_ready, 1)

            def ffn(n, half, m=None):
                for c in range(CK):
                    for f in range(NF if isinstance(n, int) and n == 0 and c < CK - 1 else LO_POOL):
                        pool.wait_ge(h_hi_ready, TILES * n + NF * c + f + 1)
                        nc.gpsimd.tensor_tensor(h_lo[:, f, :], h[:, f, :], h_hi[:, f, :].bitcast(F32), ALU.subtract).then_inc(lo_pool, 1)

            over_ffns(pool, ffn)

        @block.tensor
        def _(pe):
            pe.wait_ge(small_in, 96)
            nc.tensor.transpose(bank_c[0][:, 0:FFNS * NF], b1_rows[:], ident[0:FFNS * NF, 0:FFNS * NF])
            nc.tensor.transpose(bank_c[0][:, P:P + NE], r_rows[:], ident[0:NE, 0:NE])
            nc.tensor.transpose(bank_c[0][:, 2 * P:2 * P + 1], nw_row[:], ident[0:1, 0:1]).then_inc(small_turned, 1)
            for c in range(CK):
                pe.wait_ge(scaled, c + 1)
                for j in range(4):
                    last = nc.tensor.transpose(bank_y[c][:, j * P:(j + 1) * P], n_tok[:, 4 * c + j, :], ident[:])
                last.then_inc(turned, 1)
            def route():
                pe.wait_ge(nt_ready, CK)
                for t in range(T):
                    last = nc.tensor.matmul(bank_c[1][:, t * NE:(t + 1) * NE], nt[:, t * P:(t + 1) * P], r_t[:], start=True, stop=True)
                last.then_inc(routed, 1)

            def first_product(n, half, c, f):
                k = TILES * n + NF * c + f
                if c == 0 and f == 0:
                    pe.wait_ge(w_lo_ready, n + 1)
                if isinstance(n, int) and n == 0 and f == 0:
                    pe.wait_ge(lo_ready, c + 1)
                if not (isinstance(n, int) and k < 2):
                    pe.wait_ge(rectified, k - 1)
                fs, xs = slice(f * P, (f + 1) * P), slice(c * CH, (c + 1) * CH)
                out = bank_h[f % 2][:]
                nc.tensor.matmul(out, w_lo[half][0][:, fs], nt_hi[:, xs], start=True, stop=False)
                nc.tensor.matmul(out, w_hi[half][0][:, fs], nt_lo[:, xs], start=False, stop=False)
                nc.tensor.matmul(out, w_hi[half][0][:, fs], nt_hi[:, xs], start=False, stop=True).then_inc(h_filled, 1)

            def add_biases(c, start):
                nc.tensor.matmul(bank_y[c][:], b2[:], comb_t[:, c * CH:(c + 1) * CH], start=start, stop=False)

            def second_product(n, half, c, f):
                first_ffn, last_ffn = (isinstance(n, int) and n == v for v in (0, NE))
                if last_ffn and f == 0 and c < CK - 1:
                    add_biases(c, False)
                if first_ffn:
                    pe.wait_ge(lo_pool, NF * c + f + 1)
                elif f < LO_POOL:
                    pe.wait_ge(lo_pool, LO_POOL * CK * (n - 1) + TILES - 1 + LO_POOL * c + f + 1)
                else:
                    pe.wait_ge(lo_dve, CK * (n - 1) + c + 2)
                fs = slice(f * P, (f + 1) * P)
                out = bank_y[c][:]
                nc.tensor.matmul(out, w_lo[half][1][:, fs], h_hi[:, f, :], start=first_ffn and f == 0, stop=False)
                nc.tensor.matmul(out, w_hi[half][1][:, fs], h_lo[:, f, :], start=False, stop=False)
                nc.tensor.matmul(out, w_hi[half][1][:, fs], h_hi[:, f, :], start=False,
                                 stop=last_ffn and f == NF - 1).then_inc(h_used, 1)

            def turn_gates():
                pe.wait_ge(comb_ready, 1)
                for c in range(CK):
                    if c >= 2:
                        pe.wait_ge(comb_t_ready, c - 1)
                    for j in range(4):
                        last = nc.tensor.transpose(bank_c[c % 2][0:NE, j * P:(j + 1) * P], comb_e[:, 4 * c + j, :], ident[:])
                    last.then_inc(comb_turned, 1)

            def turn_output(c):
                pe.wait_ge(y_copied, c + 1)
                pe.wait_ge(comb_t_ready, CK) if c < 2 else pe.wait_ge(y_added, c - 1)
                for j in range(4):
                    last = nc.tensor.transpose(bank_c[c % 2][:, j * P:(j + 1) * P], y_t[:, c % 2, j * P:(j + 1) * P], ident[:])
                last.then_inc(y_turned, 1)

            def ffn(n, half, m=None):
                first_ffn, last_ffn = (isinstance(n, int) and n == v for v in (0, NE))
                for c in range(CK):
                    for f in range(NF):
                        first_product(n, half, c, f)
                        if c:
                            second_product(n, half, c - 1, f)
                        elif not first_ffn:
                            second_product(n - 1, 1 - half, CK - 1, f)
                        if last_ffn and c >= 2 and f == 1:
                            turn_output(c - 2)
                    if first_ffn and c == 0:
                        route()
                    if first_ffn and c == GATES_AT:
                        turn_gates()
                if first_ffn:
                    pe.wait_ge(comb_t_ready, CK)
                    add_biases(CK - 1, True)

            over_ffns(pe, ffn)
            for f in range(NF):
                second_product(NE, 0, CK - 1, f)
            for c in range(CK - 2, CK):
                turn_output(c)

        @block.scalar
        def _(act):
            act.wait_ge(squared, T)
            act.wait_ge(eps_ready, 1)
            nc.scalar.activation(root[:], sums[:], ACT.Sqrt, bias=tiny[:], scale=1.0 / P).then_inc(rooted, 1)
            act.wait_ge(small_turned, 1)
            nc.scalar.copy(b1[:], bank_c[0][:, 0:FFNS * NF])
            nc.scalar.copy(r_t[:], bank_c[0][:, P:P + NE])
            nc.scalar.copy(nw[:], bank_c[0][:, 2 * P:2 * P + 1]).then_inc(small_ready, 1)
            act.wait_ge(small_ready, 1)
            def split_weights(n, half):
                act.wait_ge(w_in, 32 * n + 32)
                if not (isinstance(n, int) and n < 2):
                    act.wait_ge(h_used, TILES * (n - 1))
                for w in range(2):
                    nc.scalar.copy(w_hi[half][w][:], w_raw[w][:]).then_inc(w_hi_ready, 1)
                nc.scalar.copy(b1_now[:, half, :], b1[:, bass.ds(NF * n, NF)]).then_inc(b1_ready, 1)

            split_weights(0, 0)
            for c in range(CK):
                cs = slice(c * CH, (c + 1) * CH)
                act.wait_ge(turned, c + 1)
                nc.scalar.activation(nt[:, cs], bank_y[c][:], ACT.Copy, scale=nw[:]).then_inc(nt_ready, 1)
                act.wait_ge(nt_ready, c + 1)
                nc.scalar.copy(nt_hi[:, cs], nt[:, cs]).then_inc(hi_ready, 1)

            def rectify(n, half, c, f):
                k = TILES * n + NF * c + f
                act.wait_ge(h_filled, k + 1)
                if isinstance(n, int) and n == 0:
                    if c:
                        act.wait_ge(lo_pool, k - 3)
                    dst = h[:, f, :]
                else:
                    dst = r[:, f % 2, :]
                nc.scalar.activation(dst, bank_h[f % 2][:], ACT.Relu, bias=b1_now[:, half, f:f + 1]).then_inc(rectified, 1)

            def lead(n, c, f):
                k = TILES * n + NF * c + f
                if isinstance(n, int) and n == 0:
                    act.wait_ge(rectified, k + 1)
                else:
                    act.wait_ge(h_gated, TILES * (n - 1) + NF * c + f + 1)
                if not (isinstance(n, int) and k < NF):
                    act.wait_ge(h_used, k - NF + 1)
                nc.scalar.copy(h_hi[:, f, :], h[:, f, :]).then_inc(h_hi_ready, 1)

            def copy_output(c):
                act.wait_ge(h_used, TILES * NE + NF * (c + 1))
                if c >= 2:
                    act.wait_ge(y_turned, c - 1)
                nc.scalar.copy(y_t[:, c % 2, :], bank_y[c][:]).then_inc(y_copied, 1)

            def ffn(n, half, m=None):
                first_ffn, last_ffn = (isinstance(n, int) and n == v for v in (0, NE))
                act.wait_ge(b1_ready, n + 1)
                for c in range(CK):
                    for f in range(NF):
                        rectify(n, half, c, f)
                        if first_ffn:
                            lead(n, c, f)
                        elif c or f:
                            lead(n, c if f else c - 1, (f - 1) % NF)
                        if c == 2 and f == 0 and not last_ffn:
                            split_weights(n + 1, 1 - half)
                        if last_ffn and c >= 2 and f == 0:
                            copy_output(c - 2)
                        if last_ffn and c >= 2 and f == NF - 1:
                            ln.root(act, c - 2)
                    if first_ffn and c == 0:
                        act.wait_ge(routed, 1)
                        nc.scalar.activation(prob[:].rearrange("p t e -> p (t e)"), bank_c[1][:, 0:T * NE], ACT.Sigmoid).then_inc(gated, 1)
                    if first_ffn and c == GATES_AT:
                        for g in range(CK):
                            act.wait_ge(comb_turned, g + 1)
                            nc.scalar.copy(comb_t[:, g * CH:(g + 1) * CH], bank_c[g % 2][0:NE, :]).then_inc(comb_t_ready, 1)
                if not first_ffn:
                    lead(n, CK - 1, NF - 1)

            over_ffns(act, ffn)
            for c in range(CK - 2, CK):
                copy_output(c)
            for c in range(CK - 2, CK):
                ln.root(act, c)

        @block.vector
        def _(dve):
            ln.start(dve)
            nc.vector.memset(tiny[:], 1e-8).then_inc(eps_ready, 1)
            for t in range(T):
                nc.vector.tensor_tensor_reduce(out=n_tok[:, t, :], in0=X[:, t, :], in1=X[:, t, :], scale=1.0, scalar=0.0,
                                               op0=ALU.mult, op1=ALU.add, accum_out=sums[:, t:t + 1]).then_inc(squared, 1)
            dve.wait_ge(rooted, 1)
            nc.vector.reciprocal(rroot[:], root[:]).then_inc(inverted, 1)
            dve.wait_ge(inverted, 1)
            for c in range(CK):
                for j in range(4):
                    t = 4 * c + j
                    last = nc.vector.tensor_scalar(n_tok[:, t, :], X[:, t, :], rroot[:, t:t + 1], None, ALU.mult)
                last.then_inc(scaled, 1)
            def split_weights(n, half):
                dve.wait_ge(w_hi_ready, 2 * n + 2)
                for w in range(2):
                    last = nc.vector.tensor_tensor(w_lo[half][w][:], w_raw[w][:], w_hi[half][w][:].bitcast(F32), ALU.subtract)
                last.then_inc(w_lo_ready, 1)

            split_weights(0, 0)
            for c in range(CK):
                cs = slice(c * CH, (c + 1) * CH)
                dve.wait_ge(hi_ready, c + 1)
                nc.vector.tensor_tensor(nt_lo[:, cs], nt[:, cs], nt_hi[:, cs].bitcast(F32), ALU.subtract).then_inc(lo_ready, 1)

            def gate(n, half, c, f):
                dve.wait_ge(rectified, TILES * n + NF * c + f + 1)
                if f < LO_POOL:
                    dve.wait_ge(lo_pool, LO_POOL * CK * (n - 1) + TILES - 1 + LO_POOL * (c - 1) + f + 1)
                nc.vector.tensor_tensor(h[:, f, :], r[:, f % 2, :], gates[half][:, c * CH:(c + 1) * CH], ALU.mult).then_inc(h_gated, 1)

            def rest(n, c):
                dve.wait_ge(h_hi_ready, TILES * n + NF * (c + 1))
                nc.vector.tensor_tensor(h_lo[:, NF - 1, :], h[:, NF - 1, :], h_hi[:, NF - 1, :].bitcast(F32),
                                        ALU.subtract).then_inc(lo_dve, 1)

            def add_output(c):
                x = X[:, 4 * c:4 * c + 4, :]
                dve.wait_ge(y_turned, c + 1)
                nc.vector.tensor_tensor(x, x, bank_c[c % 2][:].rearrange("p (t d) -> p t d", d=P), ALU.add).then_inc(y_added, 1)
                dve.wait_ge(y_added, c + 1)
                ln.moments_of(dve, x, c)

            def normalise(c):
                ln.apply(dve, X[:, 4 * c:4 * c + 4, :], y[:, 4 * c:4 * c + 4, :], c)

            def ffn(n, half, m=None):
                first_ffn, last_ffn = (isinstance(n, int) and n == v for v in (0, NE))
                if first_ffn:
                    choose_gates()
                    split_weights(1, 1)
                    nc.vector.tensor_tensor(X[:], X[:], shared_b2[:].unsqueeze(1).broadcast_to((P, T, P)), ALU.add).then_inc(b2_added, 1)
                    dve.wait_ge(b2_added, 1)
                    rest(0, CK - 1)
                    return
                dve.wait_ge(gates_in[half], 16 * (m + 1))
                for c in range(CK):
                    for f in range(NF):
                        gate(n, half, c, f)
                        if f == 0 and c:
                            rest(n, c - 1)
                        if c == 2 and f == 1 and not last_ffn:
                            split_weights(n + 1, 1 - half)
                        if last_ffn and c >= 2 and f == 2:
                            add_output(c - 2)
                    if last_ffn and c >= 2:
                        normalise(c - 2)
                rest(n, CK - 1)

            def choose_gates():
                steps = 0

                def then(ins):
                    nonlocal steps
                    steps += 1
                    ins.then_inc(pick, 1)
                    dve.wait_ge(pick, steps)

                dve.wait_ge(gated, 1)
                for t in range(T):
                    last = nc.vector.max(top[:, t, :], prob[:, t, :])
                last.then_inc(picked, 1)
                dve.wait_ge(picked, 1)
                for t in range(T):
                    last = nc.vector.max_index(top_at[:, t, :], top[:, t, :], prob[:, t, :])
                dve.wait_ge(lane_ready, 1)
                then(last)
                wide = lambda ap: ap.broadcast_to((P, T, NE))
                then(nc.vector.tensor_copy(at[:], top_at[:, :, 0:2]))
                then(nc.vector.tensor_copy(lane[:], lane_i[:]))
                then(nc.vector.tensor_tensor(first[:], wide(lane[:].unsqueeze(1)), wide(at[:, :, 0:1]), ALU.is_equal))
                then(nc.vector.tensor_tensor(second[:], wide(lane[:].unsqueeze(1)), wide(at[:, :, 1:2]), ALU.is_equal))
                then(nc.vector.tensor_tensor(first[:], first[:], second[:], ALU.add))
                then(nc.vector.tensor_tensor(first[:], first[:], prob[:], ALU.mult))
                then(nc.vector.tensor_tensor(total[:], top[:, :, 0], top[:, :, 1], ALU.add))
                then(nc.vector.tensor_scalar(total[:], total[:], 1e-6, None, ALU.add))
                then(nc.vector.reciprocal(share[:], total[:]))
                nc.vector.tensor_tensor(comb_e[:], first[:], wide(share[:].unsqueeze(2)), ALU.mult).then_inc(comb_ready, 1)

            over_ffns(dve, ffn)
            for c in range(CK - 2, CK):
                add_output(c)
                normalise(c)


def build(nc, a, out):
    B, S, D = a["L0_attn_query"].shape
    H, _, E = a["L0_attn_Wq"].shape
    T = B * S // P
    with ExitStack() as ctx:
        sb = lambda n, s, d: ctx.enter_context(nc.sbuf_tensor(n, s, d))
        persist = {"B": B, "Wq": a["L0_attn_Wq"], "Wk": a["L0_attn_Wk"], "Wp": a["L0_attn_Wp"],
                   "X": sb("x_tokens", [P, T, D], F32), "ident": sb("ident", [P, P], F32)}
        with ExitStack() as layer0:
            sb0 = lambda n, s, d: layer0.enter_context(nc.sbuf_tensor(n, s, d))
            persist.update(xhi=sb0("xhi", [P, B * S], F32R), xlo=sb0("xlo", [P, B * S], F32R),
                           V=sb0("v_parts", [P, H, T, 2 * E + 2], F16))
            attend_heads(nc, a, persist)
        persist["w_rows"] = sb("w_rows", [P, 4, P], F32)
        quantised_ffn(nc, a, persist)
        attend_once(nc, a, persist)
        mix_experts(nc, a, persist, out)


_INS = ['L0_attn_query',
        'L0_attn_Wq',
        'L0_attn_Wk',
        'L0_attn_Wv',
        'L0_attn_Wp',
        'L0_attn_bp',
        'L0_ffn_ln_gamma',
        'L0_ffn_ln_beta',
        'L0_ffn_fc1_q',
        'L0_ffn_fc1_scales',
        'L0_ffn_fc1_bias',
        'L0_ffn_fc2_q',
        'L0_ffn_fc2_scales',
        'L0_ffn_fc2_bias',
        'L1_attn_wq',
        'L1_attn_wk',
        'L1_attn_wv',
        'L1_attn_wo',
        'L1_ffn_norm_weight',
        'L1_ffn_router_w',
        'L1_ffn_sw1',
        'L1_ffn_sb1',
        'L1_ffn_sw2',
        'L1_ffn_sb2',
        'L1_ffn_ew1',
        'L1_ffn_eb1',
        'L1_ffn_ew2',
        'L1_ffn_eb2']
_OUTS = [((2, 1024, 128), "float32")]


def kernel(**inputs):
    import numpy as _np
    import concourse.bacc as _bacc
    from concourse import mybir as _mybir
    from concourse.bass_utils import run_bass_kernel_spmd as _run

    nc = _bacc.Bacc("TRN2", target_bir_lowering=False, num_devices=1)
    arrays, args = {}, {}
    for name in _INS:
        a = _np.ascontiguousarray(inputs[name])
        arrays[f"in_{name}_dram"] = a
        args[name] = nc.dram_tensor(f"in_{name}_dram", a.shape, _mybir.dt.from_np(a.dtype), kind="ExternalInput").ap()
    shape, dtype = _OUTS[0]
    out = nc.dram_tensor("out_0_dram", shape, _mybir.dt.from_np(_np.dtype(dtype)), kind="ExternalOutput").ap()
    build(nc, args, out)
    r = _run(nc, [arrays], core_ids=[0])
    return r.results[0]["out_0_dram"]
```
